# Optimizing a Trainium2 kernel written in Bass

```python
import numpy as np
import jax
import jax.numpy as jnp

def _softmax(x, axis=-1):
    return jax.nn.softmax(x, axis=axis)

def _gelu(x):
    return jax.nn.gelu(x, approximate=True)

def _silu(x):
    return jax.nn.silu(x)

def _sigmoid(x):
    return jax.nn.sigmoid(x)

def _layernorm(x, axis=-1, eps=1e-05):
    m = jnp.mean(x, axis=axis, keepdims=True)
    v = jnp.var(x, axis=axis, keepdims=True)
    return (x - m) / jnp.sqrt(v + eps)

def _scatter_add(tgt, idx, src, axis=0):
    return tgt.at[idx].add(src)

def _segment_sum(src, seg, n):
    return jax.ops.segment_sum(src, seg, n)
kernel_name = 'mk_decoder_preln_d1_seqx_r4_968334'

def setup_inputs(seed: int=0):
    np.random.seed(seed)
    _w = jnp.asarray

    def _rec_inputs():
        import jax
        import jax.numpy as jnp
        _rk = jax.random.key(seed)
        x = 7.22e-05 + 1 * jax.random.normal(jax.random.fold_in(_rk, 1), (16, 256, 256), jnp.float32)
        _lenS = 256 - jax.random.randint(jax.random.fold_in(_rk, 7), (16,), 0, max(1, 256 // 4) + 1, jnp.int32)
        _lenS2 = 77 - jax.random.randint(jax.random.fold_in(_rk, 8), (16,), 0, max(1, 77 // 4) + 1, jnp.int32)
        _ctx_1024P = jax.random.normal(jax.random.fold_in(_rk, 11), (16, 16, 256), jnp.float32)
        _ctx_1024c = jax.random.dirichlet(jax.random.fold_in(_rk, 511), 0.3 * jnp.ones((16,), jnp.float32), (16, 77))
        _ctx_1024t = jnp.einsum('bsk,bkd->bsd', _ctx_1024c, _ctx_1024P)
        _ctx_1024t = _ctx_1024t * jax.lax.rsqrt(jnp.mean(jnp.square(_ctx_1024t)) + 1e-12) * 0.953939
        ctx_1024 = 4.13588e-05 + 0.999923 * (_ctx_1024t + 0.3 * jax.random.normal(jax.random.fold_in(_rk, 611), (16, 77, 256), jnp.float32))
        _validS = jnp.arange(256)[None, :] < _lenS[:, None]
        _validS2 = jnp.arange(77)[None, :] < _lenS2[:, None]
        _causal = jnp.tril(jnp.ones((256, 256), dtype=bool))
        mask_Bx1xSxS2_bf1 = jnp.ones((16, 1, 256, 77), dtype=bool)
        return (x, ctx_1024, mask_Bx1xSxS2_bf1)
    x, ctx_1024, mask_Bx1xSxS2_bf1 = _rec_inputs()

    def _L0_attn_setup():
        import jax, jax.numpy as jnp
        import numpy as np
        B, T, E, H = (2, 512, 256, 16)
        HD = E // H

        def _xavier(key, shape):
            limit = float(np.sqrt(6.0 / (shape[0] + shape[1])))
            return jax.random.uniform(key, shape, dtype=jnp.float32, minval=-limit, maxval=limit)
        key = jax.random.key(seed)
        kx, kq, kk, kv = jax.random.split(key, 4)
        return {'x': jax.random.normal(kx, (B, T, E), dtype=jnp.float32), 'w_Q': _xavier(kq, (E, E)), 'w_K': _xavier(kk, (E, E)), 'w_V': _xavier(kv, (E, E))}
    _L0_attn_all = _L0_attn_setup()
    _L0_attn_in = {k: v for k, v in _L0_attn_all.items() if k in ('w_Q', 'w_K', 'w_V')}
    del _L0_attn_all

    def _L0_xattn_setup():
        import jax, jax.numpy as jnp
        import numpy as np
        B, S, D, H = (4, 512, 256, 16)
        DK = D // H

        def _split_heads(x):
            b, s, _ = x.shape
            return x.reshape(b, s, H, DK).transpose(0, 2, 1, 3)
        key = jax.random.key(seed)
        ks = jax.random.split(key, 12)
        s = 0.02
        return {'query': jax.random.normal(ks[0], (B, S, D), jnp.float32), 'key': jax.random.normal(ks[1], (B, S, D), jnp.float32), 'value': jax.random.normal(ks[2], (B, S, D), jnp.float32), 'mask': jnp.ones((B, 1, S, S), dtype=bool), 'Wq': jax.random.normal(ks[3], (D, D), jnp.float32) * s, 'bq': jnp.zeros((D,), jnp.float32), 'Wk': jax.random.normal(ks[4], (D, D), jnp.float32) * s, 'bk': jnp.zeros((D,), jnp.float32), 'Wv': jax.random.normal(ks[5], (D, D), jnp.float32) * s, 'bv': jnp.zeros((D,), jnp.float32), 'Wo': jax.random.normal(ks[6], (D, D), jnp.float32) * s, 'bo': jnp.zeros((D,), jnp.float32)}
    _L0_xattn_all = _L0_xattn_setup()
    _L0_xattn_in = {k: v for k, v in _L0_xattn_all.items() if k in ('Wq', 'bq', 'Wk', 'bk', 'Wv', 'bv', 'Wo', 'bo')}
    del _L0_xattn_all

    def _L0_ffn_setup():
        import jax, jax.numpy as jnp
        import numpy as np
        B, S, D, E, F, K = (4, 256, 256, 8, 704, 1)
        key = jax.random.key(seed)
        ks = jax.random.split(key, 8)
        sc = 0.02
        return {'x_bsD': jax.random.normal(ks[0], (B, S, D), jnp.float32), 'router_DE': jax.random.normal(ks[1], (D, E), jnp.float32) * sc, 'w1_eDF': jax.random.normal(ks[2], (E, D, F), jnp.float32) * sc, 'w3_eDF': jax.random.normal(ks[3], (E, D, F), jnp.float32) * sc, 'w2_eFD': jax.random.normal(ks[4], (E, F, D), jnp.float32) * sc, 'ws1_DF': jax.random.normal(ks[5], (D, F), jnp.float32) * sc, 'ws3_DF': jax.random.normal(ks[6], (D, F), jnp.float32) * sc, 'ws2_FD': jax.random.normal(ks[7], (F, D), jnp.float32) * sc}
    _L0_ffn_all = _L0_ffn_setup()
    _L0_ffn_in = {k: v for k, v in _L0_ffn_all.items() if k in ('router_DE', 'w1_eDF', 'w3_eDF', 'w2_eFD', 'ws1_DF', 'ws3_DF', 'ws2_FD')}
    del _L0_ffn_all
    return {'x': x, 'ctx_1024': ctx_1024, 'mask_Bx1xSxS2_bf1': mask_Bx1xSxS2_bf1, 'L0_attn_w_Q': _L0_attn_in['w_Q'], 'L0_attn_w_K': _L0_attn_in['w_K'], 'L0_attn_w_V': _L0_attn_in['w_V'], 'L0_xattn_Wq': _L0_xattn_in['Wq'], 'L0_xattn_bq': _L0_xattn_in['bq'], 'L0_xattn_Wk': _L0_xattn_in['Wk'], 'L0_xattn_bk': _L0_xattn_in['bk'], 'L0_xattn_Wv': _L0_xattn_in['Wv'], 'L0_xattn_bv': _L0_xattn_in['bv'], 'L0_xattn_Wo': _L0_xattn_in['Wo'], 'L0_xattn_bo': _L0_xattn_in['bo'], 'L0_ffn_router_DE': _L0_ffn_in['router_DE'], 'L0_ffn_w1_eDF': _L0_ffn_in['w1_eDF'], 'L0_ffn_w3_eDF': _L0_ffn_in['w3_eDF'], 'L0_ffn_w2_eFD': _L0_ffn_in['w2_eFD'], 'L0_ffn_ws1_DF': _L0_ffn_in['ws1_DF'], 'L0_ffn_ws3_DF': _L0_ffn_in['ws3_DF'], 'L0_ffn_ws2_FD': _L0_ffn_in['ws2_FD']}

def reference(x, ctx_1024, mask_Bx1xSxS2_bf1, L0_attn_w_Q, L0_attn_w_K, L0_attn_w_V, L0_xattn_Wq, L0_xattn_bq, L0_xattn_Wk, L0_xattn_bk, L0_xattn_Wv, L0_xattn_bv, L0_xattn_Wo, L0_xattn_bo, L0_ffn_router_DE, L0_ffn_w1_eDF, L0_ffn_w3_eDF, L0_ffn_w2_eFD, L0_ffn_ws1_DF, L0_ffn_ws3_DF, L0_ffn_ws2_FD):
    import jax
    import jax.numpy as jnp

    def _L0_attn_ref(x, w_Q, w_K, w_V):
        import jax, jax.numpy as jnp
        import numpy as np
        B, T, E, H = (2, 512, 256, 16)
        HD = E // H

        def _xavier(key, shape):
            limit = float(np.sqrt(6.0 / (shape[0] + shape[1])))
            return jax.random.uniform(key, shape, dtype=jnp.float32, minval=-limit, maxval=limit)
        Bs, Ts, Es = x.shape
        q = (x @ w_Q).reshape(Bs, Ts, H, HD).transpose(0, 2, 1, 3)
        k = (x @ w_K).reshape(Bs, Ts, H, HD).transpose(0, 2, 1, 3)
        v = (x @ w_V).reshape(Bs, Ts, H, HD).transpose(0, 2, 1, 3)
        scores = jnp.einsum('bhtd,bhsd->bhts', q, k) / jnp.sqrt(jnp.asarray(HD, x.dtype))
        probs = jax.nn.softmax(scores, axis=-1)
        attn = jnp.einsum('bhts,bhsd->bhtd', probs, v)
        return attn.transpose(0, 2, 1, 3).reshape(Bs, Ts, H * HD)

    def _L0_xattn_ref(query, key, value, mask, Wq, bq, Wk, bk, Wv, bv, Wo, bo):
        import jax, jax.numpy as jnp
        import numpy as np
        B, S, D, H = (4, 512, 256, 16)
        DK = D // H

        def _split_heads(x):
            b, s, _ = x.shape
            return x.reshape(b, s, H, DK).transpose(0, 2, 1, 3)
        q = _split_heads(query @ Wq.T + bq)
        k = _split_heads(key @ Wk.T + bk)
        v = _split_heads(value @ Wv.T + bv)
        scores = jnp.einsum('bhqd,bhkd->bhqk', q, k) / jnp.sqrt(jnp.float32(DK))
        scores = jnp.where(mask, scores, jnp.float32(-1000000000.0))
        p = jax.nn.softmax(scores, axis=-1)
        out = jnp.einsum('bhqk,bhkd->bhqd', p, v)
        out = out.transpose(0, 2, 1, 3).reshape(query.shape[0], -1, D)
        return out @ Wo.T + bo

    def _L0_ffn_ref(x_bsD, router_DE, w1_eDF, w3_eDF, w2_eFD, ws1_DF, ws3_DF, ws2_FD):
        import jax, jax.numpy as jnp
        import numpy as np
        B, S, D, E, F, K = (4, 256, 256, 8, 704, 1)
        b, s, d = x_bsD.shape
        a = b * s
        x_aD = x_bsD.reshape(a, d)
        scores_aE = x_aD @ router_DE
        vals_aK, idx_aK = jax.lax.top_k(scores_aE, K)
        masked_aE = jnp.full_like(scores_aE, -jnp.inf).at[jnp.arange(a)[:, None], idx_aK].set(vals_aK)
        gates_Ea = jax.nn.sigmoid(masked_aE).T
        routed_in_EaD = jax.lax.stop_gradient(gates_Ea[:, :, None] * x_aD[None, :, :])
        mid_EaF = jax.nn.silu(jnp.einsum('ead,edf->eaf', routed_in_EaD, w1_eDF)) * jnp.einsum('ead,edf->eaf', routed_in_EaD, w3_eDF)
        routed_out_EaD = jnp.einsum('eaf,efd->ead', mid_EaF, w2_eFD)
        shared_aD = jax.nn.silu(x_aD @ ws1_DF) * (x_aD @ ws3_DF) @ ws2_FD
        out_aD = shared_aD + routed_out_EaD.sum(axis=0)
        return out_aD.reshape(b, s, d)
    x = x + _L0_attn_ref(_layernorm(x, axis=-1), L0_attn_w_Q, L0_attn_w_K, L0_attn_w_V)
    x = x + _L0_xattn_ref(_layernorm(x, axis=-1), ctx_1024, ctx_1024, mask_Bx1xSxS2_bf1, L0_xattn_Wq, L0_xattn_bq, L0_xattn_Wk, L0_xattn_bk, L0_xattn_Wv, L0_xattn_bv, L0_xattn_Wo, L0_xattn_bo)
    x = x + _L0_ffn_ref(_layernorm(x, axis=-1), L0_ffn_router_DE, L0_ffn_w1_eDF, L0_ffn_w3_eDF, L0_ffn_w2_eFD, L0_ffn_ws1_DF, L0_ffn_ws3_DF, L0_ffn_ws2_FD)
    return x

_drawn_inputs = setup_inputs


def setup_inputs(seed=0):
    import zlib

    import numpy as np

    out = dict(_drawn_inputs(seed))
    spreads = {'L0_xattn_bq': (0.0, 0.8),
     'L0_xattn_bk': (0.0, 2.0),
     'L0_xattn_bv': (0.0, 0.1),
     'L0_xattn_bo': (0.0, 0.1)}
    factors = {'L0_xattn_Wq': 8.0,
     'L0_xattn_Wk': 8.0,
     'L0_ffn_router_DE': 5.76,
     'L0_ffn_w1_eDF': 5.413,
     'L0_ffn_w3_eDF': 5.394,
     'L0_ffn_w2_eFD': 5.404,
     'L0_ffn_ws1_DF': 8.0,
     'L0_ffn_ws3_DF': 8.0,
     'L0_ffn_ws2_FD': 8.0}
    for name, (base, spread) in spreads.items():
        noise = np.random.default_rng([zlib.crc32(name.encode()), seed]).standard_normal(out[name].shape)
        drawn = base * np.exp(spread * noise) if base else spread * noise
        out[name] = jnp.asarray(drawn.astype(out[name].dtype))
    for name, factor in factors.items():
        out[name] = (out[name] * factor).astype(out[name].dtype)
    return out
```

```python
import numpy as np
import concourse.bass as bass
from concourse import mybir
from contextlib import ExitStack

F32 = mybir.dt.float32
F16 = mybir.dt.float16
BF16 = mybir.dt.bfloat16
I32 = mybir.dt.int32
U32 = mybir.dt.uint32
U8 = mybir.dt.uint8
ALU = mybir.AluOpType
ACT = mybir.ActivationFunctionType
AX = mybir.AxisListType

NB, S, D = 16, 256, 256
SC = 77
SCP = 80
H, HD = 16, 16
P = 128
TT = S // P
KD = D // P
NE, F = 8, 704
FT = -(-F // P)
FR = F - (FT - 1) * P
NTOK = NB * S
EPS = 1e-5
SCALE = float(HD) ** -0.5
NEG = 1e9
HP = 2 * HD * 1
KM = 3 * HD
KX = KM + 1
W1 = KD * F
W2 = FT * D
EW = 2 * W1 + W2
NSLOT = (NTOK + NE * (P - 1)) // P
FH = F // 2
PAD_ROW = NTOK


def frow(ft):
    return P if ft < FT - 1 else FR


class Batch:

    def __init__(self, j, c):
        self.j, self.c, self.par = j, c, c % 2
        self.b = j * 2 + c if not isinstance(j, int) else 2 * j + c

    def n(self, per, more):
        return self.j * (2 * per) + (per * self.c + more)

    def half(self, per, more):
        return self.j * per + (per * (self.c // 2) + more)


RING = 4
SLOTS_AHEAD = RING + 2


class Slot:

    def __init__(self, j, c):
        self.j, self.c, self.ring = j, c, c % RING
        self.s = j * RING + c

    def of(self, more):
        return Slot(self.j, self.c + more)

    def reads(self, more=0):
        return self.j * 16 + 16 * (self.c // RING + more)

    @property
    def exists(self):
        return not isinstance(self.s, int) or 0 <= self.s < NSLOT


def over_slots(eng, step):
    rounds = (NSLOT - 1 - SLOTS_AHEAD) // RING
    for s in range(SLOTS_AHEAD):
        step(Slot(0, s))
    with eng.Fori(0, rounds) as j:
        for c in range(RING):
            step(Slot(j, c + SLOTS_AHEAD))
    for s in range(SLOTS_AHEAD + rounds * RING, NSLOT + 1):
        step(Slot(0, s))


def at_least(eng, sem, value):
    if isinstance(value, int) and value <= 0:
        return
    eng.wait_ge(sem, value)


def decoder_layer(nc, x, ctx, mask, wq, wk, wv, xq, xbq, xk, xbk, xv, xbv, xo, xbo,
                  router, w1, w3, w2, s1, s3, s2, out):
    es = ExitStack()
    with es:
        def sem(name):
            return es.enter_context(nc.semaphore(name))

        TOTAL = 52800
        ALL = es.enter_context(nc.sbuf_tensor("ALL", [P, TOTAL], F32))
        BANKS = es.enter_context(nc.psum_tensor("BANKS", [P, 8, 512], F32))
        top = {"at": 0}

        def part(shape, dt=F32):
            per = int(np.prod(shape[1:]))
            size = {F32: 4, I32: 4, U32: 4, F16: 2, BF16: 2, U8: 1}[dt]
            words = -(-per * size // 32) * 8
            v = ALL[0:shape[0], top["at"]:top["at"] + words]
            top["at"] += words
            assert top["at"] <= TOTAL, top["at"]
            if dt != F32:
                v = v.bitcast(dt)
            v = v[:, 0:per]
            if len(shape) == 2:
                return v
            names = "abcd"[:len(shape) - 1]
            return v.rearrange(f"p ({' '.join(names)}) -> p {' '.join(names)}",
                               **{n: s for n, s in zip(names, shape[1:])})

        ident = part([P, P])
        identb = part([P, P], BF16)
        below = part([P, P], BF16)
        onesb = part([P, P], BF16)
        base = part([P, NE])
        e4096 = part([P, NE])
        erow = part([P, NE])
        slot_e = part([1, 64], I32)
        slot_i = part([1, 64], I32)
        consts_end = top["at"]
        experts = ALL[:, consts_end:consts_end + NE * EW]
        EARLY = 2

        top["at"] = consts_end + NE * EW
        G = part([P, RING, 2 * D])
        gT = part([P, 2, KD, P])
        th2 = part([P, F])
        u2 = part([P, F])
        mid2 = part([P, F])
        midT = part([P, FT, P])
        y2 = part([P, RING, D])
        idt = part([P, RING], I32)

        top["at"] = consts_end + EARLY * EW
        Wq, Wk, Wv = (part([P, KD, D]) for _ in range(3))
        Xq, Xk, Xv, Xo = (part([P, KD, D]) for _ in range(4))
        Wr = part([P, KD, NE])
        S1, S3 = part([P, KD, F]), part([P, KD, F])
        S2 = part([P, FT, D])
        bq, bk = part([P, KD]), part([P, KD])
        bv, bo = part([P, D]), part([P, D])
        mean77 = part([SC, P])
        xa, x1, x2 = part([P, 2, TT, D]), part([P, 2, TT, D]), part([P, 2, TT, D])
        R = part([P, 2, TT, 2 * D])
        xn = [part([P, TT, D]) for _ in range(3)]
        st, mv = part([P, 3, TT, 6]), part([P, 3, TT, 2])
        ve, rstd, mhalf = part([P, 3, TT]), part([P, 3, TT]), part([P, TT])
        xTa, xTb = part([P, KD, S]), part([P, KD, S])
        xTc = part([P, 2, KD, S])
        qh, ql, kh, kl = (part([P, KD, S], F16) for _ in range(4))
        q2h, q2l = (part([P, KD, S], F16) for _ in range(2))
        k2h, k2l = (part([P, KD, SCP], F16) for _ in range(2))
        Q1, K1 = part([P, 2, H // 2, S], F16), part([P, 2, H // 2, S], F16)
        Q2 = part([P, H // 2, S], F16)
        K2 = part([P, 2, H // 2, SCP], F16)
        V1 = part([P, 2, TT, H, HP])
        V2 = part([SC, 2, H, HP])
        vmean = part([P, 2, D])
        P1 = part([P, 8, TT, S])
        P2 = part([SC, 4, 2, S])
        OT = part([P, 4, S])
        m1, m2 = part([P, TT, H]), part([P, TT, H])
        neg1, neg2 = part([H, S], F16), part([H, S], F16)
        rden = part([P, H])
        tmp = part([P, D])
        attn = part([P, TT, D])
        aT = part([P, KD, S])
        xo1 = part([P, TT, D])
        cx = part([SC, 2, D])
        cT = part([P, KD, SCP])
        mk = part([P, 2, TT, SC], U8)
        madd = part([P, 2, TT, SCP], BF16)
        anyk, any9, nany = part([P, 2, TT]), part([P, TT]), part([P, 2, TT])
        lg = part([P, TT, NE])
        top8, idx8 = part([P, TT, 8]), part([P, TT, 8], U32)
        idxf = part([P, TT])
        oh = part([P, TT, NE], BF16)
        tg, gate = part([P, TT]), part([P, TT])
        pr, prm, posf = part([P, TT, NE]), part([P, TT, NE]), part([P, TT])
        posi, toki = part([P, 2, TT], I32), part([P, 2, TT], I32)
        tokf = part([P, TT])
        one_tok, one_tok2 = part([P, 1]), part([P, 1])
        thd, ud = part([P, 2, S]), part([P, 2, S])
        mid = part([P, FT, S])
        fill = part([P, NTOK * (NE + 1) // P], I32)
        zrow = part([1, 2 * D])
        cnt, cnti, tiles = part([1, NE]), part([1, NE], I32), part([1, NE])
        cum, cumb = part([1, NE]), part([1, NE])
        srow, acc, accb = part([1, 64]), part([1, 2, 64]), part([1, 2, 64])
        one8 = part([1, 64])

        qk_d = nc.dram_tensor("qk_parts", [4, D, S], F16, kind="Internal").ap()
        q2_d = nc.dram_tensor("q2_parts", [2, D, S], F16, kind="Internal").ap()
        k2_d = nc.dram_tensor("k2_parts", [2, D, SCP], F16, kind="Internal").ap()
        rows_d = nc.dram_tensor("token_rows", [NTOK + 1, 2 * D], F32, kind="Internal").ap()
        list_d = nc.dram_tensor("token_list", [NTOK * (NE + 1), 1], I32, kind="Internal").ap()

        loaded = sem("weights_loaded")
        loaded2 = sem("bias_loaded")
        early = sem("early_experts_loaded")
        late = sem("late_experts_loaded")
        consts = sem("constants_made")
        chain_c = sem("constants_chain")
        dram_init = sem("dram_initialised")
        x_in = [sem(f"x_loaded{i}") for i in range(2)]
        ln_v = [sem(f"ln{i}_variance") for i in range(3)]
        ln_r = [sem(f"ln{i}_rstd") for i in range(3)]
        ln_e = [sem(f"ln{i}_pool") for i in range(3)]
        ln_x = [sem(f"ln{i}_normed") for i in range(3)]
        a_full, a_free, a_hi = sem("a_bank_full"), sem("a_bank_free"), sem("a_high_parts")
        m_full, m_free, m_hi = sem("m_bank_full"), sem("m_bank_free"), sem("m_high_parts")
        a_wr, a_rd = sem("a_parts_written"), sem("a_stacks_built")
        c_wr, c_rd = sem("c_parts_written"), sem("c_stacks_built")
        sm_full = [sem(f"max_bank{i}_full") for i in range(2)]
        sm_free = [sem(f"max_bank{i}_free") for i in range(2)]
        ex_full = [sem(f"exp_bank{i}_full") for i in range(2)]
        ex_free = [sem(f"exp_bank{i}_free") for i in range(2)]
        mrow1, mrow2 = sem("max_row_self"), sem("max_row_cross")
        pv1, pv2 = sem("pv_self_done"), sem("pv_cross_done")
        attn_ready = sem("attn_ready")
        x1_done, mask_done = sem("x1_done"), sem("mask_done")
        top_found, onehot, gated = sem("top_found"), sem("onehot_ready"), sem("gate_tanh")
        pos_ready = sem("positions_ready")
        listed = [sem(f"tokens_listed{i}") for i in range(2)]
        ff_full = [sem(f"ff_bank{i}_full") for i in range(2)]
        ff_free = [sem(f"ff_bank{i}_free") for i in range(2)]
        ff_tanh = sem("ff_tanh")
        rows_out = [sem(f"rows_written{i}") for i in range(2)]
        dve = sem("vector_chain")
        table = sem("slot_table_ready")
        id_in = [sem(f"slot_ids_loaded{i}") for i in range(RING)]
        g_in = [sem(f"slot_rows_gathered{i}") for i in range(RING)]
        y_out = [sem(f"slot_rows_scattered{i}") for i in range(RING)]
        gt_full, gt_free = sem("slot_xT_full"), sem("slot_xT_free")
        h1_full, h3_full = sem("slot_h1_full"), sem("slot_h3_full")
        t_done, u_done, mid_done = sem("slot_tanh"), sem("slot_u"), sem("slot_mid")
        mt_full, mt_free = sem("slot_midT_full"), sem("slot_midT_free")
        y_full, y_ready = sem("slot_y_full"), sem("slot_y_ready")

        block = es.enter_context(nc.Block())

        A_XT, A_Q, A_K, A_V, A_CT, A_K2, A_V2, A_VM, A_N = range(9)
        (M_MT, M_O0, M_O1, M_T0, M_T1, M_XT, M_Q2, M_MT2, M_P0, M_P1, M_U0, M_U1, M_AT, M_OP,
         M_X3, M_RT, M_RK, M_N) = range(18)
        MF = {u: n for n, u in enumerate(u for u in range(M_N) if u not in (M_O0, M_O1, M_P0, M_P1))}
        MFN = len(MF)
        X_N = 12
        bankA, bankM = BANKS[:, 5, :], BANKS[:, 4, :]
        CONSTS = 1
        A_WR, A_RD, C_WR, C_RD = 6 * 16, 18 * 16, 2 * 16, 6 * 16

        def plain_wait(eng, sem_, value):
            if isinstance(value, int):
                at_least(eng, sem_, value)
                return
            with eng.register() as r:
                eng.reg_mov(r, value)
                eng.wait_ge(consts, CONSTS)
                eng.wait_ge(sem_, r)

        def split(ap, n):
            return ap.rearrange("p (n s) -> p n s", n=n)

        class Chain:

            def __init__(self, eng, start):
                self.eng, self.start, self.k = eng, start, 0

            def __call__(self, ins, before_plain=False):
                self.k += 1
                ins.then_inc(dve, 1)
                if before_plain:
                    plain_wait(self.eng, dve, self.start + self.k)
                else:
                    self.eng.wait_ge(dve, self.start + self.k)

        LINKS = {"A": 5, "B": 6, "C": 22, "D": 7}
        LINK_N = sum(LINKS.values())

        ITERATIONS = NB + 2

        def stages(i_j, i_c):
            i = i_c if isinstance(i_j, int) else None
            def live(d):
                return i is None or 0 <= i - d < NB
            return [Batch(i_j, i_c - d) if live(d) else None for d in range(3)]

        def over_batches(eng, body):
            for i in range(4):
                body(*stages(0, i))
            with eng.Fori(2, NB // 2) as j:
                for c in range(2):
                    body(*stages(j, c))
            for i in range(NB, NB + 2):
                body(*stages(0, i))

        def load_expert(eng, e, sem_):
            o = e * EW
            W = experts
            eng.dma_start(W[:, o:o + W1].rearrange("p (k n) -> p k n", k=KD),
                          w1[e].rearrange("(k p) n -> p k n", p=P)).then_inc(sem_, 16)
            eng.dma_start(W[:, o + W1:o + 2 * W1].rearrange("p (k n) -> p k n", k=KD),
                          w3[e].rearrange("(k p) n -> p k n", p=P)).then_inc(sem_, 16)
            eng.dma_start(W[:, o + 2 * W1:o + 2 * W1 + (FT - 1) * D].rearrange("p (k n) -> p k n", n=D),
                          w2[e, 0:(FT - 1) * P, :].rearrange("(k p) n -> p k n", p=P)).then_inc(sem_, 16)
            eng.dma_start(W[0:FR, o + 2 * W1 + (FT - 1) * D:o + EW],
                          w2[e, (FT - 1) * P:F, :]).then_inc(sem_, 16)

        @block.sync
        def _(sp):
            for dst, src in ((Wq, wq), (Wk, wk), (Wv, wv), (Xk, xk), (Xv, xv), (Xq, xq), (Xo, xo),
                             (Wr, router), (S1, s1), (S3, s3)):
                sp.dma_start(dst, src.rearrange("(k p) n -> p k n", p=P)).then_inc(loaded, 16)
            sp.dma_start(S2[:, 0:FT - 1, :], s2[0:(FT - 1) * P, :].rearrange("(k p) n -> p k n", p=P)).then_inc(loaded, 16)
            sp.dma_start(S2[0:FR, FT - 1, :], s2[(FT - 1) * P:F, :]).then_inc(loaded, 16)

            def load(B):
                plain_wait(sp, x1_done, B.n(1, -1))
                plain_wait(sp, a_full, B.n(A_N, A_CT + 1 - 2 * A_N))
                plain_wait(sp, mask_done, B.n(1, -1))
                sp.dma_start(xa[:, B.par], x[B.b].rearrange("(t p) d -> p t d", p=P)).then_inc(x_in[B.par], 16)
                sp.dma_start(cx[:, B.par], ctx[B.b]).then_inc(x_in[B.par], 16)
                sp.dma_start(mk[:, B.par], mask[B.b, 0].rearrange("(t p) c -> p t c", p=P)).then_inc(x_in[B.par], 16)

            def put_parts(dram, n, part_, sem_):
                sp.dma_start(dram[n].rearrange("(g p) t -> p g t", p=P), part_).then_inc(sem_, 16)

            def stack(dst, dram, order, width, sem_):
                for k in range(2):
                    for n, o in enumerate(order):
                        src = dram[o].rearrange("(g k r) t -> k r g t", k=2, r=HD)[k]
                        sp.dma_start(dst[64 * k + HD * n:64 * k + HD * n + HD, :, 0:width],
                                     src[:, :, 0:width]).then_inc(sem_, 16)

            def stack_a(B):
                plain_wait(sp, a_rd, B.n(A_RD, 0))
                plain_wait(sp, a_free, B.n(A_N, A_K + 1))
                for n, p_ in enumerate((qh, ql, kh, kl)):
                    put_parts(qk_d, n, p_, a_wr)
                plain_wait(sp, a_free, B.n(A_N, A_K2 + 1))
                for n, p_ in enumerate((k2h, k2l)):
                    sp.dma_start(k2_d[n].rearrange("(g p) t -> p g t", p=P)[:, :, 0:SC], p_[:, :, 0:SC]).then_inc(a_wr, 16)
                plain_wait(sp, a_wr, B.n(A_WR, A_WR))
                stack(Q1[:, B.par], qk_d, (0, 1, 0), S, a_rd)
                stack(K1[:, B.par], qk_d, (2, 2, 3), S, a_rd)
                stack(K2[:, B.par], k2_d, (0, 0, 1), SC, a_rd)

            def max_row(dst, src, sem_):
                for k in range(2):
                    sp.dma_start(dst[64 * k + KM:64 * k + KM + 1].rearrange("p g s -> p (g s)"),
                                 src[8 * k:8 * k + 8, :]).then_inc(sem_, 16)

            def row_self(B):
                plain_wait(sp, m_free, B.n(M_N, M_MT + 1))
                max_row(Q1[:, B.par], neg1, mrow1)

            def stack_c(B):
                plain_wait(sp, c_rd, B.n(C_RD, 0))
                plain_wait(sp, m_free, B.n(M_N, M_Q2 + 1))
                put_parts(q2_d, 0, q2h, c_wr)
                put_parts(q2_d, 1, q2l, c_wr)
                plain_wait(sp, c_wr, B.n(C_WR, C_WR))
                stack(Q2, q2_d, (0, 1, 0), S, c_rd)

            def row_cross(B):
                plain_wait(sp, m_free, B.n(M_N, M_MT2 + 1))
                max_row(Q2, neg2, mrow2)

            def rows(B):
                plain_wait(sp, ff_free[0], B.n(4, 4))
                sp.dma_start(rows_d[0:NTOK].rearrange("(b t p) c -> b p t c", t=TT, p=P)[B.b],
                             R[:, B.par]).then_inc(rows_out[B.par], 16)

            load(Batch(0, 0))
            load(Batch(0, 1))

            def body(A, B, Dd):
                if B is not None:
                    row_self(B)
                if A is not None:
                    stack_a(A)
                if B is not None:
                    stack_c(B)
                    row_cross(B)
                if Dd is not None:
                    rows(Dd)

            for i in range(4):
                body(*stages(0, i))
                if i >= 1:
                    load(Batch(0, i + 1))
            with sp.Fori(2, NB // 2 - 1) as j:
                for c in range(2):
                    body(*stages(j, c))
                    load(Batch(j, c + 1))
            for i in range(NB - 2, NB + 2):
                body(*stages(0, i))
                if i + 1 < NB:
                    load(Batch(0, i + 1))

            for eng_sem in rows_out:
                sp.wait_ge(eng_sem, 16 * NB // 2)
            sp.wait_ge(table, 1)
            for e in range(EARLY, NE):
                load_expert(sp, e, late)

            def load_ids(q):
                plain_wait(sp, y_out[q.ring], q.reads())
                at = slot_i[0:1, q.s:q.s + 1] if isinstance(q.s, int) else slot_i[0:1, bass.ds(q.s, 1)]
                r = sp.value_load(at, min_val=0, max_val=NTOK * (NE + 1) - P)
                sp.dma_start(idt[:, q.ring:q.ring + 1], list_d[bass.ds(r, P), :]).then_inc(id_in[q.ring], 16)

            over_slots(sp, lambda q: load_ids(q) if q.exists else None)

        @block.tensor
        def _(pe):
            mm = pe.matmul
            pe.wait_ge(loaded, 12 * 16)
            pe.wait_ge(consts, CONSTS)

            def transpose_tokens(src, bank, full):
                for k in range(KD):
                    for t in range(TT):
                        last = pe.transpose(bank[:, k * S + t * P:k * S + t * P + P],
                                            src[:, t, k * P:k * P + P], ident)
                last.then_inc(full, 1)

            def project_T(bank, W, xT, full, width=S, step=S):
                for g in range(KD):
                    for k in range(KD):
                        last = mm(bank[:, g * step:g * step + width], W[:, k, g * P:g * P + P],
                                  xT[:, k, 0:width], start=(k == 0), stop=(k == KD - 1))
                last.then_inc(full, 1)

            def project(bank, W, xT, full):
                for t in range(TT):
                    for k in range(KD):
                        last = mm(bank[:, t * D:t * D + D], xT[:, k, t * P:t * P + P], W[:, k, :],
                                  start=(k == 0), stop=(k == KD - 1))
                last.then_inc(full, 1)

            def a_use(B, u):
                at_least(pe, a_free, B.n(A_N, u))

            def stage_a1(B):
                pe.wait_ge(ln_x[0], B.n(1, 1))
                a_use(B, A_XT)
                transpose_tokens(xn[0], bankA, a_full)
                pe.wait_ge(x_in[B.par], B.half(48, 48))
                a_use(B, A_Q)
                project_T(bankA, Wq, xTa, a_full)

            def stage_a2(B):
                a_use(B, A_K)
                project_T(bankA, Wk, xTa, a_full)

            def stage_a3(B):
                a_use(B, A_V)
                project(bankA, Wv, xTa, a_full)

            def stage_a4(B):
                a_use(B, A_CT)
                for k in range(KD):
                    last = pe.transpose(bankA[:, k * SCP:k * SCP + SC], cx[:, B.par, k * P:k * P + P],
                                        ident[0:SC, 0:SC])
                last.then_inc(a_full, 1)

            def stage_a5(B):
                a_use(B, A_K2)
                project_T(bankA, Xk, cT, a_full, SC, SCP)

            def stage_a6(B):
                a_use(B, A_V2)
                for k in range(KD):
                    last = mm(bankA[0:SC, 0:D], cT[:, k, 0:SC], Xv[:, k, :], start=(k == 0), stop=(k == KD - 1))
                last.then_inc(a_full, 1)

            def stage_a7(B):
                a_use(B, A_VM)
                mm(split(bankA[:, 0:D], H), mean77, V2[:, B.par, :, 0:HD], start=True, stop=True).then_inc(a_full, 1)

            def m_use(B, u):
                at_least(pe, m_free, B.n(M_N, u))

            def max_head(B, h):
                k, g = h % 2, h // 2
                at_least(pe, sm_free[k], B.n(X_N, g))
                for t in range(TT):
                    last = mm(BANKS[:, k, t * S:t * S + S], Q1[64 * k:64 * k + KM, B.par, g, t * P:t * P + P],
                              K1[64 * k:64 * k + KM, B.par, g, :], start=True, stop=True)
                last.then_inc(sm_full[k], 1)

            def max_T(B, m, u, done):
                for k in range(2):
                    pe.wait_ge(sm_free[k], B.n(X_N, done))
                m_use(B, u)
                for t in range(TT):
                    last = pe.transpose(bankM[0:H, t * P:t * P + P], m[:, t, :], ident)
                last.then_inc(m_full, 1)

            def exp_head(B, h):
                k, g = h % 2, h // 2
                at_least(pe, ex_free[k], B.n(X_N, g))
                for t in range(TT):
                    last = mm(BANKS[:, 2 + k, t * S:t * S + S], K1[64 * k:64 * k + KX, B.par, g, t * P:t * P + P],
                              Q1[64 * k:64 * k + KX, B.par, g, :], start=True, stop=True)
                last.then_inc(ex_full[k], 1)

            def pv_self(B, q):
                for k in range(2):
                    pe.wait_ge(ex_free[k], B.n(X_N, 2 * q + 2))
                if q % 2 == 0:
                    m_use(B, M_O0 + q // 2)
                for t in range(TT):
                    for j in range(4):
                        h = 4 * q + j
                        last = mm(bankM[32 * j:32 * j + 32, (q % 2) * S:(q % 2) * S + S],
                                  V1[:, B.par, t, h, :], P1[:, h % 8, t, :], start=(t == 0), stop=(t == TT - 1))
                last.then_inc(pv1, 1)

            def heads_T(B, t, u):
                m_use(B, u)
                for q in range(4):
                    last = pe.transpose(bankM[:, q * P:q * P + P], OT[:, q, t * P:t * P + P], ident)
                last.then_inc(m_full, 1)

            def q_cross1(B):
                pe.wait_ge(ln_x[1], B.n(1, 1))
                m_use(B, M_XT)
                transpose_tokens(xn[1], bankM, m_full)

            def q_cross2(B):
                m_use(B, M_Q2)
                project_T(bankM, Xq, xTb, m_full)

            def max_cross(B, v):
                k, quad, t = v % 2, (v // 2) % 2, v // 4
                at_least(pe, sm_free[k], B.n(X_N, 8 + v // 2))
                ob = split(BANKS[:, k, 0:4 * SC], 4)
                mm(ob, identb, madd[:, B.par, t, 0:SC].unsqueeze(1).broadcast_to([P, 4, SC]), start=True, stop=False,
                   skip_group_check=True)
                for i in range(4):
                    g = 4 * quad + i
                    last = mm(ob[:, i, :], Q2[64 * k:64 * k + KM, g, t * P:t * P + P],
                              K2[64 * k:64 * k + KM, B.par, g, 0:SC], start=False, stop=True,
                              skip_group_check=True)
                last.then_inc(sm_full[k], 1)

            def exp_cross(B, v):
                k, w = v % 2, v // 2
                at_least(pe, ex_free[k], B.n(X_N, 8 + w))
                ob = split(BANKS[0:SC, 2 + k, :], 2)
                for t in range(TT):
                    mm(ob[:, :, t * P:t * P + P], madd[:, B.par, t, 0:SC],
                       identb.unsqueeze(1).broadcast_to([P, 2, P]), start=(t == 0), stop=False,
                       skip_group_check=True)
                for i in range(2):
                    last = mm(ob[:, i, :], K2[64 * k:64 * k + KX, B.par, 2 * w + i, 0:SC],
                              Q2[64 * k:64 * k + KX, 2 * w + i, :], start=False, stop=True,
                              skip_group_check=True)
                last.then_inc(ex_full[k], 1)

            def pv_cross(B, w):
                for k in range(2):
                    pe.wait_ge(ex_free[k], B.n(X_N, 8 + w + 1))
                if w % 2 == 0:
                    m_use(B, M_P0 + w // 2)
                for j in range(4):
                    last = mm(bankM[32 * j:32 * j + 32, (w % 2) * S:(w % 2) * S + S],
                              V2[:, B.par, 4 * w + j, :], P2[:, (2 * w + j % 2) % 4, j // 2, :], start=True, stop=True)
                last.then_inc(pv2, 1)

            def attn_T(B):
                m_use(B, M_AT)
                pe.wait_ge(attn_ready, B.n(1, 1))
                transpose_tokens(attn, bankM, m_full)

            def out_proj(B):
                m_use(B, M_OP)
                project(bankM, Xo, aT, m_full)

            def x3_T(B):
                pe.wait_ge(ln_x[2], B.n(1, 1))
                m_use(B, M_X3)
                transpose_tokens(xn[2], bankM, m_full)

            def route(B):
                m_use(B, M_RT)
                for t in range(TT):
                    for k in range(KD):
                        last = mm(bankM[:, t * NE:t * NE + NE], xTc[:, B.par, k, t * P:t * P + P], Wr[:, k, :],
                                  start=(k == 0), stop=(k == KD - 1))
                last.then_inc(m_full, 1)

            def rank(B):
                pe.wait_ge(onehot, B.n(1, 1))
                m_use(B, M_RK)
                mm(bankM[:, 0:NE], below, oh[:, 0, :], start=True, stop=True)
                mm(bankM[:, NE:2 * NE], below, oh[:, 1, :], start=True, stop=False)
                mm(bankM[:, NE:2 * NE], onesb, oh[:, 0, :], start=False, stop=True)
                mm(bankM[:, 2 * NE:3 * NE], onesb, oh[:, 0, :], start=True, stop=False)
                mm(bankM[:, 2 * NE:3 * NE], onesb, oh[:, 1, :], start=False, stop=True).then_inc(m_full, 1)

            def ff_up(B, f):
                k, r = f % 2, frow(f)
                at_least(pe, ff_free[k], B.n(4 - k, f // 2))
                for n, W in enumerate((S1, S3)):
                    for c in range(KD):
                        last = mm(BANKS[0:r, 6 + k, n * S:n * S + S], W[:, c, f * P:f * P + r],
                                  xTc[:, B.par, c, :], start=(c == 0), stop=(c == KD - 1))
                last.then_inc(ff_full[k], 1)

            def ff_down(B):
                pe.wait_ge(ff_free[0], B.n(4, 3))
                pe.wait_ge(ff_free[1], B.n(3, 3))
                for t in range(TT):
                    for f in range(FT):
                        r = frow(f)
                        last = mm(BANKS[:, 6, t * D:t * D + D], mid[0:r, f, t * P:t * P + P], S2[0:r, f, :],
                                  start=(f == 0), stop=(f == FT - 1))
                last.then_inc(ff_full[0], 1)

            def body(A, B, Dd):
                def on(stage, step, *args):
                    if stage is not None:
                        step(stage, *args)

                if B is not None:
                    pe.wait_ge(a_rd, B.n(A_RD, A_RD))
                for h in range(H):
                    on(B, max_head, h)
                    if h % 3 == 2:
                        on(Dd, ff_up, h // 3)
                on(B, max_T, m1, M_MT, 8)
                on(Dd, ff_up, 5)
                on(A, stage_a1)
                on(A, stage_a2)
                if B is not None:
                    pe.wait_ge(mrow1, B.n(32, 32))
                for q in range(5):
                    for h in range(4 * q, min(4 * q + 4, H)):
                        on(B, exp_head, h)
                    if q == 1:
                        on(A, stage_a3)
                    if q == 2:
                        on(A, stage_a4)
                    if q == 3:
                        on(A, stage_a5)
                    if q > 0:
                        on(B, pv_self, q - 1)
                on(A, stage_a6)
                on(B, heads_T, 0, M_T0)
                on(A, stage_a7)
                on(B, heads_T, 1, M_T1)
                on(B, q_cross1)
                on(B, q_cross2)
                on(Dd, ff_down)
                if B is not None:
                    pe.wait_ge(c_rd, B.n(C_RD, C_RD))
                    pe.wait_ge(mask_done, B.n(1, 1))
                for v in range(8):
                    on(B, max_cross, v)
                on(B, max_T, m2, M_MT2, X_N)
                if B is not None:
                    pe.wait_ge(mrow2, B.n(32, 32))
                for w in range(5):
                    if w < 4:
                        on(B, exp_cross, 2 * w)
                        on(B, exp_cross, 2 * w + 1)
                    if w > 0:
                        on(B, pv_cross, w - 1)
                on(B, heads_T, 0, M_U0)
                on(B, heads_T, 1, M_U1)
                on(B, attn_T)
                on(B, out_proj)
                on(B, x3_T)
                on(B, route)
                on(B, rank)

            over_batches(pe, body)

            pe.wait_ge(early, 64 * EARLY)
            pe.wait_ge(late, 64 * (NE - EARLY))
            pe.wait_ge(table, 1)
            pe.wait_ge(m_free, NB * M_N)
            pe.wait_ge(ff_free[0], NB * 4)

            def slot_xT(q):
                pe.wait_ge(g_in[q.ring], q.reads(1))
                at_least(pe, gt_free, q.s)
                for k in range(KD):
                    last = pe.transpose(BANKS[:, 6, k * P:k * P + P], G[:, q.ring, k * P:k * P + P], ident)
                last.then_inc(gt_full, 1)

            def slot_up(q, e, first, bank, full):
                for n in range(2):
                    for k in range(KD):
                        last = mm(BANKS[:, bank + n, 0:FH], gT[:, q.ring % 2, k, :],
                                  experts[:, bass.ds(e + (first + k * F + n * FH), FH)],
                                  start=(k == 0), stop=(k == KD - 1))
                last.then_inc(full, 1)

            def slot_midT(q):
                pe.wait_ge(mid_done, q.s + 1)
                at_least(pe, mt_free, q.s)
                for f in range(FT):
                    r = frow(f)
                    last = pe.transpose(BANKS[0:r, 4 + f // 3, (f % 3) * P:(f % 3) * P + P],
                                        mid2[:, f * P:f * P + r], ident)
                last.then_inc(mt_full, 1)

            def slot_down(q, e):
                pe.wait_ge(mt_free, q.s + 1)
                at_least(pe, y_ready, q.s)
                for f in range(FT):
                    r = frow(f)
                    last = mm(BANKS[:, 7, 0:D], midT[0:r, f, :],
                              experts[0:r, bass.ds(e + (2 * W1 + f * D), D)],
                              start=(f == 0), stop=(f == FT - 1))
                last.then_inc(y_full, 1)

            def entry(q):
                at = slot_e[0:1, q.s:q.s + 1] if isinstance(q.s, int) else slot_e[0:1, bass.ds(q.s, 1)]
                return pe.value_load(at, min_val=0, max_val=(NE - 1) * EW)

            def step(q):
                after, before = q.of(1), q.of(-1)
                if after.exists:
                    slot_xT(after)
                if q.exists:
                    e = entry(q)
                    pe.wait_ge(gt_free, q.s + 1)
                    at_least(pe, u_done, q.s)
                    slot_up(q, e, 0, 0, h1_full)
                if before.exists:
                    slot_midT(before)
                if q.exists:
                    slot_up(q, e, W1, 2, h3_full)
                if before.exists:
                    slot_down(before, entry(before))

            slot_xT(Slot(0, 0))
            over_slots(pe, step)

        @block.scalar
        def _(act):
            def copy(dst, src, sem_, scale=1.0):
                act.activation(dst, src, ACT.Copy, scale=scale).then_inc(sem_, 1)

            def parts_hi(dst, bank, bias, width, step, sem_):
                for g in range(KD):
                    act.activation(dst[:, g, 0:width], bank[:, g * step:g * step + width], ACT.Identity,
                                   bias=bias[:, g:g + 1]).then_inc(sem_, 1)

            act.wait_ge(loaded2, 64)
            act.wait_ge(consts, CONSTS)

            def a_xT(B):
                act.wait_ge(a_full, B.n(A_N, A_XT + 1))
                copy(xTa.rearrange("p k s -> p (k s)"), bankA, a_free)

            def a_q(B):
                act.wait_ge(a_full, B.n(A_N, A_Q + 1))
                at_least(act, a_wr, B.n(A_WR, 0))
                copy(qh.rearrange("p k s -> p (k s)"), bankA, a_hi)

            def a_k(B):
                act.wait_ge(a_full, B.n(A_N, A_K + 1))
                copy(kh.rearrange("p k s -> p (k s)"), bankA, a_hi)

            def a_v(B):
                act.wait_ge(a_full, B.n(A_N, A_V + 1))
                for t in range(TT):
                    ins = act.activation(V1[:, B.par, t, :, 0:HD], split(bankA[:, t * D:t * D + D], H), ACT.Copy)
                ins.then_inc(a_free, 1)

            def a_cT(B):
                act.wait_ge(a_full, B.n(A_N, A_CT + 1))
                copy(cT[:, :, 0:SC], split(bankA[:, 0:KD * SCP], KD)[:, :, 0:SC], a_free)

            def a_k2(B):
                act.wait_ge(a_full, B.n(A_N, A_K2 + 1))
                parts_hi(k2h, bankA, bk, SC, SCP, a_hi)

            def a_vm(B):
                act.wait_ge(a_full, B.n(A_N, A_VM + 1))
                copy(vmean[:, B.par], bankA[:, 0:D], a_free)

            def neg(B, u, dst, row_sem):
                act.wait_ge(m_full, B.n(MFN, MF[u] + 1))
                at_least(act, row_sem, B.n(32, 0))
                copy(dst, bankM[0:H, 0:S], m_free, scale=-1.0)

            def exp_head(B, h):
                k, g = h % 2, h // 2
                act.wait_ge(ex_full[k], B.n(X_N, g + 1))
                if h % 4 == 0:
                    at_least(act, pv1, B.n(4, h // 4 - 1))
                act.activation(P1[:, h % 8].rearrange("p t s -> p (t s)"), BANKS[:, 2 + k, :], ACT.Exp,
                               scale=SCALE).then_inc(ex_free[k], 1)

            def exp_cross(B, v):
                k, w = v % 2, v // 2
                act.wait_ge(ex_full[k], B.n(X_N, 8 + w + 1))
                if k == 0:
                    at_least(act, pv2, B.n(4, w - 1))
                act.activation(P2[:, v % 4].rearrange("p t s -> p (t s)"), BANKS[0:SC, 2 + k, :], ACT.Exp,
                               scale=SCALE).then_inc(ex_free[k], 1)

            def heads(B, u, pv_sem):
                act.wait_ge(pv_sem, B.n(4, 2 * u + 2))
                copy(OT[:, 2 * u:2 * u + 2, :].rearrange("p q s -> p (q s)"), bankM, m_free)

            def m_copy(B, u, dst):
                act.wait_ge(m_full, B.n(MFN, MF[u] + 1))
                copy(dst.rearrange("p k s -> p (k s)"), bankM, m_free)

            def q_cross(B):
                act.wait_ge(m_full, B.n(MFN, MF[M_Q2] + 1))
                at_least(act, c_wr, B.n(C_WR, 0))
                parts_hi(q2h, bankM, bq, S, S, m_hi)

            def gate_tanh(B):
                act.wait_ge(top_found, B.n(1, 1))
                act.activation(tg, top8[:, :, 0], ACT.Tanh, scale=0.5).then_inc(gated, 1)

            def ff(B, f):
                k, r = f % 2, frow(f)
                act.wait_ge(ff_full[k], B.n(4 - k, f // 2 + 1))
                if f >= 2:
                    act.wait_ge(ff_free[k], B.n(4 - k, f // 2))
                else:
                    at_least(act, ff_free[k], B.n(4 - k, 0))
                act.activation(thd[0:r, k, :], BANKS[0:r, 6 + k, 0:S], ACT.Tanh, scale=0.5).then_inc(ff_tanh, 1)

            def body(A, B, Dd):
                def on(stage, step, *args):
                    if stage is not None:
                        step(stage, *args)

                for f in range(5):
                    on(Dd, ff, f)
                on(B, neg, M_MT, neg1, mrow1)
                on(Dd, ff, 5)
                on(A, a_xT)
                on(A, a_q)
                on(A, a_k)
                for q in range(5):
                    for h in range(4 * q, min(4 * q + 4, H)):
                        on(B, exp_head, h)
                    if q == 1:
                        on(A, a_v)
                    if q == 2:
                        on(A, a_cT)
                    if q == 3:
                        on(A, a_k2)
                    if q in (2, 4):
                        on(B, heads, q // 2 - 1, pv1)
                on(A, a_vm)
                on(B, m_copy, M_XT, xTb)
                on(B, q_cross)
                on(B, neg, M_MT2, neg2, mrow2)
                for w in range(5):
                    if w < 4:
                        on(B, exp_cross, 2 * w)
                        on(B, exp_cross, 2 * w + 1)
                    if w in (2, 4):
                        on(B, heads, w // 2 - 1, pv2)
                on(B, m_copy, M_AT, aT)
                if B is not None:
                    act.wait_ge(m_full, B.n(MFN, MF[M_X3] + 1))
                    copy(xTc[:, B.par].rearrange("p k s -> p (k s)"), bankM, m_free)
                on(B, gate_tanh)

            over_batches(act, body)
            act.wait_ge(dve, NB * LINK_N)
            act.wait_ge(ff_free[0], NB * 4)
            act.wait_ge(m_free, NB * M_N)
            act.wait_ge(table, 1)

            def slot_xT(q):
                act.wait_ge(gt_full, q.s + 1)
                copy(gT[:, q.ring % 2].rearrange("p k s -> p (k s)"), BANKS[:, 6, 0:KD * P], gt_free)

            def slot_tanh(q):
                act.wait_ge(h1_full, q.s + 1)
                at_least(act, u_done, q.s)
                act.activation(split(th2, 2), BANKS[:, 0:2, 0:FH], ACT.Tanh, scale=0.5).then_inc(t_done, 1)

            def slot_midT(q):
                act.wait_ge(mt_full, q.s + 1)
                act.activation(midT[:, 0:3, :].rearrange("p f s -> p (f s)"), BANKS[:, 4, 0:3 * P], ACT.Copy)
                act.activation(midT[:, 3:FT - 1, :].rearrange("p f s -> p (f s)"), BANKS[:, 5, 0:2 * P], ACT.Copy)
                act.activation(midT[0:FR, FT - 1, :], BANKS[0:FR, 5, 2 * P:3 * P], ACT.Copy).then_inc(mt_free, 1)

            def step(q):
                if q.of(1).exists:
                    slot_xT(q.of(1))
                if q.exists:
                    slot_tanh(q)
                if q.of(-1).exists:
                    slot_midT(q.of(-1))

            slot_xT(Slot(0, 0))
            over_slots(act, step)

        @block.vector
        def _(v):
            v.wait_ge(consts, CONSTS)
            v.wait_ge(loaded2, 64)

            def normed(B, n, src, link):
                for t in range(TT):
                    ins = v.bn_stats(st[:, n, t, :], src[:, t, :])
                link(ins, True)
                for t in range(TT):
                    ins = v.bn_aggr(mv[:, n, t, :], st[:, n, t, :])
                link(ins)
                v.tensor_scalar(ve[:, n, :], mv[:, n, :, 1], EPS, None, ALU.add).then_inc(ln_v[n], 1)
                v.wait_ge(ln_r[n], B.n(1, 1))
                if n:
                    at_least(v, m_full, B.n(MFN, MF[(M_XT, M_X3)[n - 1]] + 1 - MFN))
                else:
                    at_least(v, a_full, B.n(A_N, A_XT + 1 - A_N))
                for t in range(TT):
                    ins = v.tensor_scalar(xn[n][:, t, :], src[:, t, :], mv[:, n, t, 0:1], rstd[:, n, t:t + 1],
                                          ALU.subtract, ALU.mult)
                ins.then_inc(ln_x[n], 1)

            def parts_lo(dst, bank, hi, free):
                v.tensor_tensor(dst.rearrange("p k s -> p (k s)"), bank, hi.rearrange("p k s -> p (k s)"),
                                ALU.subtract).then_inc(free, 1)

            def parts_lo_bias(dst, bank, bias, hi, width, step, free):
                for g in range(KD):
                    ins = v.scalar_tensor_tensor(dst[:, g, 0:width], bank[:, g * step:g * step + width],
                                                 bias[:, g:g + 1], hi[:, g, 0:width], ALU.add, ALU.subtract)
                ins.then_inc(free, 1)

            def a_norm(B, link):
                v.wait_ge(x_in[B.par], B.half(48, 48))
                normed(B, 0, xa[:, B.par], link)

            def a_mask(B, link):
                at_least(v, ex_full[0], B.n(X_N, -X_N))
                at_least(v, ex_full[1], B.n(X_N, -X_N))
                link(v.tensor_reduce(anyk[:, B.par, :], mk[:, B.par], AX.X, ALU.max))
                v.tensor_scalar(nany[:, B.par, :], anyk[:, B.par, :], -1.0, 1.0, ALU.mult, ALU.add)
                link(v.tensor_scalar(any9, anyk[:, B.par, :], NEG, None, ALU.mult))
                for t in range(TT):
                    ins = v.tensor_scalar(madd[:, B.par, t, 0:SC], mk[:, B.par, t, :], 1.0, any9[:, t:t + 1],
                                          ALU.subtract, ALU.mult)
                ins.then_inc(mask_done, 1)

            def a_q(B, link):
                v.wait_ge(a_hi, B.n(4, 1))
                at_least(v, a_wr, B.n(A_WR, 0))
                parts_lo(ql, bankA, qh, a_free)

            def a_k(B, link):
                v.wait_ge(a_hi, B.n(4, 2))
                parts_lo(kl, bankA, kh, a_free)

            def a_k2(B, link):
                v.wait_ge(a_hi, B.n(4, 4))
                parts_lo_bias(k2l, bankA, bk, k2h, SC, SCP, a_free)

            def a_v2(B, link):
                v.wait_ge(a_full, B.n(A_N, A_V2 + 1))
                v.tensor_tensor(V2[:, B.par, :, 0:HD], split(bankA[0:SC, 0:D], H), split(bv[0:SC], H), ALU.add)\
                    .then_inc(a_free, 1)
                link(v.tensor_copy(one_tok, tokf[:, 0:1]))

            def max_head(B, h):
                k, g = h % 2, h // 2
                v.wait_ge(sm_full[k], B.n(X_N, g + 1))
                v.tensor_reduce(m1[:, :, 8 * k + g], split(BANKS[:, k, :], TT), AX.X, ALU.max).then_inc(sm_free[k], 1)

            def normalise(B, t, u, link, scale=None):
                v.wait_ge(m_full, B.n(MFN, MF[u] + 1))
                heads = split(bankM, H)
                link(v.reciprocal(rden, heads[:, :, HD]))
                if scale is not None:
                    link(v.tensor_scalar(rden, rden, scale, None, ALU.mult))
                v.tensor_tensor(split(tmp, H), heads[:, :, 0:HD], rden.unsqueeze(2).broadcast_to([P, H, HD]),
                                ALU.mult).then_inc(m_free, 1)
                v.wait_ge(m_free, B.n(M_N, u + 1))

            def x1_tile(B, t, link):
                normalise(B, t, M_T0 + t, link)
                link(v.tensor_tensor(x1[:, B.par, t, :], xa[:, B.par, t, :], tmp, ALU.add))

            def x1_norm(B, link):
                v.tensor_copy(one_tok, tokf[:, 0:1]).then_inc(x1_done, 1)
                normed(B, 1, x1[:, B.par], link)

            def q_cross(B, link):
                v.wait_ge(m_hi, B.n(2, 2))
                at_least(v, c_wr, B.n(C_WR, 0))
                parts_lo_bias(q2l, bankM, bq, q2h, S, S, m_free)

            def max_cross(B, n):
                k, quad, t = n % 2, (n // 2) % 2, n // 4
                v.wait_ge(sm_full[k], B.n(X_N, 8 + n // 2 + 1))
                v.tensor_reduce(m2[:, t, 8 * k + 4 * quad:8 * k + 4 * quad + 4], split(BANKS[:, k, 0:4 * SC], 4),
                                AX.X, ALU.max).then_inc(sm_free[k], 1)

            def attn_tile(B, t, link):
                normalise(B, t, M_U0 + t, link, anyk[:, B.par, t:t + 1])
                link(v.scalar_tensor_tensor(attn[:, t, :], vmean[:, B.par], nany[:, B.par, t:t + 1], tmp,
                                            ALU.mult, ALU.add))
                if t == TT - 1:
                    v.tensor_copy(one_tok, tokf[:, 0:1]).then_inc(attn_ready, 1)

            def x2_tile(B, link):
                v.wait_ge(m_full, B.n(MFN, MF[M_OP] + 1))
                v.tensor_tensor(xo1, split(bankM, TT), bo.unsqueeze(1).broadcast_to([P, TT, D]), ALU.add)\
                    .then_inc(m_free, 1)
                v.wait_ge(m_free, B.n(M_N, M_OP + 1))
                link(v.tensor_tensor(x2[:, B.par], xo1, x1[:, B.par], ALU.add))

            def route(B, link):
                v.wait_ge(m_full, B.n(MFN, MF[M_RT] + 1))
                v.tensor_copy(lg.rearrange("p t e -> p (t e)"), bankM[:, 0:TT * NE]).then_inc(m_free, 1)
                plain_wait(v, m_free, B.n(M_N, M_RT + 1))
                for t in range(TT):
                    link(v.max(top8[:, t, :], lg[:, t, :]), True)
                for t in range(TT):
                    link(v.max_index(idx8[:, t, :], top8[:, t, :], lg[:, t, :]), t == 0)
                link(v.tensor_copy(idxf, idx8[:, :, 0]))
                v.tensor_copy(one_tok, tokf[:, 0:1]).then_inc(top_found, 1)
                for t in range(TT):
                    ins = v.tensor_scalar(oh[:, t, :], erow, idxf[:, t:t + 1], None, ALU.is_equal)
                ins.then_inc(onehot, 1)
                v.wait_ge(gated, B.n(1, 1))
                link(v.tensor_scalar(gate, tg, 0.5, 0.5, ALU.mult, ALU.add))
                at_least(v, rows_out[B.par], B.half(16, 0))
                for t in range(TT):
                    ins = v.tensor_scalar(R[:, B.par, t, 0:D], xn[2][:, t, :], gate[:, t:t + 1], None, ALU.mult)
                link(ins)

            def rank(B, link):
                v.wait_ge(m_full, B.n(MFN, MF[M_RK] + 1))
                link(v.tensor_tensor(pr, split(bankM[:, 0:TT * NE], TT), base.unsqueeze(1).broadcast_to([P, TT, NE]),
                                     ALU.add))
                link(v.tensor_tensor(prm, pr, oh, ALU.mult))
                link(v.tensor_reduce(posf, prm, AX.X, ALU.add))
                at_least(v, listed[B.par], B.half(32, 0))
                link(v.tensor_copy(posi[:, B.par, :], posf))
                link(v.tensor_copy(toki[:, B.par, :], tokf))
                link(v.tensor_scalar(tokf, tokf, float(S), None, ALU.add))
                v.tensor_copy(one_tok, tokf[:, 0:1]).then_inc(pos_ready, 1)
                v.tensor_tensor(base, base, bankM[:, 2 * NE:3 * NE], ALU.add).then_inc(m_free, 1)

            def ff(B, f, link):
                k, r = f % 2, frow(f)
                v.wait_ge(ff_tanh, B.n(FT, f + 1))
                link(v.scalar_tensor_tensor(ud[0:r, k, :], thd[0:r, k, :], 1.0, BANKS[0:r, 6 + k, 0:S],
                                            ALU.add, ALU.mult))
                if f == 0:
                    at_least(v, ff_full[0], B.n(4, 0))
                v.scalar_tensor_tensor(mid[0:r, f, :], ud[0:r, k, :], 0.5, BANKS[0:r, 6 + k, S:2 * S],
                                       ALU.mult, ALU.mult).then_inc(ff_free[k], 1)

            def ff_out(B, link):
                v.wait_ge(ff_full[0], B.n(4, 4))
                v.tensor_tensor(R[:, B.par, :, D:2 * D], split(BANKS[:, 6, :], TT), x2[:, B.par], ALU.add)\
                    .then_inc(ff_free[0], 1)
                link(v.tensor_copy(one_tok, tokf[:, 0:1]))

            def body(A, B, Dd):
                anchor = B or A or Dd
                if A is not None and B is None:
                    start = 0
                elif A is not None and Dd is None:
                    start = LINKS["A"]
                elif A is not None:
                    start = LINKS["A"] * 2 + LINKS["B"] + LINKS["C"] + (Dd.n(LINK_N, 0))
                elif B is not None:
                    start = LINKS["A"] * NB + (LINKS["B"] + LINKS["C"]) * (NB - 1) + LINKS["D"] * (NB - 2)
                else:
                    start = LINK_N * NB - LINKS["D"]
                link = Chain(v, start)

                def on(stage, step, *args):
                    if stage is not None:
                        step(stage, *args)

                for h in range(H):
                    on(B, max_head, h)
                    if h % 3 == 2:
                        on(Dd, ff, h // 3, link)
                on(A, a_norm, link)
                on(A, a_mask, link)
                on(Dd, ff, 5, link)
                on(A, a_q, link)
                on(A, a_k, link)
                on(A, a_k2, link)
                on(A, a_v2, link)
                on(B, x1_tile, 0, link)
                on(B, x1_tile, 1, link)
                on(B, x1_norm, link)
                on(B, q_cross, link)
                on(Dd, ff_out, link)
                for n in range(8):
                    on(B, max_cross, n)
                on(B, attn_tile, 0, link)
                on(B, attn_tile, 1, link)
                on(B, x2_tile, link)
                if B is not None:
                    normed(B, 2, x2[:, B.par], link)
                on(B, route, link)
                on(B, rank, link)
                want = sum(LINKS[n] for n, s in (("A", A), ("B", B), ("C", B), ("D", Dd)) if s is not None)
                assert link.k == want, (link.k, want, A is None, B is None, Dd is None)

            over_batches(v, body)

            t0 = [NB * LINK_N]

            def link(ins):
                t0[0] += 1
                ins.then_inc(dve, 1)
                v.wait_ge(dve, t0[0])

            v.wait_ge(m_free, NB * M_N)
            link(v.tensor_tensor(cnt, base[0:1], e4096[0:1], ALU.subtract))
            link(v.tensor_scalar(cnt, cnt, float(P - 1), None, ALU.add))
            link(v.tensor_copy(cnti, cnt))
            link(v.tensor_scalar(cnti, cnti, 7, None, ALU.logical_shift_right))
            link(v.tensor_copy(tiles, cnti))
            link(v.tensor_copy(cum, tiles))
            for e in range(1, NE):
                link(v.tensor_tensor(cum[:, e:e + 1], cum[:, e:e + 1], cum[:, e - 1:e], ALU.add))
            link(v.memset(acc.rearrange("p a s -> p (a s)"), 0.0))
            for e in range(NE):
                link(v.tensor_scalar(accb[:, 0, :], srow, cum[:, e:e + 1], None, ALU.is_ge))
                link(v.tensor_tensor(acc[:, 0, :], acc[:, 0, :], accb[:, 0, :], ALU.add))
                link(v.scalar_tensor_tensor(acc[:, 1, :], accb[:, 0, :], tiles[:, e:e + 1], acc[:, 1, :],
                                            ALU.mult, ALU.add))
            link(v.tensor_tensor(accb[:, 1, :], srow, acc[:, 1, :], ALU.subtract))
            link(v.tensor_scalar(accb[:, 1, :], accb[:, 1, :], float(P), None, ALU.mult))
            link(v.scalar_tensor_tensor(accb[:, 0, :], acc[:, 0, :], float(NTOK), accb[:, 1, :], ALU.mult, ALU.add))
            link(v.tensor_copy(slot_i, accb[:, 0, :]))
            link(v.tensor_scalar(acc[:, 0, :], acc[:, 0, :], float(NE - 1), float(EW), ALU.min, ALU.mult))
            link(v.tensor_copy(slot_e, acc[:, 0, :]))
            for half in listed:
                v.wait_ge(half, 32 * NB // 2)
            v.memset(one_tok2, 0.0).then_inc(table, 1)

            def slot_u(q):
                v.wait_ge(t_done, q.s + 1)
                at_least(v, mid_done, q.s)
                v.scalar_tensor_tensor(split(u2, 2), split(th2, 2), 1.0, BANKS[:, 0:2, 0:FH], ALU.add, ALU.mult)\
                    .then_inc(u_done, 1)
                v.wait_ge(u_done, q.s + 1)
                v.wait_ge(h3_full, q.s + 1)
                at_least(v, mt_full, q.s)
                v.scalar_tensor_tensor(split(mid2, 2), split(u2, 2), 0.5, BANKS[:, 2:4, 0:FH], ALU.mult, ALU.mult)\
                    .then_inc(mid_done, 1)

            def slot_y(q):
                v.wait_ge(y_full, q.s + 1)
                at_least(v, y_out[q.ring], q.reads())
                v.tensor_tensor(y2[:, q.ring, :], BANKS[:, 7, 0:D], G[:, q.ring, D:2 * D], ALU.add).then_inc(y_ready, 1)

            def step(q):
                if q.exists:
                    slot_u(q)
                if q.of(-1).exists:
                    slot_y(q.of(-1))

            over_slots(v, step)

        @block.gpsimd
        def _(g):
            k = [0]

            def made(ins):
                k[0] += 1
                ins.then_inc(chain_c, 1)
                g.wait_ge(chain_c, k[0])

            for dst, src in ((bv, xbv), (bo, xbo)):
                g.dma_start(dst, src.rearrange("(a n) -> a n", a=1).broadcast_to([P, D])).then_inc(loaded2, 16)
            for dst, src in ((bq, xbq), (bk, xbk)):
                g.dma_start(dst, src.rearrange("(k p) -> p k", p=P), allow_slow_non_contiguous=True).then_inc(loaded2, 16)

            made(g.memset(ident, 0.0))
            made(g.affine_select(out=ident, in_=ident, compare_op=ALU.not_equal, fill=1.0, base=0,
                                 pattern=[[-1, P]], channel_multiplier=1))
            made(g.tensor_copy(identb, ident))
            made(g.memset(onesb, 1.0))
            made(g.memset(below, 0.0))
            made(g.affine_select(out=below, in_=below, compare_op=ALU.is_ge, fill=1.0, base=0,
                                 pattern=[[-1, P]], channel_multiplier=1))
            made(g.memset(mean77, 1.0 / SC))
            made(g.memset(mhalf, -0.5))
            made(g.iota(erow, [[1, NE]], base=0, channel_multiplier=0, allow_small_or_imprecise_dtypes=True))
            made(g.iota(e4096, [[NTOK, NE]], base=0, channel_multiplier=0, allow_small_or_imprecise_dtypes=True))
            made(g.tensor_copy(base, e4096))
            made(g.iota(srow, [[1, 64]], base=0, channel_multiplier=0, allow_small_or_imprecise_dtypes=True))
            made(g.iota(tokf, [[P, TT]], base=0, channel_multiplier=1, allow_small_or_imprecise_dtypes=True))
            made(g.memset(V1.rearrange("p a t h d -> p (a t h d)"), 0.0))
            made(g.memset(V1.rearrange("p a t h d -> p (a t h) d")[:, :, HD], 1.0))
            made(g.memset(V2.rearrange("p a h d -> p (a h d)"), 0.0))
            made(g.memset(V2.rearrange("p a h d -> p (a h) d")[:, :, HD], 1.0))
            made(g.memset(K1.rearrange("p a h s -> p (a h s)"), 1.0))
            made(g.memset(K2.rearrange("p a h s -> p (a h s)"), 1.0))
            made(g.memset(one_tok, 0.0))
            made(g.iota(fill, [[0, NTOK * (NE + 1) // P]], base=PAD_ROW, channel_multiplier=0))
            made(g.memset(zrow, 0.0))
            g.memset(one_tok2, 0.0).then_inc(consts, 1)
            g.wait_ge(consts, 1)
            g.dma_start(list_d.rearrange("(p n) a -> p (n a)", p=P), fill).then_inc(dram_init, 16)
            g.dma_start(rows_d[NTOK:NTOK + 1, :], zrow).then_inc(dram_init, 16)
            for e in range(EARLY):
                load_expert(g, e, early)
            g.wait_ge(dram_init, 32)

            def rstd_of(B, n):
                plain_wait(g, ln_v[n], B.n(1, 1))
                g.tensor_tensor(rstd[:, n, :], ve[:, n, :], mhalf, ALU.pow).then_inc(ln_r[n], 1)

            def list_tokens(B):
                plain_wait(g, pos_ready, B.n(1, 1))
                for t in range(TT):
                    g.indirect_dma_start(out=list_d, out_offset=bass.IndirectOffsetOnAxis(ap=posi[:, B.par, t:t + 1], axis=0),
                                         in_=toki[:, B.par, t:t + 1], in_offset=None).then_inc(listed[B.par], 16)

            def body(A, B, Dd):
                if A is not None:
                    rstd_of(A, 0)
                if B is not None:
                    rstd_of(B, 1)
                    rstd_of(B, 2)
                    list_tokens(B)

            over_batches(g, body)
            for half in listed:
                g.wait_ge(half, 32 * NB // 2)
            g.wait_ge(table, 1)

            def gather(q):
                plain_wait(g, id_in[q.ring], q.reads(1))
                plain_wait(g, y_ready, q.s - RING + 1)
                g.indirect_dma_start(out=G[:, q.ring, :], out_offset=None, in_=rows_d,
                                     in_offset=bass.IndirectOffsetOnAxis(ap=idt[:, q.ring:q.ring + 1], axis=0))\
                    .then_inc(g_in[q.ring], 16)

            def scatter(q):
                plain_wait(g, y_ready, q.s + 1)
                g.indirect_dma_start(out=out, out_offset=bass.IndirectOffsetOnAxis(ap=idt[:, q.ring:q.ring + 1], axis=0),
                                     in_=y2[:, q.ring, :], in_offset=None, bounds_check=NTOK - 1, oob_is_err=False)\
                    .then_inc(y_out[q.ring], 16)

            def step(q):
                if q.of(1).exists:
                    gather(q.of(1))
                if q.of(-1).exists:
                    scatter(q.of(-1))

            gather(Slot(0, 0))
            over_slots(g, step)
            for r in range(RING):
                g.wait_ge(y_out[r], 16 * ((NSLOT - r + RING - 1) // RING))


def kernel(x, ctx_1024, mask_Bx1xSxS2_bf1, L0_attn_w_Q, L0_attn_w_K, L0_attn_w_V,
           L0_xattn_Wq, L0_xattn_bq, L0_xattn_Wk, L0_xattn_bk, L0_xattn_Wv, L0_xattn_bv,
           L0_xattn_Wo, L0_xattn_bo, L0_ffn_router_DE, L0_ffn_w1_eDF, L0_ffn_w3_eDF, L0_ffn_w2_eFD,
           L0_ffn_ws1_DF, L0_ffn_ws3_DF, L0_ffn_ws2_FD):
    import concourse.bacc as bacc
    from concourse.bass_utils import run_bass_kernel_spmd

    def T(w):
        return np.ascontiguousarray(np.asarray(w).T)

    given = {
        "x": x, "ctx": ctx_1024, "mask": np.asarray(mask_Bx1xSxS2_bf1).view(np.uint8),
        "wq": L0_attn_w_Q, "wk": L0_attn_w_K, "wv": L0_attn_w_V,
        "xq": T(L0_xattn_Wq), "xbq": L0_xattn_bq, "xk": T(L0_xattn_Wk), "xbk": L0_xattn_bk,
        "xv": T(L0_xattn_Wv), "xbv": L0_xattn_bv, "xo": T(L0_xattn_Wo), "xbo": L0_xattn_bo,
        "router": L0_ffn_router_DE, "w1": L0_ffn_w1_eDF, "w3": L0_ffn_w3_eDF, "w2": L0_ffn_w2_eFD,
        "s1": L0_ffn_ws1_DF, "s3": L0_ffn_ws3_DF, "s2": L0_ffn_ws2_FD,
    }
    nc = bacc.Bacc("TRN2", target_bir_lowering=False, num_devices=1)
    arrays, aps = {}, {}
    for name, a in given.items():
        a = np.ascontiguousarray(np.asarray(a))
        arrays["in_" + name] = a
        aps[name] = nc.dram_tensor("in_" + name, a.shape, mybir.dt.from_np(a.dtype), kind="ExternalInput").ap()
    out = nc.dram_tensor("out", (NTOK, D), F32, kind="ExternalOutput").ap()
    decoder_layer(nc, out=out, **aps)
    r = run_bass_kernel_spmd(nc, [arrays], core_ids=[0])
    return r.results[0]["out"].reshape(NB, S, D)
```

```python
import numpy as np
import concourse.bass as bass
from concourse import mybir
from contextlib import ExitStack

F32 = mybir.dt.float32
F16 = mybir.dt.float16
BF16 = mybir.dt.bfloat16
I32 = mybir.dt.int32
U32 = mybir.dt.uint32
U8 = mybir.dt.uint8
ALU = mybir.AluOpType
ACT = mybir.ActivationFunctionType
AX = mybir.AxisListType

NB, S, D = 16, 256, 256
SC = 77
SCP = 80
H, HD = 16, 16
P = 128
TT = S // P
KD = D // P
NE, F = 8, 704
FT = -(-F // P)
FR = F - (FT - 1) * P
NTOK = NB * S
EPS = 1e-5
SCALE = float(HD) ** -0.5
NEG = 1e9
HP = 2 * HD * 1
KM = 3 * HD
KX = KM + 1
W1 = KD * F
W2 = FT * D
EW = 2 * W1 + W2
NSLOT = (NTOK + NE * (P - 1)) // P
FH = F // 2
PAD_ROW = NTOK


def frow(ft):
    return P if ft < FT - 1 else FR


A, B, C, E, D_ = range(5)
LAST = NB + D_


def live(stage, i):
    return 0 <= i - stage < NB


class Batch:

    def __init__(self, stage, j, i):
        self.stage, self.j, self.i = stage, j, i
        self.c = i - stage
        self.par, self.b = self.c % 2, 2 * j + self.c

    def n(self, per, more):
        return self.j * (2 * per) + (per * self.c + more)

    def half(self, per, more):
        return self.j * per + (per * (self.c // 2) + more)


def before_iteration(per, j, i):
    if isinstance(j, int):
        return sum(n * min(max(i - stage, 0), NB) for stage, n in per.items())
    return j * (2 * sum(per.values())) + sum(n * (i - stage) for stage, n in per.items())


class Uses:

    def __init__(self, order, but=()):
        self.order = [u for u in order if u[1] not in but]
        self.per = {s: sum(u[0] == s for u in self.order) for s, _ in self.order}

    def before(self, batch, name):
        at = self.order.index((batch.stage, name))
        here = sum(not isinstance(batch.j, int) or live(s, batch.i) for s, _ in self.order[:at])
        return before_iteration(self.per, batch.j, batch.i) + here

    def after(self, batch, name):
        return self.before(batch, name) + 1


RING = 6
GATHER = 3
SLOTS_AHEAD = RING + 2


class Slot:

    def __init__(self, j, c):
        self.j, self.c, self.ring = j, c, c % RING
        self.s = j * RING + c

    def of(self, more):
        return Slot(self.j, self.c + more)

    def reads(self, more=0):
        return self.j * 16 + 16 * (self.c // RING + more)

    @property
    def exists(self):
        return not isinstance(self.s, int) or 0 <= self.s < NSLOT


def over_slots(eng, step):
    rounds = (NSLOT - GATHER - SLOTS_AHEAD) // RING
    for s in range(SLOTS_AHEAD):
        step(Slot(0, s))
    with eng.Fori(0, rounds) as j:
        for c in range(RING):
            step(Slot(j, c + SLOTS_AHEAD))
    for s in range(SLOTS_AHEAD + rounds * RING, NSLOT + 1):
        step(Slot(0, s))


def at_least(eng, sem, value):
    if isinstance(value, int) and value <= 0:
        return
    eng.wait_ge(sem, value)


def decoder_layer(nc, x, ctx, mask, wq, wk, wv, xq, xbq, xk, xbk, xv, xbv, xo, xbo,
                  router, w1, w3, w2, s1, s3, s2, out):
    es = ExitStack()
    with es:
        def sem(name):
            return es.enter_context(nc.semaphore(name))

        TOTAL = 52800
        ALL = es.enter_context(nc.sbuf_tensor("ALL", [P, TOTAL], F32))
        BANKS = es.enter_context(nc.psum_tensor("BANKS", [P, 8, 512], F32))
        top = {"at": 0}

        def part(shape, dt=F32):
            per = int(np.prod(shape[1:]))
            size = {F32: 4, I32: 4, U32: 4, F16: 2, BF16: 2, U8: 1}[dt]
            words = -(-per * size // 32) * 8
            v = ALL[0:shape[0], top["at"]:top["at"] + words]
            top["at"] += words
            assert top["at"] <= TOTAL, top["at"]
            if dt != F32:
                v = v.bitcast(dt)
            v = v[:, 0:per]
            if len(shape) == 2:
                return v
            names = "abcd"[:len(shape) - 1]
            return v.rearrange(f"p ({' '.join(names)}) -> p {' '.join(names)}",
                               **{n: s for n, s in zip(names, shape[1:])})

        ident = part([P, P])
        identb = part([P, P], BF16)
        below = part([P, P], BF16)
        onesb = part([P, P], BF16)
        base = part([P, NE])
        e4096 = part([P, NE])
        erow = part([P, NE])
        slot_e = part([1, 64], I32)
        slot_i = part([1, 64], I32)
        slot_n = part([1, 64], I32)
        consts_end = top["at"]
        experts = ALL[:, consts_end:consts_end + NE * EW]
        EARLY = 2

        top["at"] = consts_end + NE * EW
        G = part([P, RING, 2 * D])
        gT = part([P, 2, KD, P])
        th2 = part([P, F])
        u2 = part([P, F])
        mid2 = part([P, F])
        midT = part([P, FT, P])
        y2 = part([P, RING, D])
        idt = part([P, RING], I32)

        top["at"] = consts_end + EARLY * EW
        Wq, Wk, Wv = (part([P, KD, D]) for _ in range(3))
        Xq, Xk, Xv, Xo = (part([P, KD, D]) for _ in range(4))
        Wr = part([P, KD, NE])
        S1, S3 = part([P, KD, F]), part([P, KD, F])
        S2 = part([P, FT, D])
        bq, bk = part([P, KD]), part([P, KD])
        bv, bo = part([P, D]), part([P, D])
        mean77 = part([SC, P])
        xa, x1, x2 = part([P, 2, TT, D]), part([P, 2, TT, D]), part([P, 2, TT, D])
        R = part([P, 2, TT, 2 * D])
        xn = [part([P, TT, D]) for _ in range(3)]
        st, mv = part([P, 3, TT, 6]), part([P, 3, TT, 2])
        ve, rstd, mhalf = part([P, 3, TT]), part([P, 3, TT]), part([P, TT])
        xTa, xTb = part([P, KD, S]), part([P, KD, S])
        xTc = part([P, 2, KD, S])
        qh, ql, kh, kl = (part([P, KD, S], F16) for _ in range(4))
        q2h, q2l = (part([P, KD, S], F16) for _ in range(2))
        k2h, k2l = (part([P, KD, SCP], F16) for _ in range(2))
        Q1, K1 = part([P, 2, H // 2, S], F16), part([P, 2, H // 2, S], F16)
        Q2 = part([P, H // 2, S], F16)
        K2 = part([P, 2, H // 2, SCP], F16)
        V1 = part([P, 2, TT, H, HP])
        V2 = part([SC, 2, H, HP])
        vmean = part([P, 2, D])
        P1 = part([P, 8, TT, S])
        P2 = part([SC, 4, 2, S])
        OT, OT2 = part([P, 4, S]), part([P, 4, S])
        m1, m2 = part([P, TT, H]), part([P, TT, H])
        neg1, neg2 = part([H, S], F16), part([H, S], F16)
        rden = part([P, H])
        tmp = part([P, D])
        attn = part([P, TT, D])
        aT = part([P, KD, S])
        xo1 = part([P, TT, D])
        cx = part([SC, 2, D])
        cT = part([P, KD, SCP])
        mk = part([P, 2, TT, SC], U8)
        madd = part([P, 2, TT, SCP], BF16)
        anyk, any9, nany = part([P, 2, TT]), part([P, TT]), part([P, 2, TT])
        lg = part([P, TT, NE])
        top8, idx8 = part([P, TT, 8]), part([P, TT, 8], U32)
        idxf = part([P, TT])
        oh = part([P, TT, NE], BF16)
        tg, gate = part([P, TT]), part([P, TT])
        pr, prm, posf = part([P, TT, NE]), part([P, TT, NE]), part([P, TT])
        posi, toki = part([P, 2, TT], I32), part([P, 2, TT], I32)
        tokf = part([P, TT])
        one_tok, one_tok2 = part([P, 1]), part([P, 1])
        thd, ud = part([P, 2, S]), part([P, 2, S])
        mid = part([P, FT, S])
        fill = part([P, NTOK * (NE + 1) // P], I32)
        zrow = part([P, 2 * D // P])
        cnt, cnti, tiles = part([1, NE]), part([1, NE], I32), part([1, NE])
        cum = part([1, NE])
        srow, acc, accb = part([1, 64]), part([1, 2, 64]), part([1, 2, 64])

        qk_d = nc.dram_tensor("qk_parts", [4, D, S], F16, kind="Internal").ap()
        q2_d = nc.dram_tensor("q2_parts", [2, D, S], F16, kind="Internal").ap()
        k2_d = nc.dram_tensor("k2_parts", [2, D, SCP], F16, kind="Internal").ap()
        rows_d = nc.dram_tensor("token_rows", [NTOK + 1, 2 * D], F32, kind="Internal").ap()
        list_d = nc.dram_tensor("token_list", [NTOK * (NE + 1), 1], I32, kind="Internal").ap()

        loaded = sem("weights_loaded")
        loaded2 = sem("bias_loaded")
        early = sem("early_experts_loaded")
        late = [sem(f"expert{e}_loaded") for e in range(NE)]
        experts_ready = sem("experts_ready")
        consts = sem("constants_made")
        chain_c = sem("constants_chain")
        dram_init = sem("dram_initialised")
        x_in = [sem(f"x_loaded{i}") for i in range(2)]
        ln_v = [sem(f"ln{i}_variance") for i in range(3)]
        ln_r = [sem(f"ln{i}_rstd") for i in range(3)]
        ln_e = [sem(f"ln{i}_pool") for i in range(3)]
        ln_x = [sem(f"ln{i}_normed") for i in range(3)]
        a_full, a_free, a_hi = sem("a_bank_full"), sem("a_bank_free"), sem("a_high_parts")
        m_full, m_free, m_hi = sem("m_bank_full"), sem("m_bank_free"), sem("m_high_parts")
        a_wr, a_rd = sem("a_parts_written"), sem("a_stacks_built")
        k_wr, k_rd, k_hi = sem("k2_parts_written"), sem("k2_stack_built"), sem("k2_high_parts")
        c_in = [sem(f"context_loaded{i}") for i in range(2)]
        c_wr, c_rd = sem("c_parts_written"), sem("c_stacks_built")
        sm_full = [sem(f"max_bank{i}_full") for i in range(2)]
        sm_free = [sem(f"max_bank{i}_free") for i in range(2)]
        ex_full = [sem(f"exp_bank{i}_full") for i in range(2)]
        ex_free = [sem(f"exp_bank{i}_free") for i in range(2)]
        mrow1, mrow2 = sem("max_row_self"), sem("max_row_cross")
        pv1, pv2 = sem("pv_self_done"), sem("pv_cross_done")
        attn_ready = sem("attn_ready")
        x1_done, mask_done = sem("x1_done"), sem("mask_done")
        top_found, onehot, gated = sem("top_found"), sem("onehot_ready"), sem("gate_tanh")
        pos_ready = sem("positions_ready")
        listed = [sem(f"tokens_listed{i}") for i in range(2)]
        ff_full = [sem(f"ff_bank{i}_full") for i in range(2)]
        ff_free = [sem(f"ff_bank{i}_free") for i in range(2)]
        ff_tanh = sem("ff_tanh")
        rows_out = [sem(f"rows_written{i}") for i in range(2)]
        dve = sem("vector_chain")
        table = sem("slot_table_ready")
        id_in = [sem(f"slot_ids_loaded{i}") for i in range(RING)]
        g_in = [sem(f"slot_rows_gathered{i}") for i in range(RING)]
        y_out = [sem(f"slot_rows_scattered{i}") for i in range(RING)]
        gt_full, gt_free = sem("slot_xT_full"), sem("slot_xT_free")
        h1_full, h3_full = sem("slot_h1_full"), sem("slot_h3_full")
        t_done, u_done, mid_done = sem("slot_tanh"), sem("slot_u"), sem("slot_mid")
        mt_full, mt_free = sem("slot_midT_full"), sem("slot_midT_free")
        y_full, y_ready = sem("slot_y_full"), sem("slot_y_ready")

        block = es.enter_context(nc.Block())

        M_ORDER = [(B, "maxT"), (C, "maxT"), (B, "O0"), (B, "O1"), (B, "T0"), (B, "T1"), (B, "xT"), (B, "q")]
        A_ORDER = [(E, "out"), (E, "xT"), (E, "route"), (E, "rank"),
                   (A, "xT"), (A, "q"), (A, "k"), (A, "v"), (B, "ctxT"), (B, "k2"), (B, "v2"),
                   (C, "P0"), (C, "P1"), (B, "mean"), (C, "T0"), (C, "T1"), (C, "attnT")]
        M_FREE, M_FULL = Uses(M_ORDER), Uses(M_ORDER, ("O0", "O1"))
        A_FREE, A_FULL = Uses(A_ORDER), Uses(A_ORDER, ("P0", "P1"))
        X = Uses([(B, n) for n in range(8)] + [(C, n) for n in range(4)])
        bankA, bankM = BANKS[:, 5, :], BANKS[:, 4, :]
        CONSTS = 1
        A_WR, A_RD, K_WR, K_RD, C_WR, C_RD = (16 * n for n in (4, 12, 2, 6, 2, 6))

        def plain_wait(eng, sem_, value):
            if isinstance(value, int):
                at_least(eng, sem_, value)
                return
            with eng.register() as r:
                eng.reg_mov(r, value)
                eng.wait_ge(consts, CONSTS)
                eng.wait_ge(sem_, r)

        def split(ap, n):
            return ap.rearrange("p (n s) -> p n s", n=n)

        class Chain:

            def __init__(self, eng, start):
                self.eng, self.start, self.k = eng, start, 0

            def __call__(self, ins, before_plain=False):
                self.k += 1
                ins.then_inc(dve, 1)
                if before_plain:
                    plain_wait(self.eng, dve, self.start + self.k)
                else:
                    self.eng.wait_ge(dve, self.start + self.k)

        LINKS = {A: 2, B: 9, C: 6, E: 15, D_: 7}

        def over_iterations(eng, body):
            for i in range(6):
                body(0, i)
            with eng.Fori(3, NB // 2) as j:
                for i in range(2):
                    body(j, i)
            for i in range(NB, LAST):
                body(0, i)

        class Iteration:

            def __init__(self, j, i):
                self.j, self.i = j, i

            def __call__(self, stage, step, *args):
                if not isinstance(self.j, int) or live(stage, self.i):
                    step(Batch(stage, self.j, self.i), *args)

        def load_expert(eng, e, sem_):
            o = e * EW
            eng.dma_start(experts[:, o:o + W1].rearrange("p (k n) -> p k n", k=KD),
                          w1[e].rearrange("(k p) n -> p k n", p=P)).then_inc(sem_, 16)
            eng.dma_start(experts[:, o + W1:o + 2 * W1].rearrange("p (k n) -> p k n", k=KD),
                          w3[e].rearrange("(k p) n -> p k n", p=P)).then_inc(sem_, 16)
            eng.dma_start(experts[:, o + 2 * W1:o + 2 * W1 + (FT - 1) * D].rearrange("p (k n) -> p k n", n=D),
                          w2[e, 0:(FT - 1) * P, :].rearrange("(k p) n -> p k n", p=P)).then_inc(sem_, 16)
            eng.dma_start(experts[0:FR, o + 2 * W1 + (FT - 1) * D:o + EW],
                          w2[e, (FT - 1) * P:F, :]).then_inc(sem_, 16)

        @block.sync
        def _(sp):
            for dst, src in ((Wq, wq), (Wk, wk), (Wv, wv), (Xk, xk), (Xv, xv), (Xq, xq), (Xo, xo),
                             (Wr, router), (S1, s1), (S3, s3)):
                sp.dma_start(dst, src.rearrange("(k p) n -> p k n", p=P)).then_inc(loaded, 16)
            sp.dma_start(S2[:, 0:FT - 1, :], s2[0:(FT - 1) * P, :].rearrange("(k p) n -> p k n", p=P)).then_inc(loaded, 16)
            sp.dma_start(S2[0:FR, FT - 1, :], s2[(FT - 1) * P:F, :]).then_inc(loaded, 16)

            def load(q):
                plain_wait(sp, x1_done, q.n(1, -1))
                sp.dma_start(xa[:, q.par], x[q.b].rearrange("(t p) d -> p t d", p=P)).then_inc(x_in[q.par], 16)

            def load_ctx(q):
                plain_wait(sp, mask_done, q.n(1, -1))
                sp.dma_start(cx[:, q.par], ctx[q.b]).then_inc(c_in[q.par], 16)
                sp.dma_start(mk[:, q.par], mask[q.b, 0].rearrange("(t p) c -> p t c", p=P)).then_inc(c_in[q.par], 16)

            def put_parts(dram, n, part_, sem_, width=S):
                sp.dma_start(dram[n].rearrange("(g p) t -> p g t", p=P)[:, :, 0:width],
                             part_[:, :, 0:width]).then_inc(sem_, 16)

            def stack(dst, dram, order, width, sem_):
                for k in range(2):
                    for n, o in enumerate(order):
                        src = dram[o].rearrange("(g k r) t -> k r g t", k=2, r=HD)[k]
                        sp.dma_start(dst[64 * k + HD * n:64 * k + HD * n + HD, :, 0:width],
                                     src[:, :, 0:width]).then_inc(sem_, 16)

            def stack_a(q):
                plain_wait(sp, a_rd, q.n(A_RD, 0))
                plain_wait(sp, a_free, A_FREE.after(q, "k"))
                for n, p_ in enumerate((qh, ql, kh, kl)):
                    put_parts(qk_d, n, p_, a_wr)
                plain_wait(sp, a_wr, q.n(A_WR, A_WR))
                stack(Q1[:, q.par], qk_d, (0, 1, 0), S, a_rd)
                stack(K1[:, q.par], qk_d, (2, 2, 3), S, a_rd)

            def stack_k2(q):
                plain_wait(sp, k_rd, q.n(K_RD, 0))
                plain_wait(sp, a_free, A_FREE.after(q, "k2"))
                for n, p_ in enumerate((k2h, k2l)):
                    put_parts(k2_d, n, p_, k_wr, SC)
                plain_wait(sp, k_wr, q.n(K_WR, K_WR))
                stack(K2[:, q.par], k2_d, (0, 0, 1), SC, k_rd)

            def stack_q2(q):
                plain_wait(sp, c_rd, q.n(C_RD, 0))
                plain_wait(sp, m_free, M_FREE.after(q, "q"))
                put_parts(q2_d, 0, q2h, c_wr)
                put_parts(q2_d, 1, q2l, c_wr)
                plain_wait(sp, c_wr, q.n(C_WR, C_WR))
                stack(Q2, q2_d, (0, 1, 0), S, c_rd)

            def max_row(q, dst, src, sem_):
                plain_wait(sp, m_free, M_FREE.after(q, "maxT"))
                for k in range(2):
                    sp.dma_start(dst[64 * k + KM:64 * k + KM + 1].rearrange("p g s -> p (g s)"),
                                 src[8 * k:8 * k + 8, :]).then_inc(sem_, 16)

            def row_self(q):
                max_row(q, Q1[:, q.par], neg1, mrow1)

            def row_cross(q):
                max_row(q, Q2, neg2, mrow2)

            def rows(q):
                plain_wait(sp, ff_free[0], q.n(4, 4))
                sp.dma_start(rows_d[0:NTOK].rearrange("(b t p) c -> b p t c", t=TT, p=P)[q.b],
                             R[:, q.par]).then_inc(rows_out[q.par], 16)

            def body(j, i, more=True):
                on = Iteration(j, i)
                on(B, row_self)
                on(C, row_cross)
                on(A, stack_a)
                on(B, stack_k2)
                on(D_, rows)
                on(B, stack_q2)
                if more:
                    load(Batch(A, j, i + 1))
                    load_ctx(Batch(A, j, i + 1))

            load(Batch(A, 0, 0))
            load_ctx(Batch(A, 0, 0))
            for i in range(6):
                body(0, i)
            with sp.Fori(3, NB // 2 - 1) as j:
                for i in range(2):
                    body(j, i)
            for i in range(NB - 2, LAST):
                body(0, i, i + 1 < NB)

            for half in rows_out:
                sp.wait_ge(half, 16 * NB // 2)
            for half in listed:
                sp.wait_ge(half, 32 * NB // 2)
            sp.wait_ge(table, 1)

            def load_ids(q):
                plain_wait(sp, y_out[q.ring], q.reads())
                at = slot_i[0:1, q.s:q.s + 1] if isinstance(q.s, int) else slot_i[0:1, bass.ds(q.s, 1)]
                r = sp.value_load(at, min_val=0, max_val=NTOK * (NE + 1) - P)
                sp.dma_start(idt[:, q.ring:q.ring + 1], list_d[bass.ds(r, P), :]).then_inc(id_in[q.ring], 16)

            def expert_ready(e):
                sp.wait_ge(late[e], 64)
                sp.sem_inc(experts_ready, 1)

            def step(q):
                if q.exists:
                    load_ids(q)
                if isinstance(q.s, int):
                    if q.s == 1:
                        for e in range(EARLY, NE):
                            load_expert(sp, e, late[e])
                    if q.s == 2:
                        sp.wait_ge(early, 64 * EARLY)
                        sp.sem_inc(experts_ready, 1)
                    if q.s == RING - 1:
                        expert_ready(EARLY)
                        expert_ready(EARLY + 1)
                    if RING <= q.s < SLOTS_AHEAD:
                        expert_ready(EARLY + 2 + q.s - RING)
                    if q.s == SLOTS_AHEAD - 1:
                        for e in range(EARLY + 2 + SLOTS_AHEAD - RING, NE):
                            expert_ready(e)

            over_slots(sp, step)

        @block.tensor
        def _(pe):
            mm = pe.matmul
            pe.wait_ge(loaded, 12 * 16)
            pe.wait_ge(consts, CONSTS)

            def transpose_tokens(src, bank, full):
                for k in range(KD):
                    for t in range(TT):
                        last = pe.transpose(bank[:, k * S + t * P:k * S + t * P + P],
                                            src[:, t, k * P:k * P + P], ident)
                last.then_inc(full, 1)

            def project_T(bank, W, xT, full, width=S, step=S):
                for g in range(KD):
                    for k in range(KD):
                        last = mm(bank[:, g * step:g * step + width], W[:, k, g * P:g * P + P],
                                  xT[:, k, 0:width], start=(k == 0), stop=(k == KD - 1))
                last.then_inc(full, 1)

            def project(bank, W, xT, full):
                for t in range(TT):
                    for k in range(KD):
                        last = mm(bank[:, t * D:t * D + D], xT[:, k, t * P:t * P + P], W[:, k, :],
                                  start=(k == 0), stop=(k == KD - 1))
                last.then_inc(full, 1)

            def a_use(q, name):
                at_least(pe, a_free, A_FREE.before(q, name))

            def m_use(q, name):
                at_least(pe, m_free, M_FREE.before(q, name))

            def a_xT(q):
                pe.wait_ge(ln_x[0], q.n(1, 1))
                a_use(q, "xT")
                transpose_tokens(xn[0], bankA, a_full)

            def a_q(q):
                a_use(q, "q")
                project_T(bankA, Wq, xTa, a_full)

            def a_k(q):
                a_use(q, "k")
                project_T(bankA, Wk, xTa, a_full)

            def a_v(q):
                a_use(q, "v")
                project(bankA, Wv, xTa, a_full)

            def ctx_T(q):
                pe.wait_ge(c_in[q.par], q.half(32, 32))
                a_use(q, "ctxT")
                for k in range(KD):
                    last = pe.transpose(bankA[:, k * SCP:k * SCP + SC], cx[:, q.par, k * P:k * P + P],
                                        ident[0:SC, 0:SC])
                last.then_inc(a_full, 1)

            def ctx_k(q):
                a_use(q, "k2")
                project_T(bankA, Xk, cT, a_full, SC, SCP)

            def ctx_v(q):
                a_use(q, "v2")
                for k in range(KD):
                    last = mm(bankA[0:SC, 0:D], cT[:, k, 0:SC], Xv[:, k, :], start=(k == 0), stop=(k == KD - 1))
                last.then_inc(a_full, 1)

            def ctx_mean(q):
                a_use(q, "mean")
                mm(split(bankA[:, 0:D], H), mean77, V2[:, q.par, :, 0:HD], start=True, stop=True).then_inc(a_full, 1)

            def max_head(q, h):
                k, g = h % 2, h // 2
                at_least(pe, sm_free[k], X.before(q, g))
                for t in range(TT):
                    last = mm(BANKS[:, k, t * S:t * S + S], Q1[64 * k:64 * k + KM, q.par, g, t * P:t * P + P],
                              K1[64 * k:64 * k + KM, q.par, g, :], start=True, stop=True)
                last.then_inc(sm_full[k], 1)

            def max_T(q, m, last_use):
                for k in range(2):
                    pe.wait_ge(sm_free[k], X.after(q, last_use))
                m_use(q, "maxT")
                for t in range(TT):
                    last = pe.transpose(bankM[0:H, t * P:t * P + P], m[:, t, :], ident)
                last.then_inc(m_full, 1)

            def exp_head(q, h):
                k, g = h % 2, h // 2
                at_least(pe, ex_free[k], X.before(q, g))
                for t in range(TT):
                    last = mm(BANKS[:, 2 + k, t * S:t * S + S], K1[64 * k:64 * k + KX, q.par, g, t * P:t * P + P],
                              Q1[64 * k:64 * k + KX, q.par, g, :], start=True, stop=True)
                last.then_inc(ex_full[k], 1)

            def pv_self(q, w):
                for k in range(2):
                    pe.wait_ge(ex_free[k], X.after(q, 2 * w + 1))
                if w % 2 == 0:
                    m_use(q, f"O{w // 2}")
                for t in range(TT):
                    for j in range(4):
                        h = 4 * w + j
                        last = mm(bankM[32 * j:32 * j + 32, (w % 2) * S:(w % 2) * S + S],
                                  V1[:, q.par, t, h, :], P1[:, h % 8, t, :], start=(t == 0), stop=(t == TT - 1))
                last.then_inc(pv1, 1)

            def heads_T(q, t):
                use, bank, src, full = (m_use, bankM, OT, m_full) if q.stage == B else (a_use, bankA, OT2, a_full)
                use(q, f"T{t}")
                for w in range(4):
                    last = pe.transpose(bank[:, w * P:w * P + P], src[:, w, t * P:t * P + P], ident)
                last.then_inc(full, 1)

            def x1_T(q):
                pe.wait_ge(ln_x[1], q.n(1, 1))
                m_use(q, "xT")
                transpose_tokens(xn[1], bankM, m_full)

            def q_cross(q):
                m_use(q, "q")
                project_T(bankM, Xq, xTb, m_full)

            def cross_ready(q):
                pe.wait_ge(c_rd, q.n(C_RD, C_RD))
                pe.wait_ge(k_rd, q.n(K_RD, K_RD))
                pe.wait_ge(mask_done, q.n(1, 1))

            def max_cross(q, v):
                k, quad, t = v % 2, (v // 2) % 2, v // 4
                at_least(pe, sm_free[k], X.before(q, v // 2))
                ob = split(BANKS[:, k, 0:4 * SC], 4)
                mm(ob, identb, madd[:, q.par, t, 0:SC].unsqueeze(1).broadcast_to([P, 4, SC]), start=True, stop=False,
                   skip_group_check=True)
                for i in range(4):
                    g = 4 * quad + i
                    last = mm(ob[:, i, :], Q2[64 * k:64 * k + KM, g, t * P:t * P + P],
                              K2[64 * k:64 * k + KM, q.par, g, 0:SC], start=False, stop=True,
                              skip_group_check=True)
                last.then_inc(sm_full[k], 1)

            def exp_cross(q, v):
                k, w = v % 2, v // 2
                at_least(pe, ex_free[k], X.before(q, w))
                ob = split(BANKS[0:SC, 2 + k, :], 2)
                for t in range(TT):
                    mm(ob[:, :, t * P:t * P + P], madd[:, q.par, t, 0:SC],
                       identb.unsqueeze(1).broadcast_to([P, 2, P]), start=(t == 0), stop=False,
                       skip_group_check=True)
                for i in range(2):
                    last = mm(ob[:, i, :], K2[64 * k:64 * k + KX, q.par, 2 * w + i, 0:SC],
                              Q2[64 * k:64 * k + KX, 2 * w + i, :], start=False, stop=True,
                              skip_group_check=True)
                last.then_inc(ex_full[k], 1)

            def pv_cross(q, w):
                for k in range(2):
                    pe.wait_ge(ex_free[k], X.after(q, w))
                if w % 2 == 0:
                    a_use(q, f"P{w // 2}")
                for j in range(4):
                    last = mm(bankA[32 * j:32 * j + 32, (w % 2) * S:(w % 2) * S + S],
                              V2[:, q.par, 4 * w + j, :], P2[:, (2 * w + j % 2) % 4, j // 2, :], start=True, stop=True)
                last.then_inc(pv2, 1)

            def attn_T(q):
                pe.wait_ge(attn_ready, q.n(1, 1))
                a_use(q, "attnT")
                transpose_tokens(attn, bankA, a_full)

            def out_proj(q):
                a_use(q, "out")
                project(bankA, Xo, aT, a_full)

            def x3_T(q):
                pe.wait_ge(ln_x[2], q.n(1, 1))
                a_use(q, "xT")
                transpose_tokens(xn[2], bankA, a_full)

            def route(q):
                a_use(q, "route")
                for t in range(TT):
                    for k in range(KD):
                        last = mm(bankA[:, t * NE:t * NE + NE], xTc[:, q.par, k, t * P:t * P + P], Wr[:, k, :],
                                  start=(k == 0), stop=(k == KD - 1))
                last.then_inc(a_full, 1)

            def rank(q):
                pe.wait_ge(onehot, q.n(1, 1))
                a_use(q, "rank")
                mm(bankA[:, 0:NE], below, oh[:, 0, :], start=True, stop=True)
                mm(bankA[:, NE:2 * NE], below, oh[:, 1, :], start=True, stop=False)
                mm(bankA[:, NE:2 * NE], onesb, oh[:, 0, :], start=False, stop=True)
                mm(bankA[:, 2 * NE:3 * NE], onesb, oh[:, 0, :], start=True, stop=False)
                mm(bankA[:, 2 * NE:3 * NE], onesb, oh[:, 1, :], start=False, stop=True).then_inc(a_full, 1)

            def ff_up(q, f):
                k, r = f % 2, frow(f)
                at_least(pe, ff_free[k], q.n(4 - k, f // 2))
                for n, W in enumerate((S1, S3)):
                    for c in range(KD):
                        last = mm(BANKS[0:r, 6 + k, n * S:n * S + S], W[:, c, f * P:f * P + r],
                                  xTc[:, q.par, c, :], start=(c == 0), stop=(c == KD - 1))
                last.then_inc(ff_full[k], 1)

            def ff_down(q, t):
                pe.wait_ge(ff_free[0], q.n(4, 3))
                pe.wait_ge(ff_free[1], q.n(3, 3))
                for f in range(FT):
                    r = frow(f)
                    last = mm(BANKS[:, 6, t * D:t * D + D], mid[0:r, f, t * P:t * P + P], S2[0:r, f, :],
                              start=(f == 0), stop=(f == FT - 1))
                if t == TT - 1:
                    last.then_inc(ff_full[0], 1)

            def stacks_ready(q):
                pe.wait_ge(a_rd, q.n(A_RD, A_RD))

            def row_ready(q, sem_):
                pe.wait_ge(sem_, q.n(32, 32))

            def body(j, i):
                on = Iteration(j, i)
                on(B, stacks_ready)
                for h in range(H):
                    on(B, max_head, h)
                    if h == 2:
                        on(E, out_proj)
                    if h % 3 == 2:
                        on(D_, ff_up, h // 3)
                    if h == 8:
                        on(E, x3_T)
                    if h == 11:
                        on(E, route)
                    if h == 14:
                        on(E, rank)
                on(B, max_T, m1, 7)
                on(D_, ff_up, 5)
                on(C, cross_ready)
                for v in range(8):
                    on(C, max_cross, v)
                    if v == 3:
                        on(A, a_xT)
                on(A, a_q)
                on(C, max_T, m2, 3)
                on(A, a_k)
                on(B, row_ready, mrow1)
                for w in range(5):
                    for h in range(4 * w, min(4 * w + 4, H)):
                        on(B, exp_head, h)
                    if w == 1:
                        on(A, a_v)
                    if w == 2:
                        on(B, ctx_T)
                    if w == 3:
                        on(B, ctx_k)
                    if w == 4:
                        on(B, ctx_v)
                    if w > 0:
                        on(B, pv_self, w - 1)
                on(C, row_ready, mrow2)
                for w in range(5):
                    if w < 4:
                        on(C, exp_cross, 2 * w)
                        on(C, exp_cross, 2 * w + 1)
                    if w > 0:
                        on(C, pv_cross, w - 1)
                    if w in (1, 2):
                        on(B, heads_T, w - 1)
                on(B, ctx_mean)
                on(B, x1_T)
                on(C, heads_T, 0)
                on(D_, ff_down, 0)
                on(C, heads_T, 1)
                on(B, q_cross)
                on(C, attn_T)
                on(D_, ff_down, 1)

            over_iterations(pe, body)

            pe.wait_ge(table, 1)
            pe.wait_ge(m_free, NB * len(M_ORDER))
            pe.wait_ge(a_free, NB * len(A_ORDER))
            pe.wait_ge(ff_free[0], NB * 4)

            def slot_xT(q):
                pe.wait_ge(g_in[q.ring], q.reads(1))
                at_least(pe, gt_free, q.s)
                for k in range(KD):
                    last = pe.transpose(BANKS[:, 6, k * P:k * P + P], G[:, q.ring, k * P:k * P + P], ident)
                last.then_inc(gt_full, 1)

            def slot_up(q, e, first, bank, full):
                for n in range(2):
                    for k in range(KD):
                        last = mm(BANKS[:, bank + n, 0:FH], gT[:, q.ring % 2, k, :],
                                  experts[:, bass.ds(e + (first + k * F + n * FH), FH)],
                                  start=(k == 0), stop=(k == KD - 1))
                last.then_inc(full, 1)

            def slot_midT(q):
                pe.wait_ge(mid_done, q.s + 1)
                at_least(pe, mt_free, q.s)
                for f in range(FT):
                    r = frow(f)
                    last = pe.transpose(BANKS[0:r, 4 + f // 3, (f % 3) * P:(f % 3) * P + P],
                                        mid2[:, f * P:f * P + r], ident)
                last.then_inc(mt_full, 1)

            def slot_down(q, e):
                pe.wait_ge(mt_free, q.s + 1)
                at_least(pe, y_ready, q.s)
                for f in range(FT):
                    r = frow(f)
                    last = mm(BANKS[:, 7, 0:D], midT[0:r, f, :],
                              experts[0:r, bass.ds(e + (2 * W1 + f * D), D)],
                              start=(f == 0), stop=(f == FT - 1))
                last.then_inc(y_full, 1)

            def entry(q, of=slot_e, low=0, high=(NE - 1) * EW):
                at = of[0:1, q.s:q.s + 1] if isinstance(q.s, int) else of[0:1, bass.ds(q.s, 1)]
                return pe.value_load(at, min_val=low, max_val=high)

            def step(q):
                after, before = q.of(1), q.of(-1)
                if q.exists:
                    e = entry(q)
                    plain_wait(pe, experts_ready, entry(q, slot_n, 1, NE))
                    pe.wait_ge(gt_free, q.s + 1)
                    at_least(pe, u_done, q.s)
                    slot_up(q, e, 0, 0, h1_full)
                if before.exists:
                    slot_midT(before)
                if q.exists:
                    slot_up(q, e, W1, 2, h3_full)
                if after.exists:
                    slot_xT(after)
                if before.exists:
                    slot_down(before, entry(before))

            slot_xT(Slot(0, 0))
            over_slots(pe, step)

        @block.scalar
        def _(act):
            def copy(dst, src, sem_, scale=1.0):
                act.activation(dst, src, ACT.Copy, scale=scale).then_inc(sem_, 1)

            def parts_hi(dst, bank, bias, width, step, sem_):
                for g in range(KD):
                    act.activation(dst[:, g, 0:width], bank[:, g * step:g * step + width], ACT.Identity,
                                   bias=bias[:, g:g + 1]).then_inc(sem_, 1)

            act.wait_ge(loaded2, 64)
            act.wait_ge(consts, CONSTS)

            def flat(ap):
                return ap.rearrange("p k s -> p (k s)")

            def a_xT(q):
                act.wait_ge(a_full, A_FULL.after(q, "xT"))
                copy(flat(xTa), bankA, a_free)

            def a_hi_part(q, name, dst):
                act.wait_ge(a_full, A_FULL.after(q, name))
                at_least(act, a_wr, q.n(A_WR, 0))
                copy(flat(dst), bankA, a_hi)

            def a_v(q):
                act.wait_ge(a_full, A_FULL.after(q, "v"))
                for t in range(TT):
                    ins = act.activation(V1[:, q.par, t, :, 0:HD], split(bankA[:, t * D:t * D + D], H), ACT.Copy)
                ins.then_inc(a_free, 1)

            def ctx_T(q):
                act.wait_ge(a_full, A_FULL.after(q, "ctxT"))
                copy(cT[:, :, 0:SC], split(bankA[:, 0:KD * SCP], KD)[:, :, 0:SC], a_free)

            def ctx_k(q):
                act.wait_ge(a_full, A_FULL.after(q, "k2"))
                at_least(act, k_wr, q.n(K_WR, 0))
                parts_hi(k2h, bankA, bk, SC, SCP, k_hi)

            def ctx_mean(q):
                act.wait_ge(a_full, A_FULL.after(q, "mean"))
                copy(vmean[:, q.par], bankA[:, 0:D], a_free)

            def neg(q, dst, row_sem):
                act.wait_ge(m_full, M_FULL.after(q, "maxT"))
                at_least(act, row_sem, q.n(32, 0))
                copy(dst, bankM[0:H, 0:S], m_free, scale=-1.0)

            def exp_head(q, h):
                k, g = h % 2, h // 2
                act.wait_ge(ex_full[k], X.after(q, g))
                if h % 4 == 0:
                    at_least(act, pv1, q.n(4, h // 4 - 1))
                act.activation(flat(P1[:, h % 8]), BANKS[:, 2 + k, :], ACT.Exp, scale=SCALE).then_inc(ex_free[k], 1)

            def exp_cross(q, v):
                k, w = v % 2, v // 2
                act.wait_ge(ex_full[k], X.after(q, w))
                if k == 0:
                    at_least(act, pv2, q.n(4, w - 1))
                act.activation(flat(P2[:, v % 4]), BANKS[0:SC, 2 + k, :], ACT.Exp, scale=SCALE).then_inc(ex_free[k], 1)

            def heads(q, u):
                if q.stage == B:
                    act.wait_ge(pv1, q.n(4, 2 * u + 2))
                    copy(flat(OT[:, 2 * u:2 * u + 2, :]), bankM, m_free)
                else:
                    act.wait_ge(pv2, q.n(4, 2 * u + 2))
                    copy(flat(OT2[:, 2 * u:2 * u + 2, :]), bankA, a_free)

            def x1_T(q):
                act.wait_ge(m_full, M_FULL.after(q, "xT"))
                copy(flat(xTb), bankM, m_free)

            def attn_T(q):
                act.wait_ge(a_full, A_FULL.after(q, "attnT"))
                copy(flat(aT), bankA, a_free)

            def q_cross(q):
                act.wait_ge(m_full, M_FULL.after(q, "q"))
                at_least(act, c_wr, q.n(C_WR, 0))
                parts_hi(q2h, bankM, bq, S, S, m_hi)

            def x3_T(q):
                act.wait_ge(a_full, A_FULL.after(q, "xT"))
                copy(flat(xTc[:, q.par]), bankA, a_free)

            def gate_tanh(q):
                act.wait_ge(top_found, q.n(1, 1))
                act.activation(tg, top8[:, :, 0], ACT.Tanh, scale=0.5).then_inc(gated, 1)

            def ff(q, f):
                k, r = f % 2, frow(f)
                act.wait_ge(ff_full[k], q.n(4 - k, f // 2 + 1))
                at_least(act, ff_free[k], q.n(4 - k, f // 2))
                act.activation(thd[0:r, k, :], BANKS[0:r, 6 + k, 0:S], ACT.Tanh, scale=0.5).then_inc(ff_tanh, 1)

            def body(j, i):
                on = Iteration(j, i)
                on(D_, ff, 0)
                on(D_, ff, 1)
                on(E, x3_T)
                on(D_, ff, 2)
                on(E, gate_tanh)
                on(D_, ff, 3)
                on(D_, ff, 4)
                on(B, neg, neg1, mrow1)
                on(D_, ff, 5)
                on(A, a_xT)
                on(A, a_hi_part, "q", qh)
                on(C, neg, neg2, mrow2)
                on(A, a_hi_part, "k", kh)
                for w in range(5):
                    for h in range(4 * w, min(4 * w + 4, H)):
                        on(B, exp_head, h)
                    if w == 1:
                        on(A, a_v)
                    if w == 2:
                        on(B, ctx_T)
                    if w == 3:
                        on(B, ctx_k)
                    if w in (2, 4):
                        on(B, heads, w // 2 - 1)
                for w in range(5):
                    if w < 4:
                        on(C, exp_cross, 2 * w)
                        on(C, exp_cross, 2 * w + 1)
                    if w in (2, 4):
                        on(C, heads, w // 2 - 1)
                on(B, ctx_mean)
                on(B, x1_T)
                on(B, q_cross)
                on(C, attn_T)

            over_iterations(act, body)
            act.wait_ge(dve, NB * sum(LINKS.values()))
            act.wait_ge(ff_free[0], NB * 4)
            act.wait_ge(m_free, NB * len(M_ORDER))
            act.wait_ge(a_free, NB * len(A_ORDER))
            act.wait_ge(table, 1)

            def slot_xT(q):
                act.wait_ge(gt_full, q.s + 1)
                copy(gT[:, q.ring % 2].rearrange("p k s -> p (k s)"), BANKS[:, 6, 0:KD * P], gt_free)

            def slot_tanh(q):
                act.wait_ge(h1_full, q.s + 1)
                at_least(act, u_done, q.s)
                act.activation(split(th2, 2), BANKS[:, 0:2, 0:FH], ACT.Tanh, scale=0.5).then_inc(t_done, 1)

            def slot_midT(q):
                act.wait_ge(mt_full, q.s + 1)
                act.activation(midT[:, 0:3, :].rearrange("p f s -> p (f s)"), BANKS[:, 4, 0:3 * P], ACT.Copy)
                act.activation(midT[:, 3:FT - 1, :].rearrange("p f s -> p (f s)"), BANKS[:, 5, 0:2 * P], ACT.Copy)
                act.activation(midT[0:FR, FT - 1, :], BANKS[0:FR, 5, 2 * P:3 * P], ACT.Copy).then_inc(mt_free, 1)

            def step(q):
                if q.exists:
                    slot_tanh(q)
                if q.of(-1).exists:
                    slot_midT(q.of(-1))
                if q.of(1).exists:
                    slot_xT(q.of(1))

            slot_xT(Slot(0, 0))
            over_slots(act, step)

        @block.vector
        def _(v):
            v.wait_ge(consts, CONSTS)
            v.wait_ge(loaded2, 64)

            def stats(q, n, src, link):
                for t in range(TT):
                    ins = v.bn_stats(st[:, n, t, :], src[:, t, :])
                link(ins, True)
                for t in range(TT):
                    ins = v.bn_aggr(mv[:, n, t, :], st[:, n, t, :])
                link(ins)
                v.tensor_scalar(ve[:, n, :], mv[:, n, :, 1], EPS, None, ALU.add).then_inc(ln_v[n], 1)

            def norm(q, n, src):
                v.wait_ge(ln_r[n], q.n(1, 1))
                for t in range(TT):
                    ins = v.tensor_scalar(xn[n][:, t, :], src[:, t, :], mv[:, n, t, 0:1], rstd[:, n, t:t + 1],
                                          ALU.subtract, ALU.mult)
                ins.then_inc(ln_x[n], 1)

            def a_stats(q, link):
                v.wait_ge(x_in[q.par], q.half(16, 16))
                stats(q, 0, xa[:, q.par], link)

            def a_norm(q):
                norm(q, 0, xa[:, q.par])

            def a_lo_part(q, n, dst, hi):
                v.wait_ge(a_hi, q.n(2, n + 1))
                at_least(v, a_wr, q.n(A_WR, 0))
                v.tensor_tensor(dst.rearrange("p k s -> p (k s)"), bankA, hi.rearrange("p k s -> p (k s)"),
                                ALU.subtract).then_inc(a_free, 1)

            def parts_lo_bias(dst, bank, bias, hi, width, step, free):
                for g in range(KD):
                    ins = v.scalar_tensor_tensor(dst[:, g, 0:width], bank[:, g * step:g * step + width],
                                                 bias[:, g:g + 1], hi[:, g, 0:width], ALU.add, ALU.subtract)
                ins.then_inc(free, 1)

            def ctx_mask(q, link):
                v.wait_ge(c_in[q.par], q.half(32, 32))
                link(v.tensor_reduce(anyk[:, q.par, :], mk[:, q.par], AX.X, ALU.max))
                v.tensor_scalar(nany[:, q.par, :], anyk[:, q.par, :], -1.0, 1.0, ALU.mult, ALU.add)
                link(v.tensor_scalar(any9, anyk[:, q.par, :], NEG, None, ALU.mult))
                for t in range(TT):
                    ins = v.tensor_scalar(madd[:, q.par, t, 0:SC], mk[:, q.par, t, :], 1.0, any9[:, t:t + 1],
                                          ALU.subtract, ALU.mult)
                link(ins)
                v.wait_ge(a_full, A_FULL.after(q, "ctxT"))
                v.tensor_copy(one_tok, tokf[:, 0:1]).then_inc(mask_done, 1)

            def ctx_k(q):
                v.wait_ge(k_hi, q.n(2, 2))
                at_least(v, k_wr, q.n(K_WR, 0))
                parts_lo_bias(k2l, bankA, bk, k2h, SC, SCP, a_free)

            def ctx_v(q):
                v.wait_ge(a_full, A_FULL.after(q, "v2"))
                v.tensor_tensor(V2[:, q.par, :, 0:HD], split(bankA[0:SC, 0:D], H), split(bv[0:SC], H), ALU.add)\
                    .then_inc(a_free, 1)

            def max_head(q, h):
                k, g = h % 2, h // 2
                v.wait_ge(sm_full[k], X.after(q, g))
                v.tensor_reduce(m1[:, :, 8 * k + g], split(BANKS[:, k, :], TT), AX.X, ALU.max).then_inc(sm_free[k], 1)

            def normalise(q, t, link, scale=None):
                bank, full, free, nfull, nfree = ((bankM, m_full, m_free, M_FULL, M_FREE) if q.stage == B
                                                  else (bankA, a_full, a_free, A_FULL, A_FREE))
                v.wait_ge(full, nfull.after(q, f"T{t}"))
                heads = split(bank, H)
                link(v.reciprocal(rden, heads[:, :, HD]))
                if scale is not None:
                    link(v.tensor_scalar(rden, rden, scale, None, ALU.mult))
                v.tensor_tensor(split(tmp, H), heads[:, :, 0:HD], rden.unsqueeze(2).broadcast_to([P, H, HD]),
                                ALU.mult).then_inc(free, 1)
                v.wait_ge(free, nfree.after(q, f"T{t}"))

            def x1_tile(q, t, link):
                normalise(q, t, link)
                link(v.tensor_tensor(x1[:, q.par, t, :], xa[:, q.par, t, :], tmp, ALU.add))

            def x1_stats(q, link):
                v.tensor_copy(one_tok, tokf[:, 0:1]).then_inc(x1_done, 1)
                stats(q, 1, x1[:, q.par], link)

            def x1_norm(q):
                norm(q, 1, x1[:, q.par])

            def q_cross(q):
                v.wait_ge(m_hi, q.n(2, 2))
                at_least(v, c_wr, q.n(C_WR, 0))
                parts_lo_bias(q2l, bankM, bq, q2h, S, S, m_free)

            def max_cross(q, n):
                k, quad, t = n % 2, (n // 2) % 2, n // 4
                v.wait_ge(sm_full[k], X.after(q, n // 2))
                v.tensor_reduce(m2[:, t, 8 * k + 4 * quad:8 * k + 4 * quad + 4], split(BANKS[:, k, 0:4 * SC], 4),
                                AX.X, ALU.max).then_inc(sm_free[k], 1)

            def attn_tile(q, t, link):
                normalise(q, t, link, anyk[:, q.par, t:t + 1])
                link(v.scalar_tensor_tensor(attn[:, t, :], vmean[:, q.par], nany[:, q.par, t:t + 1], tmp,
                                            ALU.mult, ALU.add))
                if t == TT - 1:
                    v.tensor_copy(one_tok, tokf[:, 0:1]).then_inc(attn_ready, 1)

            def x2_tile(q, link):
                v.wait_ge(a_full, A_FULL.after(q, "out"))
                v.tensor_tensor(xo1, split(bankA, TT), bo.unsqueeze(1).broadcast_to([P, TT, D]), ALU.add)\
                    .then_inc(a_free, 1)
                v.wait_ge(a_free, A_FREE.after(q, "out"))
                link(v.tensor_tensor(x2[:, q.par], xo1, x1[:, q.par], ALU.add))
                stats(q, 2, x2[:, q.par], link)

            def x2_norm(q):
                norm(q, 2, x2[:, q.par])

            def route(q, link):
                v.wait_ge(a_full, A_FULL.after(q, "route"))
                v.tensor_copy(lg.rearrange("p t e -> p (t e)"), bankA[:, 0:TT * NE]).then_inc(a_free, 1)
                plain_wait(v, a_free, A_FREE.after(q, "route"))
                for t in range(TT):
                    link(v.max(top8[:, t, :], lg[:, t, :]), True)
                for t in range(TT):
                    link(v.max_index(idx8[:, t, :], top8[:, t, :], lg[:, t, :]), t == 0)
                link(v.tensor_copy(idxf, idx8[:, :, 0]))
                v.tensor_copy(one_tok, tokf[:, 0:1]).then_inc(top_found, 1)
                for t in range(TT):
                    ins = v.tensor_scalar(oh[:, t, :], erow, idxf[:, t:t + 1], None, ALU.is_equal)
                ins.then_inc(onehot, 1)

            def gated_rows(q, link):
                v.wait_ge(gated, q.n(1, 1))
                link(v.tensor_scalar(gate, tg, 0.5, 0.5, ALU.mult, ALU.add))
                at_least(v, rows_out[q.par], q.half(16, 0))
                for t in range(TT):
                    ins = v.tensor_scalar(R[:, q.par, t, 0:D], xn[2][:, t, :], gate[:, t:t + 1], None, ALU.mult)
                link(ins)

            def rank(q, link):
                v.wait_ge(a_full, A_FULL.after(q, "rank"))
                link(v.tensor_tensor(pr, split(bankA[:, 0:TT * NE], TT), base.unsqueeze(1).broadcast_to([P, TT, NE]),
                                     ALU.add))
                link(v.tensor_tensor(prm, pr, oh, ALU.mult))
                link(v.tensor_reduce(posf, prm, AX.X, ALU.add))
                at_least(v, listed[q.par], q.half(32, 0))
                v.tensor_copy(posi[:, q.par, :], posf)
                link(v.tensor_copy(toki[:, q.par, :], tokf))
                link(v.tensor_scalar(tokf, tokf, float(S), None, ALU.add))
                v.tensor_copy(one_tok, tokf[:, 0:1]).then_inc(pos_ready, 1)
                v.tensor_tensor(base, base, bankA[:, 2 * NE:3 * NE], ALU.add).then_inc(a_free, 1)

            def ff(q, f, link):
                k, r = f % 2, frow(f)
                v.wait_ge(ff_tanh, q.n(FT, f + 1))
                link(v.scalar_tensor_tensor(ud[0:r, k, :], thd[0:r, k, :], 1.0, BANKS[0:r, 6 + k, 0:S],
                                            ALU.add, ALU.mult))
                if f == 0:
                    at_least(v, ff_full[0], q.n(4, 0))
                v.scalar_tensor_tensor(mid[0:r, f, :], ud[0:r, k, :], 0.5, BANKS[0:r, 6 + k, S:2 * S],
                                       ALU.mult, ALU.mult).then_inc(ff_free[k], 1)

            def ff_out(q, link):
                v.wait_ge(ff_full[0], q.n(4, 4))
                v.tensor_tensor(R[:, q.par, :, D:2 * D], split(BANKS[:, 6, :], TT), x2[:, q.par], ALU.add)\
                    .then_inc(ff_free[0], 1)
                link(v.tensor_copy(one_tok, tokf[:, 0:1]))

            def body(j, i):
                on = Iteration(j, i)
                link = Chain(v, before_iteration(LINKS, j, i))
                for h in range(3):
                    on(B, max_head, h)
                on(E, x2_tile, link)
                for h in range(3, 6):
                    on(B, max_head, h)
                on(E, x2_norm)
                on(D_, ff, 0, link)
                for h in range(6, 9):
                    on(B, max_head, h)
                on(D_, ff, 1, link)
                for h in range(9, 12):
                    on(B, max_head, h)
                on(D_, ff, 2, link)
                on(E, route, link)
                for h in range(12, 15):
                    on(B, max_head, h)
                on(D_, ff, 3, link)
                on(E, gated_rows, link)
                on(A, a_stats, link)
                on(B, max_head, 15)
                on(D_, ff, 4, link)
                on(E, rank, link)
                on(A, a_norm)
                on(D_, ff, 5, link)
                for n in range(8):
                    on(C, max_cross, n)
                on(A, a_lo_part, 0, ql, qh)
                on(A, a_lo_part, 1, kl, kh)
                on(B, ctx_mask, link)
                on(B, ctx_k)
                on(B, ctx_v)
                on(B, x1_tile, 0, link)
                on(B, x1_tile, 1, link)
                on(B, x1_stats, link)
                on(B, x1_norm)
                on(C, attn_tile, 0, link)
                on(C, attn_tile, 1, link)
                on(B, q_cross)
                on(D_, ff_out, link)
                want = sum(n for stage, n in LINKS.items() if not isinstance(j, int) or live(stage, i))
                assert link.k == want, (link.k, want, i)

            over_iterations(v, body)

            t0 = [NB * sum(LINKS.values())]

            def link(ins):
                t0[0] += 1
                ins.then_inc(dve, 1)
                v.wait_ge(dve, t0[0])

            v.wait_ge(a_free, NB * len(A_ORDER))
            link(v.tensor_tensor(cnt, base[0:1], e4096[0:1], ALU.subtract))
            link(v.tensor_scalar(cnt, cnt, float(P - 1), None, ALU.add))
            link(v.tensor_copy(cnti, cnt))
            link(v.tensor_scalar(cnti, cnti, 7, None, ALU.logical_shift_right))
            link(v.tensor_copy(tiles, cnti))
            link(v.tensor_copy(cum, tiles))
            for e in range(1, NE):
                link(v.tensor_tensor(cum[:, e:e + 1], cum[:, e:e + 1], cum[:, e - 1:e], ALU.add))
            link(v.memset(acc.rearrange("p a s -> p (a s)"), 0.0))
            for e in range(NE):
                link(v.tensor_scalar(accb[:, 0, :], srow, cum[:, e:e + 1], None, ALU.is_ge))
                link(v.tensor_tensor(acc[:, 0, :], acc[:, 0, :], accb[:, 0, :], ALU.add))
                link(v.scalar_tensor_tensor(acc[:, 1, :], accb[:, 0, :], tiles[:, e:e + 1], acc[:, 1, :],
                                            ALU.mult, ALU.add))
            link(v.tensor_tensor(accb[:, 1, :], srow, acc[:, 1, :], ALU.subtract))
            link(v.tensor_scalar(accb[:, 1, :], accb[:, 1, :], float(P), None, ALU.mult))
            link(v.scalar_tensor_tensor(accb[:, 0, :], acc[:, 0, :], float(NTOK), accb[:, 1, :], ALU.mult, ALU.add))
            link(v.tensor_copy(slot_i, accb[:, 0, :]))
            link(v.tensor_scalar(acc[:, 0, :], acc[:, 0, :], float(NE - 1), None, ALU.min))
            link(v.tensor_scalar(accb[:, 0, :], acc[:, 0, :], float(2 - EARLY), 1.0, ALU.add, ALU.max))
            link(v.tensor_copy(slot_n, accb[:, 0, :]))
            link(v.tensor_scalar(acc[:, 0, :], acc[:, 0, :], float(EW), None, ALU.mult))
            link(v.tensor_copy(slot_e, acc[:, 0, :]))
            v.memset(one_tok2, 0.0).then_inc(table, 1)

            def slot_u(q):
                v.wait_ge(t_done, q.s + 1)
                at_least(v, mid_done, q.s)
                v.scalar_tensor_tensor(split(u2, 2), split(th2, 2), 1.0, BANKS[:, 0:2, 0:FH], ALU.add, ALU.mult)\
                    .then_inc(u_done, 1)
                v.wait_ge(u_done, q.s + 1)
                v.wait_ge(h3_full, q.s + 1)
                at_least(v, mt_full, q.s)
                v.scalar_tensor_tensor(split(mid2, 2), split(u2, 2), 0.5, BANKS[:, 2:4, 0:FH], ALU.mult, ALU.mult)\
                    .then_inc(mid_done, 1)

            def slot_y(q):
                v.wait_ge(y_full, q.s + 1)
                at_least(v, y_out[q.ring], q.reads())
                v.tensor_tensor(y2[:, q.ring, :], BANKS[:, 7, 0:D], G[:, q.ring, D:2 * D], ALU.add).then_inc(y_ready, 1)

            def step(q):
                if q.exists:
                    slot_u(q)
                if q.of(-1).exists:
                    slot_y(q.of(-1))

            over_slots(v, step)

        @block.gpsimd
        def _(g):
            k = [0]

            def made(ins):
                k[0] += 1
                ins.then_inc(chain_c, 1)
                g.wait_ge(chain_c, k[0])

            for dst, src in ((bv, xbv), (bo, xbo)):
                g.dma_start(dst, src.rearrange("(a n) -> a n", a=1).broadcast_to([P, D])).then_inc(loaded2, 16)
            for dst, src in ((bq, xbq), (bk, xbk)):
                g.dma_start(dst, src.rearrange("(k p) -> p k", p=P), allow_slow_non_contiguous=True).then_inc(loaded2, 16)

            made(g.memset(ident, 0.0))
            made(g.affine_select(out=ident, in_=ident, compare_op=ALU.not_equal, fill=1.0, base=0,
                                 pattern=[[-1, P]], channel_multiplier=1))
            made(g.tensor_copy(identb, ident))
            made(g.memset(onesb, 1.0))
            made(g.memset(below, 0.0))
            made(g.affine_select(out=below, in_=below, compare_op=ALU.is_ge, fill=1.0, base=0,
                                 pattern=[[-1, P]], channel_multiplier=1))
            made(g.memset(mean77, 1.0 / SC))
            made(g.memset(mhalf, -0.5))
            made(g.iota(erow, [[1, NE]], base=0, channel_multiplier=0, allow_small_or_imprecise_dtypes=True))
            made(g.iota(e4096, [[NTOK, NE]], base=0, channel_multiplier=0, allow_small_or_imprecise_dtypes=True))
            made(g.tensor_copy(base, e4096))
            made(g.iota(srow, [[1, 64]], base=0, channel_multiplier=0, allow_small_or_imprecise_dtypes=True))
            made(g.iota(tokf, [[P, TT]], base=0, channel_multiplier=1, allow_small_or_imprecise_dtypes=True))
            made(g.memset(V1.rearrange("p a t h d -> p (a t h d)"), 0.0))
            made(g.memset(V1.rearrange("p a t h d -> p (a t h) d")[:, :, HD], 1.0))
            made(g.memset(V2.rearrange("p a h d -> p (a h d)"), 0.0))
            made(g.memset(V2.rearrange("p a h d -> p (a h) d")[:, :, HD], 1.0))
            made(g.memset(K1.rearrange("p a h s -> p (a h s)"), 1.0))
            made(g.memset(K2.rearrange("p a h s -> p (a h s)"), 1.0))
            made(g.memset(one_tok, 0.0))
            made(g.iota(fill, [[0, NTOK * (NE + 1) // P]], base=PAD_ROW, channel_multiplier=0))
            made(g.memset(zrow, 0.0))
            g.memset(one_tok2, 0.0).then_inc(consts, 1)
            g.wait_ge(consts, 1)
            g.dma_start(list_d.rearrange("(p n) a -> p (n a)", p=P), fill).then_inc(dram_init, 16)
            g.dma_start(rows_d[NTOK].rearrange("(p n) -> p n", p=P), zrow).then_inc(dram_init, 16)
            for e in range(EARLY):
                load_expert(g, e, early)
            g.wait_ge(dram_init, 32)

            def rstd_of(q, n):
                plain_wait(g, ln_v[n], q.n(1, 1))
                g.tensor_tensor(rstd[:, n, :], ve[:, n, :], mhalf, ALU.pow).then_inc(ln_r[n], 1)

            def list_tokens(q):
                plain_wait(g, pos_ready, q.n(1, 1))
                for t in range(TT):
                    g.indirect_dma_start(out=list_d, out_offset=bass.IndirectOffsetOnAxis(ap=posi[:, q.par, t:t + 1], axis=0),
                                         in_=toki[:, q.par, t:t + 1], in_offset=None).then_inc(listed[q.par], 16)

            def body(j, i):
                on = Iteration(j, i)
                on(E, rstd_of, 2)
                on(A, rstd_of, 0)
                on(E, list_tokens)
                on(B, rstd_of, 1)

            over_iterations(g, body)
            g.wait_ge(table, 1)

            def gather(q):
                plain_wait(g, id_in[q.ring], q.reads(1))
                plain_wait(g, y_ready, q.s - RING + 1)
                g.indirect_dma_start(out=G[:, q.ring, :], out_offset=None, in_=rows_d,
                                     in_offset=bass.IndirectOffsetOnAxis(ap=idt[:, q.ring:q.ring + 1], axis=0))\
                    .then_inc(g_in[q.ring], 16)

            def scatter(q):
                plain_wait(g, y_ready, q.s + 1)
                g.indirect_dma_start(out=out, out_offset=bass.IndirectOffsetOnAxis(ap=idt[:, q.ring:q.ring + 1], axis=0),
                                     in_=y2[:, q.ring, :], in_offset=None, bounds_check=NTOK - 1, oob_is_err=False)\
                    .then_inc(y_out[q.ring], 16)

            def step(q):
                if q.of(GATHER).exists:
                    gather(q.of(GATHER))
                if q.of(-1).exists:
                    scatter(q.of(-1))

            for s in range(GATHER):
                gather(Slot(0, s))
            over_slots(g, step)
            for r in range(RING):
                g.wait_ge(y_out[r], 16 * ((NSLOT - r + RING - 1) // RING))


def kernel(x, ctx_1024, mask_Bx1xSxS2_bf1, L0_attn_w_Q, L0_attn_w_K, L0_attn_w_V,
           L0_xattn_Wq, L0_xattn_bq, L0_xattn_Wk, L0_xattn_bk, L0_xattn_Wv, L0_xattn_bv,
           L0_xattn_Wo, L0_xattn_bo, L0_ffn_router_DE, L0_ffn_w1_eDF, L0_ffn_w3_eDF, L0_ffn_w2_eFD,
           L0_ffn_ws1_DF, L0_ffn_ws3_DF, L0_ffn_ws2_FD):
    import concourse.bacc as bacc
    from concourse.bass_utils import run_bass_kernel_spmd

    def T(w):
        return np.ascontiguousarray(np.asarray(w).T)

    given = {
        "x": x, "ctx": ctx_1024, "mask": np.asarray(mask_Bx1xSxS2_bf1).view(np.uint8),
        "wq": L0_attn_w_Q, "wk": L0_attn_w_K, "wv": L0_attn_w_V,
        "xq": T(L0_xattn_Wq), "xbq": L0_xattn_bq, "xk": T(L0_xattn_Wk), "xbk": L0_xattn_bk,
        "xv": T(L0_xattn_Wv), "xbv": L0_xattn_bv, "xo": T(L0_xattn_Wo), "xbo": L0_xattn_bo,
        "router": L0_ffn_router_DE, "w1": L0_ffn_w1_eDF, "w3": L0_ffn_w3_eDF, "w2": L0_ffn_w2_eFD,
        "s1": L0_ffn_ws1_DF, "s3": L0_ffn_ws3_DF, "s2": L0_ffn_ws2_FD,
    }
    nc = bacc.Bacc("TRN2", target_bir_lowering=False, num_devices=1)
    arrays, aps = {}, {}
    for name, a in given.items():
        a = np.ascontiguousarray(np.asarray(a))
        arrays["in_" + name] = a
        aps[name] = nc.dram_tensor("in_" + name, a.shape, mybir.dt.from_np(a.dtype), kind="ExternalInput").ap()
    out = nc.dram_tensor("out", (NTOK, D), F32, kind="ExternalOutput").ap()
    decoder_layer(nc, out=out, **aps)
    r = run_bass_kernel_spmd(nc, [arrays], core_ids=[0])
    return r.results[0]["out"].reshape(NB, S, D)
```

```python
import numpy as np
import concourse.bass as bass
from concourse import mybir
from contextlib import ExitStack

F32 = mybir.dt.float32
F16 = mybir.dt.float16
BF16 = mybir.dt.bfloat16
I32 = mybir.dt.int32
U32 = mybir.dt.uint32
U8 = mybir.dt.uint8
ALU = mybir.AluOpType
ACT = mybir.ActivationFunctionType
AX = mybir.AxisListType

NB, S, D = 16, 256, 256
SC = 77
SCP = 80
H, HD = 16, 16
P = 128
TT = S // P
KD = D // P
NE, F = 8, 704
FT = -(-F // P)
FR = F - (FT - 1) * P
NTOK = NB * S
EPS = 1e-5
SCALE = float(HD) ** -0.5
NEG = 1e9
HP = 2 * HD
KM = 3 * HD
KX = KM + 1
W1 = KD * F
W2 = FT * D
EW = 2 * W1 + W2
NSLOT = (NTOK + NE * (P - 1)) // P
FH = F // 2
PAD_ROW = NTOK


def frow(ft):
    return P if ft < FT - 1 else FR


A, B, C, E, D_ = range(5)
LAST = NB + D_


def live(stage, i):
    return 0 <= i - stage < NB


class Batch:

    def __init__(self, stage, j, i):
        self.stage, self.j, self.i = stage, j, i
        self.c = i - stage
        self.par, self.b = self.c % 2, 2 * j + self.c

    def n(self, per, more):
        return self.j * (2 * per) + (per * self.c + more)

    def half(self, per, more):
        return self.j * per + (per * (self.c // 2) + more)


def before_iteration(per, j, i):
    if isinstance(j, int):
        return sum(n * min(max(i - stage, 0), NB) for stage, n in per.items())
    return j * (2 * sum(per.values())) + sum(n * (i - stage) for stage, n in per.items())


class Uses:

    def __init__(self, order, but=()):
        self.order = [u for u in order if u[1] not in but]
        self.per = {s: sum(u[0] == s for u in self.order) for s, _ in self.order}

    def before(self, batch, name):
        at = self.order.index((batch.stage, name))
        here = sum(not isinstance(batch.j, int) or live(s, batch.i) for s, _ in self.order[:at])
        return before_iteration(self.per, batch.j, batch.i) + here

    def after(self, batch, name):
        return self.before(batch, name) + 1


RING = 6
GATHER = 3
SLOTS_AHEAD = RING + 2


class Slot:

    def __init__(self, j, c):
        self.j, self.c, self.ring = j, c, c % RING
        self.s = j * RING + c

    def of(self, more):
        return Slot(self.j, self.c + more)

    def reads(self, more=0):
        return self.j * 16 + 16 * (self.c // RING + more)

    @property
    def exists(self):
        return not isinstance(self.s, int) or 0 <= self.s < NSLOT


def over_slots(eng, step):
    rounds = (NSLOT - GATHER - SLOTS_AHEAD) // RING
    for s in range(SLOTS_AHEAD):
        step(Slot(0, s))
    with eng.Fori(0, rounds) as j:
        for c in range(RING):
            step(Slot(j, c + SLOTS_AHEAD))
    for s in range(SLOTS_AHEAD + rounds * RING, NSLOT + 1):
        step(Slot(0, s))


def at_least(eng, sem, value):
    if isinstance(value, int) and value <= 0:
        return
    eng.wait_ge(sem, value)


def decoder_layer(nc, x, ctx, mask, wq, wk, wv, xq, xbq, xk, xbk, xv, xbv, xo, xbo,
                  router, w1, w3, w2, s1, s3, s2, out):
    es = ExitStack()
    with es:
        def sem(name):
            return es.enter_context(nc.semaphore(name))

        TOTAL = 52800
        ALL = es.enter_context(nc.sbuf_tensor("ALL", [P, TOTAL], F32))
        BANKS = es.enter_context(nc.psum_tensor("BANKS", [P, 8, 512], F32))
        top = {"at": 0}

        def part(shape, dt=F32):
            per = int(np.prod(shape[1:]))
            size = {F32: 4, I32: 4, U32: 4, F16: 2, BF16: 2, U8: 1}[dt]
            words = -(-per * size // 32) * 8
            v = ALL[0:shape[0], top["at"]:top["at"] + words]
            top["at"] += words
            assert top["at"] <= TOTAL, top["at"]
            if dt != F32:
                v = v.bitcast(dt)
            v = v[:, 0:per]
            if len(shape) == 2:
                return v
            names = "abcd"[:len(shape) - 1]
            return v.rearrange(f"p ({' '.join(names)}) -> p {' '.join(names)}",
                               **{n: s for n, s in zip(names, shape[1:])})

        ident = part([P, P])
        identb = part([P, P], BF16)
        below = part([P, P], BF16)
        onesb = part([P, P], BF16)
        base = part([P, NE])
        e4096 = part([P, NE])
        erow = part([P, NE])
        slot_e = part([1, 64], I32)
        slot_i = part([1, 64], I32)
        idt = part([P, RING], I32)
        slot_n = part([1, 64], I32)
        consts_end = top["at"]
        RAW = 2
        raw_at = [consts_end + EW * n for n in (0, 1, 0, 1, RAW + NE - 2, RAW + NE - 1, 0, 1)]
        raw = [ALL[:, at:at + EW] for at in raw_at]
        top["at"] = consts_end + RAW * EW
        experts = ALL[:, top["at"]:top["at"] + NE * EW].bitcast(F16)
        EARLY = 2
        SPLIT_AFTER = {0: 2, 1: 3, 3: 4, 4: 5, 5: 6, 6: 7}

        top["at"] = consts_end + (RAW + NE) * EW
        G = part([P, RING, 2 * D])
        gTp = [part([P, 2, KD, P], F16) for _ in range(2)]
        th2 = part([P, F])
        u2 = part([P, F])
        mid2 = part([P, F])
        midTp = [part([P, FT, P], F16) for _ in range(2)]
        y2 = part([P, RING, D])

        top["at"] = consts_end + RAW * EW
        Wq, Wk, Wv = (part([P, KD, D]) for _ in range(3))
        Xq, Xk, Xv = (part([P, KD, D]) for _ in range(3))
        Q1, K1 = part([P, 2, H // 2, S], F16), part([P, 2, H // 2, S], F16)
        V1 = part([P, TT, H, HP])
        xTa = part([P, KD, S])
        assert top["at"] >= consts_end + (RAW + EARLY) * EW
        Xo = part([P, KD, D])
        Wr = part([P, KD, NE])
        S1, S3 = ([part([P, KD, F], F16) for _ in range(2)] for _ in range(2))
        S2 = [part([P, FT, D], F16) for _ in range(2)]
        bq, bk = part([P, KD]), part([P, KD])
        bv, bo = part([P, D]), part([P, D])
        mean77 = part([SC, P])
        xa, x1, x2 = part([P, 2, TT, D]), part([P, 2, TT, D]), part([P, 2, TT, D])
        R = part([P, 2, TT, 2 * D])
        xn = [part([P, TT, D]) for _ in range(3)]
        st, mv = part([P, 3, TT, 6]), part([P, 3, TT, 2])
        ve, rstd, mhalf = part([P, 3, TT]), part([P, 3, TT]), part([P, TT])
        xTb = part([P, KD, S])
        xTc = part([P, KD, S])
        xTp = [part([P, KD, S], F16) for _ in range(2)]
        qh, ql, kh, kl = (part([P, KD, S], F16) for _ in range(4))
        q2h, q2l = (part([P, KD, S], F16) for _ in range(2))
        q2 = part([P, KD, S])
        k2h, k2l = (part([P, KD, SCP], F16) for _ in range(2))
        Q2 = part([P, H // 2, S], F16)
        K2 = part([P, 2, H // 2, SCP], F16)
        V2 = part([SC, 2, H, HP])
        vmean = part([P, 2, D])
        P1 = part([P, 8, TT, S])
        P2 = part([SC, 4, 2, S])
        OT, OT2 = part([P, 4, S]), part([P, 4, S])
        m1, m2 = part([P, TT, H]), part([P, TT, H])
        neg1, neg2 = part([H, S], F16), part([H, S], F16)
        rden = part([P, H])
        tmp = part([P, D])
        attn = part([P, TT, D])
        aT = part([P, KD, S])
        cx = part([SC, 2, D])
        cT = part([P, KD, SCP])
        mk = part([P, 2, TT, SC], U8)
        madd = part([P, 2, TT, SCP], BF16)
        anyk, any9, nany = part([P, 2, TT]), part([P, TT]), part([P, 2, TT])
        lg = part([P, TT, NE])
        top8, idx8 = part([P, TT, 8]), part([P, TT, 8], U32)
        idxf = part([P, TT])
        oh = part([P, TT, NE], BF16)
        tg, gate = part([P, TT]), part([P, TT])
        pr, prm, posf = part([P, TT, NE]), part([P, TT, NE]), part([P, TT])
        posi, toki = part([P, 2, TT], I32), part([P, 2, TT], I32)
        tokf = part([P, TT])
        signal1, signal2 = part([P, 1]), part([P, 1])
        thd, ud = part([P, 2, S]), part([P, 2, S])
        mid = part([P, 2, S])
        midp = [part([P, FT, S], F16) for _ in range(2)]
        P1_flat = P1.rearrange("p a t s -> p (a t s)")
        S1_in, S3_in = (P1_flat[:, n * W1:n * W1 + W1] for n in range(2))
        S2_in = R.rearrange("p a t c -> p (a t c)")[:, 0:W2]
        fill = part([P, NTOK * (NE + 1) // P], I32)
        zrow = part([P, 2 * D // P])
        cnt, cnti, tiles = part([1, NE]), part([1, NE], I32), part([1, NE])
        cum = part([1, NE])
        srow, acc, accb = part([1, 64]), part([1, 2, 64]), part([1, 2, 64])

        qk_d = nc.dram_tensor("qk_parts", [4, D, S], F16, kind="Internal").ap()
        q2_d = nc.dram_tensor("q2_parts", [2, D, S], F16, kind="Internal").ap()
        k2_d = nc.dram_tensor("k2_parts", [2, D, SCP], F16, kind="Internal").ap()
        rows_d = nc.dram_tensor("token_rows", [NTOK + 1, 2 * D], F32, kind="Internal").ap()
        list_d = nc.dram_tensor("token_list", [NTOK * (NE + 1), 1], I32, kind="Internal").ap()

        loaded = sem("weights_loaded")
        q2_split = sem("cross_queries_split")
        shared_hi, shared_lo = sem("shared_weights_high"), sem("shared_weights_split")
        x3_hi, x3_copied = sem("x3T_high_part"), sem("x3T_copied")
        mid_hi, mid_parts = sem("mid_high_part"), sem("mid_split")
        loaded_rest = sem("weights_after_qkv_loaded")
        loaded_bias = sem("bias_loaded")
        expert_in = [sem(f"expert{e}_loaded") for e in range(NE)]
        expert_hi, expert_split = sem("experts_high_parts"), sem("experts_split")
        gt_hi, mt_hi = sem("slot_xT_high_part"), sem("slot_midT_high_parts")
        consts, tables = sem("constants_made"), sem("tables_made")
        pads, padded = sem("zeros_of_paddings"), sem("paddings_made")
        chain_c = sem("constants_chain")
        dram_init = sem("dram_initialised")
        x_in = [sem(f"x_loaded{i}") for i in range(2)]
        ln_v = [sem(f"ln{i}_variance") for i in range(3)]
        ln_r = [sem(f"ln{i}_rstd") for i in range(3)]
        x1_bias = sem("x1_with_output_bias")
        gate_made, gated_rows = sem("gate_made"), sem("gated_rows_made")
        ln_x = [sem(f"ln{i}_normed") for i in range(3)]
        a_full, a_free, a_hi = sem("a_bank_full"), sem("a_bank_free"), sem("a_high_parts")
        m_full, m_free = sem("m_bank_full"), sem("m_bank_free")
        a_wr, a_rd = sem("a_parts_written"), sem("a_stacks_built")
        k_wr, k_rd, k_hi = sem("k2_parts_written"), sem("k2_stack_built"), sem("k2_high_parts")
        c_in = [sem(f"context_loaded{i}") for i in range(2)]
        c_wr, c_rd = sem("c_parts_written"), sem("c_stacks_built")
        s_full = [sem(f"score_bank{i}_full") for i in range(4)]
        s_free = [sem(f"score_bank{i}_free") for i in range(4)]
        mrow1, mrow2 = sem("max_row_self"), sem("max_row_cross")
        pv1, pv2 = sem("pv_self_done"), sem("pv_cross_done")
        attn_ready = sem("attn_ready")
        x1_done, mask_done = sem("x1_done"), sem("mask_done")
        top_found, onehot, gated = sem("top_found"), sem("onehot_ready"), sem("gate_tanh")
        pos_ready = sem("positions_ready")
        listed = [sem(f"tokens_listed{i}") for i in range(2)]
        ff_full = [sem(f"ff_bank{i}_full") for i in range(2)]
        ff_free = [sem(f"ff_bank{i}_free") for i in range(2)]
        ff_tanh = sem("ff_tanh")
        rows_out = [sem(f"rows_written{i}") for i in range(2)]
        dve = sem("vector_chain")
        table, table_chain = sem("slot_table_ready"), sem("slot_table_chain")
        id_in = [sem(f"slot_ids_loaded{i}") for i in range(RING)]
        g_in = [sem(f"slot_rows_gathered{i}") for i in range(RING)]
        y_out = [sem(f"slot_rows_scattered{i}") for i in range(RING)]
        gt_full, gt_free = sem("slot_xT_full"), sem("slot_xT_free")
        h1_full, h3_full = sem("slot_h1_full"), sem("slot_h3_full")
        t_done, u_done, mid_done = sem("slot_tanh"), sem("slot_u"), sem("slot_mid")
        mt_full, mt_free = sem("slot_midT_full"), sem("slot_midT_free")
        y_full, y_ready = sem("slot_y_full"), sem("slot_y_ready")

        block = es.enter_context(nc.Block())

        M_ORDER = [(B, "maxT"), (C, "maxT"), (B, "O0"), (B, "O1"), (B, "T0"), (B, "T1"), (B, "xT"), (B, "q")]
        A_ORDER = [(E, "attnT"), (E, "out"), (B, "v"), (E, "xT"), (E, "route"), (A, "xT"), (A, "q"),
                   (E, "rank"), (B, "ctxT"), (A, "k"), (B, "k2"), (B, "v2"), (B, "mean"),
                   (C, "P0"), (C, "P1"), (C, "T0"), (C, "T1")]
        M_FREE, M_FULL = Uses(M_ORDER), Uses(M_ORDER, ("O0", "O1"))
        A_FREE, A_FULL = Uses(A_ORDER), Uses(A_ORDER, ("P0", "P1"))
        X = Uses([(B, f"max{n}") for n in range(4)] + [(C, f"max{n}") for n in range(2)]
                 + [(B, f"exp{n}") for n in range(4)] + [(C, f"exp{n}") for n in range(2)])
        bankA, bankM = BANKS[:, 5, :], BANKS[:, 4, :]
        CONSTS = 1
        A_WR, A_RD, K_WR, K_RD, C_WR, C_RD = (16 * n for n in (4, 12, 2, 6, 2, 6))

        def plain_wait(eng, sem_, value):
            if isinstance(value, int):
                at_least(eng, sem_, value)
                return
            with eng.register() as r:
                eng.reg_mov(r, value)
                eng.wait_ge(consts, CONSTS)
                eng.wait_ge(sem_, r)

        def split(ap, n):
            return ap.rearrange("p (n s) -> p n s", n=n)

        class Chain:

            def __init__(self, eng, start, sem_=dve):
                self.eng, self.start, self.sem, self.k = eng, start, sem_, 0

            def __call__(self, ins, before_plain=False):
                self.k += 1
                ins.then_inc(self.sem, 1)
                if before_plain:
                    plain_wait(self.eng, self.sem, self.start + self.k)
                else:
                    self.eng.wait_ge(self.sem, self.start + self.k)

        LINKS = {A: 2, B: 9, C: 6, E: 18, D_: 1}

        def over_iterations(eng, body):
            for i in range(6):
                body(0, i)
            with eng.Fori(3, NB // 2) as j:
                for i in range(2):
                    body(j, i)
            for i in range(NB, LAST):
                body(0, i)

        class Iteration:

            def __init__(self, j, i):
                self.j, self.i = j, i

            def __call__(self, stage, step, *args):
                if not isinstance(self.j, int) or live(stage, self.i):
                    step(Batch(stage, self.j, self.i), *args)

        def load_expert(eng, e):
            def arrive(first, weights):
                size = D * len(range(0, weights.shape[0], P)) if weights.shape[1] == D else W1
                eng.dma_start(raw[e][:, first:first + size].rearrange("p (k n) -> p k n", n=weights.shape[1]),
                              weights.rearrange("(k p) n -> p k n", p=P)).then_inc(expert_in[e], 16)

            arrive(0, w1[e])
            arrive(W1, w3[e])
            arrive(2 * W1, w2[e, 0:(FT - 1) * P, :])
            eng.dma_start(raw[e][0:FR, EW - D:EW], w2[e, (FT - 1) * P:F, :]).then_inc(expert_in[e], 16)

        MID_PIECES = ((P, 0, 3), (P, 3, FT - 1), (FR, FT - 1, FT))

        def mid_bank(r, f0, f1):
            return BANKS[0:r, 4 + f0 // 3, (f0 % 3) * P:(f0 % 3 + f1 - f0) * P]

        THIRDS = 3

        def expert_third(e, n):
            for rows_, a, b in (((P, 0, W1),), ((P, W1, 2 * W1),), ((P, 2 * W1, EW - D), (FR, EW - D, EW)))[n]:
                at = 2 * EW * e
                yield raw[e][0:rows_, a:b], experts[0:rows_, at + a:at + b], experts[0:rows_, at + EW + a:at + EW + b]

        def expert_high(act, e, thirds=range(THIRDS)):
            for n in thirds:
                act.wait_ge(expert_in[e], 64)
                for w, hi, _ in expert_third(e, n):
                    ins = act.activation(hi, w, ACT.Copy)
                ins.then_inc(expert_hi, 1)

        def expert_low(v, e, thirds=range(THIRDS)):
            for n in thirds:
                v.wait_ge(expert_in[e], 64)
                v.wait_ge(expert_hi, THIRDS * e + n + 1)
                for w, hi, lo in expert_third(e, n):
                    ins = v.tensor_tensor(lo, w, hi, ALU.subtract)
            if n == THIRDS - 1:
                ins.then_inc(expert_split, 1)

        @block.sync
        def _(sp):
            sp.dma_start(xa[:, 0], x[0].rearrange("(t p) d -> p t d", p=P)).then_inc(x_in[0], 16)
            for dst, src in ((Wq, wq), (Wk, wk), (Wv, wv)):
                sp.dma_start(dst, src.rearrange("(k p) n -> p k n", p=P)).then_inc(loaded, 16)
            sp.wait_ge(loaded, 3 * 16)
            for dst, src in ((Xk, xk), (Xv, xv), (Xq, xq), (Xo, xo), (Wr, router),
                             (S1_in.rearrange("p (k n) -> p k n", k=KD), s1),
                             (S3_in.rearrange("p (k n) -> p k n", k=KD), s3)):
                sp.dma_start(dst, src.rearrange("(k p) n -> p k n", p=P)).then_inc(loaded_rest, 16)
            sp.dma_start(S2_in[:, 0:(FT - 1) * D].rearrange("p (k n) -> p k n", n=D),
                         s2[0:(FT - 1) * P, :].rearrange("(k p) n -> p k n", p=P)).then_inc(loaded_rest, 16)
            sp.dma_start(S2_in[0:FR, (FT - 1) * D:W2], s2[(FT - 1) * P:F, :]).then_inc(loaded_rest, 16)

            def load(q):
                plain_wait(sp, x1_done, q.n(1, -1))
                sp.dma_start(xa[:, q.par], x[q.b].rearrange("(t p) d -> p t d", p=P)).then_inc(x_in[q.par], 16)

            def load_ctx(q):
                plain_wait(sp, mask_done, q.n(1, -1))
                sp.dma_start(cx[:, q.par], ctx[q.b]).then_inc(c_in[q.par], 16)
                sp.dma_start(mk[:, q.par], mask[q.b, 0].rearrange("(t p) c -> p t c", p=P)).then_inc(c_in[q.par], 16)

            def put_parts(dram, n, part_, sem_, width=S):
                sp.dma_start(dram[n].rearrange("(g p) t -> p g t", p=P)[:, :, 0:width],
                             part_[:, :, 0:width]).then_inc(sem_, 16)

            def stack(dst, dram, order, width, sem_):
                for k in range(2):
                    for n, o in enumerate(order):
                        src = dram[o].rearrange("(g k r) t -> k r g t", k=2, r=HD)[k]
                        sp.dma_start(dst[64 * k + HD * n:64 * k + HD * n + HD, :, 0:width],
                                     src[:, :, 0:width]).then_inc(sem_, 16)

            def stack_a(q):
                plain_wait(sp, a_rd, q.n(A_RD, 0))
                plain_wait(sp, a_free, A_FREE.after(q, "k"))
                for n, p_ in enumerate((qh, ql, kh, kl)):
                    put_parts(qk_d, n, p_, a_wr)
                plain_wait(sp, a_wr, q.n(A_WR, A_WR))
                stack(Q1[:, q.par], qk_d, (0, 1, 0), S, a_rd)
                stack(K1[:, q.par], qk_d, (2, 2, 3), S, a_rd)

            def stack_k2(q):
                plain_wait(sp, k_rd, q.n(K_RD, 0))
                plain_wait(sp, a_free, A_FREE.after(q, "k2"))
                for n, p_ in enumerate((k2h, k2l)):
                    put_parts(k2_d, n, p_, k_wr, SC)
                plain_wait(sp, k_wr, q.n(K_WR, K_WR))
                stack(K2[:, q.par], k2_d, (0, 0, 1), SC, k_rd)

            def stack_q2(q):
                plain_wait(sp, c_rd, q.n(C_RD, 0))
                plain_wait(sp, q2_split, q.n(1, 1))
                put_parts(q2_d, 0, q2h, c_wr)
                put_parts(q2_d, 1, q2l, c_wr)
                plain_wait(sp, c_wr, q.n(C_WR, C_WR))
                stack(Q2, q2_d, (0, 1, 0), S, c_rd)

            def max_row(q, dst, src, sem_):
                plain_wait(sp, m_free, M_FREE.after(q, "maxT"))
                for k in range(2):
                    sp.dma_start(dst[64 * k + KM:64 * k + KM + 1].rearrange("p g s -> p (g s)"),
                                 src[8 * k:8 * k + 8, :]).then_inc(sem_, 16)

            def row_self(q):
                max_row(q, Q1[:, q.par], neg1, mrow1)

            def row_cross(q):
                max_row(q, Q2, neg2, mrow2)

            def rows(q):
                plain_wait(sp, gated_rows, q.n(1, 1))
                plain_wait(sp, ff_free[0], q.n(4, 4))
                sp.dma_start(rows_d[0:NTOK].rearrange("(b t p) c -> b p t c", t=TT, p=P)[q.b],
                             R[:, q.par]).then_inc(rows_out[q.par], 16)

            def body(j, i, more=True):
                on = Iteration(j, i)
                on(D_, rows)
                on(B, row_self)
                on(C, row_cross)
                on(A, stack_a)
                on(B, stack_k2)
                on(B, stack_q2)
                if more:
                    load(Batch(A, j, i + 1))
                    load_ctx(Batch(A, j, i + 1))

            load_ctx(Batch(A, 0, 0))
            for i in range(6):
                if i == 0:
                    sp.wait_ge(padded, 1)
                if i == 5:
                    for e in range(EARLY):
                        load_expert(sp, e)
                body(0, i)
            with sp.Fori(3, NB // 2 - 1) as j:
                for i in range(2):
                    body(j, i)
            for i in range(NB - 2, LAST):
                body(0, i, i + 1 < NB)
                if LAST - 3 <= i < LAST - 1:
                    e = EARLY + i - (LAST - 3)
                    sp.wait_ge(expert_split, e - 1)
                    load_expert(sp, e)

            sp.wait_ge(table, 1)
            for half in listed:
                sp.wait_ge(half, 32 * NB // 2)

            def load_ids(q):
                plain_wait(sp, y_out[q.ring], q.reads())
                at = slot_i[0:1, q.s:q.s + 1] if isinstance(q.s, int) else slot_i[0:1, bass.ds(q.s, 1)]
                r = sp.value_load(at, min_val=0, max_val=NTOK * (NE + 1) - P)
                sp.dma_start(idt[:, q.ring:q.ring + 1], list_d[bass.ds(r, P), :]).then_inc(id_in[q.ring], 16)

            def step(q):
                if q.exists:
                    load_ids(q)
                if isinstance(q.s, int):
                    if q.s == RING - 1:
                        for half in rows_out:
                            sp.wait_ge(half, 16 * NB // 2)
                        load_expert(sp, 4)
                        load_expert(sp, 5)
                    if RING <= q.s < RING + 2:
                        e = 6 + q.s - RING
                        sp.wait_ge(expert_split, e - 3)
                        load_expert(sp, e)

            over_slots(sp, step)

        @block.tensor
        def _(pe):
            mm = pe.matmul
            pe.wait_ge(loaded, 3 * 16)
            pe.wait_ge(consts, CONSTS)

            def transpose_tokens(src, bank, full):
                for k in range(KD):
                    for t in range(TT):
                        last = pe.transpose(bank[:, k * S + t * P:k * S + t * P + P],
                                            src[:, t, k * P:k * P + P], ident)
                last.then_inc(full, 1)

            def project_T(bank, W, xT, full, width=S, step=S):
                for g in range(KD):
                    for k in range(KD):
                        last = mm(bank[:, g * step:g * step + width], W[:, k, g * P:g * P + P],
                                  xT[:, k, 0:width], start=(k == 0), stop=(k == KD - 1))
                last.then_inc(full, 1)

            def project(bank, W, xT, full):
                for t in range(TT):
                    for k in range(KD):
                        last = mm(bank[:, t * D:t * D + D], xT[:, k, t * P:t * P + P], W[:, k, :],
                                  start=(k == 0), stop=(k == KD - 1))
                last.then_inc(full, 1)

            def a_use(q, name):
                at_least(pe, a_free, A_FREE.before(q, name))

            def m_use(q, name):
                at_least(pe, m_free, M_FREE.before(q, name))

            def a_xT(q):
                pe.wait_ge(ln_x[0], q.n(1, 1))
                a_use(q, "xT")
                transpose_tokens(xn[0], bankA, a_full)

            def a_q(q):
                a_use(q, "q")
                project_T(bankA, Wq, xTa, a_full)

            def a_k(q):
                a_use(q, "k")
                project_T(bankA, Wk, xTa, a_full)

            def values(q):
                a_use(q, "v")
                project(bankA, Wv, xTa, a_full)

            def ctx_T(q):
                pe.wait_ge(c_in[q.par], q.half(32, 32))
                a_use(q, "ctxT")
                for k in range(KD):
                    last = pe.transpose(bankA[:, k * SCP:k * SCP + SC], cx[:, q.par, k * P:k * P + P],
                                        ident[0:SC, 0:SC])
                last.then_inc(a_full, 1)

            def ctx_k(q):
                a_use(q, "k2")
                project_T(bankA, Xk, cT, a_full, SC, SCP)

            def ctx_v(q):
                a_use(q, "v2")
                for k in range(KD):
                    last = mm(bankA[0:SC, 0:D], cT[:, k, 0:SC], Xv[:, k, :], start=(k == 0), stop=(k == KD - 1))
                last.then_inc(a_full, 1)

            def ctx_mean(q):
                a_use(q, "mean")
                mm(split(bankA[:, 0:D], H), mean77, V2[:, q.par, :, 0:HD], start=True, stop=True).then_inc(a_full, 1)

            def max_head(q, h):
                k, g = h % 2, h // 2
                at_least(pe, s_free[h % 4], X.before(q, f"max{h // 4}"))
                for t in range(TT):
                    last = mm(BANKS[:, h % 4, t * S:t * S + S], Q1[64 * k:64 * k + KM, q.par, g, t * P:t * P + P],
                              K1[64 * k:64 * k + KM, q.par, g, :], start=True, stop=True)
                last.then_inc(s_full[h % 4], 1)

            def max_T(q, m, last_use):
                for bank in range(4):
                    pe.wait_ge(s_free[bank], X.after(q, last_use))
                m_use(q, "maxT")
                for t in range(TT):
                    last = pe.transpose(bankM[0:H, t * P:t * P + P], m[:, t, :], ident)
                last.then_inc(m_full, 1)

            def exp_head(q, h):
                k, g = h % 2, h // 2
                at_least(pe, s_free[h % 4], X.before(q, f"exp{h // 4}"))
                for t in range(TT):
                    last = mm(BANKS[:, h % 4, t * S:t * S + S], K1[64 * k:64 * k + KX, q.par, g, t * P:t * P + P],
                              Q1[64 * k:64 * k + KX, q.par, g, :], start=True, stop=True)
                last.then_inc(s_full[h % 4], 1)

            def pv_self(q, w):
                for bank in range(4):
                    pe.wait_ge(s_free[bank], X.after(q, f"exp{w}"))
                if w % 2 == 0:
                    m_use(q, f"O{w // 2}")
                for t in range(TT):
                    for j in range(4):
                        h = 4 * w + j
                        last = mm(bankM[32 * j:32 * j + 32, (w % 2) * S:(w % 2) * S + S],
                                  V1[:, t, h, :], P1[:, h % 8, t, :], start=(t == 0), stop=(t == TT - 1))
                last.then_inc(pv1, 1)

            def heads_T(q, t):
                use, bank, full = (a_use, bankA, a_full) if q.stage == C else (m_use, bankM, m_full)
                src = OT if q.stage == B else OT2
                use(q, f"T{t}")
                for w in range(4):
                    last = pe.transpose(bank[:, w * P:w * P + P], src[:, w, t * P:t * P + P], ident)
                last.then_inc(full, 1)

            def x1_T(q):
                pe.wait_ge(ln_x[1], q.n(1, 1))
                m_use(q, "xT")
                transpose_tokens(xn[1], bankM, m_full)

            def q_cross(q):
                m_use(q, "q")
                project_T(bankM, Xq, xTb, m_full)

            def cross_ready(q):
                pe.wait_ge(c_rd, q.n(C_RD, C_RD))
                pe.wait_ge(k_rd, q.n(K_RD, K_RD))
                pe.wait_ge(mask_done, q.n(1, 1))

            def max_cross(q, v):
                k, quad, t = v % 2, (v // 2) % 2, v // 4
                at_least(pe, s_free[v % 4], X.before(q, f"max{v // 4}"))
                ob = split(BANKS[:, v % 4, 0:4 * SC], 4)
                mm(ob, identb, madd[:, q.par, t, 0:SC].unsqueeze(1).broadcast_to([P, 4, SC]), start=True, stop=False,
                   skip_group_check=True)
                for i in range(4):
                    g = 4 * quad + i
                    last = mm(ob[:, i, :], Q2[64 * k:64 * k + KM, g, t * P:t * P + P],
                              K2[64 * k:64 * k + KM, q.par, g, 0:SC], start=False, stop=True,
                              skip_group_check=True)
                last.then_inc(s_full[v % 4], 1)

            def exp_cross(q, v):
                k, w = v % 2, v // 2
                at_least(pe, s_free[v % 4], X.before(q, f"exp{v // 4}"))
                ob = split(BANKS[0:SC, v % 4, :], 2)
                for t in range(TT):
                    mm(ob[:, :, t * P:t * P + P], madd[:, q.par, t, 0:SC],
                       identb.unsqueeze(1).broadcast_to([P, 2, P]), start=(t == 0), stop=False,
                       skip_group_check=True)
                for i in range(2):
                    last = mm(ob[:, i, :], K2[64 * k:64 * k + KX, q.par, 2 * w + i, 0:SC],
                              Q2[64 * k:64 * k + KX, 2 * w + i, :], start=False, stop=True,
                              skip_group_check=True)
                last.then_inc(s_full[v % 4], 1)

            def pv_cross(q, w):
                for v in (2 * w, 2 * w + 1):
                    pe.wait_ge(s_free[v % 4], X.after(q, f"exp{v // 4}"))
                if w % 2 == 0:
                    a_use(q, f"P{w // 2}")
                for j in range(4):
                    last = mm(bankA[32 * j:32 * j + 32, (w % 2) * S:(w % 2) * S + S],
                              V2[:, q.par, 4 * w + j, :], P2[:, (2 * w + j % 2) % 4, j // 2, :], start=True, stop=True)
                last.then_inc(pv2, 1)

            def attn_T(q):
                pe.wait_ge(attn_ready, q.n(1, 1))
                a_use(q, "attnT")
                transpose_tokens(attn, bankA, a_full)

            def out_part(q, n):
                t, k = n // KD, n % KD
                if n == 0:
                    a_use(q, "out")
                last = mm(bankA[:, t * D:t * D + D], aT[:, k, t * P:t * P + P], Xo[:, k, :],
                          start=(k == 0), stop=(k == KD - 1))
                if n == TT * KD - 1:
                    last.then_inc(a_full, 1)

            def x3_T(q):
                pe.wait_ge(ln_x[2], q.n(1, 1))
                a_use(q, "xT")
                transpose_tokens(xn[2], bankA, a_full)

            def route(q):
                pe.wait_ge(x3_copied, q.n(1, 1))
                a_use(q, "route")
                for t in range(TT):
                    for k in range(KD):
                        last = mm(bankA[:, t * NE:t * NE + NE], xTc[:, k, t * P:t * P + P], Wr[:, k, :],
                                  start=(k == 0), stop=(k == KD - 1))
                last.then_inc(a_full, 1)

            def rank(q):
                pe.wait_ge(onehot, q.n(1, 1))
                a_use(q, "rank")
                mm(bankA[:, 0:NE], below, oh[:, 0, :], start=True, stop=True)
                mm(bankA[:, NE:2 * NE], below, oh[:, 1, :], start=True, stop=False)
                mm(bankA[:, NE:2 * NE], onesb, oh[:, 0, :], start=False, stop=True)
                mm(bankA[:, 2 * NE:3 * NE], onesb, oh[:, 0, :], start=True, stop=False)
                mm(bankA[:, 2 * NE:3 * NE], onesb, oh[:, 1, :], start=False, stop=True).then_inc(a_full, 1)

            TERMS = ((0, 0), (1, 0), (0, 1))

            def ff_up(q, f, parts=(0, 1)):
                k, r = f % 2, frow(f)
                if 0 in parts:
                    at_least(pe, ff_free[k], q.n(4 - k, f // 2))
                if f == 0:
                    pe.wait_ge(x3_hi, q.n(1, 1))
                for n in parts:
                    for m, (w, xp) in enumerate(TERMS):
                        if f == n == 0 and m == 2:
                            pe.wait_ge(a_free, A_FREE.after(q, "xT"))
                        for c in range(KD):
                            last = mm(BANKS[0:r, 6 + k, n * S:n * S + S], (S1, S3)[n][w][:, c, f * P:f * P + r],
                                      xTp[xp][:, c, :], start=(m == c == 0), stop=(m == 2 and c == KD - 1))
                if 1 in parts:
                    last.then_inc(ff_full[k], 1)

            def ff_down(q, n):
                t, f = n // FT, n % FT
                r = frow(f)
                if n == 0:
                    pe.wait_ge(ff_free[0], q.n(4, 3))
                    pe.wait_ge(ff_free[1], q.n(3, 3))
                if t == 0:
                    pe.wait_ge(mid_parts, q.n(FT, f + 1))
                for m, (w, xp) in enumerate(TERMS):
                    last = mm(BANKS[:, 6, t * D:t * D + D], midp[xp][0:r, f, t * P:t * P + P], S2[w][0:r, f, :],
                              start=(m == f == 0), stop=(m == 2 and f == FT - 1))
                if n == TT * FT - 1:
                    last.then_inc(ff_full[0], 1)

            DOWN = (2, 3, 4, 7, 9, 10, 11, 12, 13)

            def stacks_ready(q):
                pe.wait_ge(a_rd, q.n(A_RD, A_RD))

            def row_ready(q, sem_):
                pe.wait_ge(sem_, q.n(32, 32))

            def body(j, i):
                on = Iteration(j, i)
                if isinstance(j, int) and i == 1:
                    pe.wait_ge(loaded_rest, 9 * 16)
                    pe.wait_ge(padded, 1)
                    pe.wait_ge(tables, 1)
                if isinstance(j, int) and i == E:
                    pe.wait_ge(shared_lo, 1)
                on(B, stacks_ready)
                for h in range(H):
                    on(B, max_head, h)
                    if h == 1:
                        on(E, attn_T)
                    if 3 <= h < 7:
                        on(E, out_part, h - 3)
                    if h == 8:
                        on(B, values)
                    if h in DOWN:
                        on(D_, ff_down, DOWN.index(h))
                for n in range(len(DOWN), TT * FT):
                    on(D_, ff_down, n)
                on(C, cross_ready)
                on(C, max_cross, 0)
                on(E, x3_T)
                on(B, max_T, m1, "max3")
                for v in range(1, 8):
                    on(C, max_cross, v)
                    if v in (3, 4, 7):
                        on(E, ff_up, (3, 4, 7).index(v))
                    if v == 4:
                        on(E, route)
                on(C, max_T, m2, "max1")
                on(B, row_ready, mrow1)
                for w in range(5):
                    for h in range(4 * w, min(4 * w + 4, H)):
                        on(B, exp_head, h)
                        if h == 1:
                            on(E, ff_up, 3)
                        if h == 2:
                            on(A, a_xT)
                        if h == 4:
                            on(A, a_q)
                        if h == 13:
                            on(A, a_k)
                        if h >= 4 and h % 4 == 2:
                            on(B, pv_self, w - 1)
                    if w == 2:
                        on(B, ctx_T)
                    if w == 4:
                        on(B, ctx_k)
                        on(B, pv_self, 3)
                    if w == 1:
                        on(E, rank)
                on(C, row_ready, mrow2)
                for w in range(5):
                    if w < 4:
                        on(C, exp_cross, 2 * w)
                        on(C, exp_cross, 2 * w + 1)
                    if w == 0:
                        on(B, ctx_v)
                    if w == 1:
                        on(B, ctx_mean)
                        on(B, heads_T, 0)
                    if w == 4:
                        on(E, ff_up, 4, (0,))
                    if w > 0:
                        on(C, pv_cross, w - 1)
                    if w == 2:
                        on(B, heads_T, 1)
                on(E, ff_up, 4, (1,))
                on(C, heads_T, 0)
                on(E, ff_up, 5)
                on(B, x1_T)
                on(C, heads_T, 1)
                on(B, q_cross)

            over_iterations(pe, body)

            pe.wait_ge(table, 1)
            pe.wait_ge(m_free, NB * len(M_ORDER))
            pe.wait_ge(a_free, NB * len(A_ORDER))
            pe.wait_ge(ff_free[0], NB * 4)

            def slot_xT(q):
                pe.wait_ge(g_in[q.ring], q.reads(1))
                at_least(pe, gt_free, q.s)
                for k in range(KD):
                    last = pe.transpose(BANKS[:, 6, k * P:k * P + P], G[:, q.ring, k * P:k * P + P], ident)
                last.then_inc(gt_full, 1)

            def slot_up(q, e, first, bank, full):
                for n in range(2):
                    for m, (w, xp) in enumerate(TERMS):
                        for k in range(KD):
                            last = mm(BANKS[:, bank + n, 0:FH], gTp[xp][:, q.ring % 2, k, :],
                                      experts[:, bass.ds(e + (w * EW + first + k * F + n * FH), FH)],
                                      start=(m == k == 0), stop=(m == 2 and k == KD - 1))
                last.then_inc(full, 1)

            def slot_midT(q):
                pe.wait_ge(mid_done, q.s + 1)
                at_least(pe, mt_free, q.s)
                for f in range(FT):
                    r = frow(f)
                    last = pe.transpose(BANKS[0:r, 4 + f // 3, (f % 3) * P:(f % 3) * P + P],
                                        mid2[:, f * P:f * P + r], ident)
                last.then_inc(mt_full, 1)

            def slot_down(q, e):
                pe.wait_ge(mt_free, q.s + 1)
                at_least(pe, y_ready, q.s)
                for f in range(FT):
                    r = frow(f)
                    for m, (w, xp) in enumerate(TERMS):
                        last = mm(BANKS[:, 7, 0:D], midTp[xp][0:r, f, :],
                                  experts[0:r, bass.ds(e + (w * EW + 2 * W1 + f * D), D)],
                                  start=(f == m == 0), stop=(f == FT - 1 and m == 2))
                last.then_inc(y_full, 1)

            def entry(q, of=slot_e, low=0, high=(NE - 1) * 2 * EW):
                at = of[0:1, q.s:q.s + 1] if isinstance(q.s, int) else of[0:1, bass.ds(q.s, 1)]
                return pe.value_load(at, min_val=low, max_val=high)

            def step(q):
                after, before = q.of(1), q.of(-1)
                if q.exists:
                    e, splits = entry(q), entry(q, slot_n, 1, NE)
                if before.exists:
                    slot_midT(before)
                if q.exists:
                    plain_wait(pe, expert_split, splits)
                    pe.wait_ge(gt_free, q.s + 1)
                    at_least(pe, u_done, q.s)
                    slot_up(q, e, 0, 0, h1_full)
                    slot_up(q, e, W1, 2, h3_full)
                if after.exists:
                    slot_xT(after)
                if before.exists:
                    slot_down(before, entry(before))

            slot_xT(Slot(0, 0))
            over_slots(pe, step)

        @block.scalar
        def _(act):
            def copy(dst, src, sem_, scale=1.0):
                act.activation(dst, src, ACT.Copy, scale=scale).then_inc(sem_, 1)

            def parts_hi(dst, bank, bias, width, step, sem_):
                for g in range(KD):
                    act.activation(dst[:, g, 0:width], bank[:, g * step:g * step + width], ACT.Identity,
                                   bias=bias[:, g:g + 1]).then_inc(sem_, 1)

            act.wait_ge(loaded_bias, 64)
            act.wait_ge(consts, CONSTS)

            def flat(ap):
                return ap.rearrange("p k s -> p (k s)")

            def a_xT(q):
                act.wait_ge(a_full, A_FULL.after(q, "xT"))
                copy(flat(xTa), bankA, a_free)

            def a_hi_part(q, name, dst):
                act.wait_ge(a_full, A_FULL.after(q, name))
                at_least(act, a_wr, q.n(A_WR, 0))
                copy(flat(dst), bankA, a_hi)

            def values(q):
                act.wait_ge(a_full, A_FULL.after(q, "v"))
                for t in range(TT):
                    ins = act.activation(V1[:, t, :, 0:HD], split(bankA[:, t * D:t * D + D], H), ACT.Copy)
                ins.then_inc(a_free, 1)

            def ctx_T(q):
                act.wait_ge(a_full, A_FULL.after(q, "ctxT"))
                copy(cT[:, :, 0:SC], split(bankA[:, 0:KD * SCP], KD)[:, :, 0:SC], a_free)

            def ctx_k(q):
                act.wait_ge(a_full, A_FULL.after(q, "k2"))
                at_least(act, k_wr, q.n(K_WR, 0))
                parts_hi(k2h, bankA, bk, SC, SCP, k_hi)

            def ctx_mean(q):
                act.wait_ge(a_full, A_FULL.after(q, "mean"))
                copy(vmean[:, q.par], bankA[:, 0:D], a_free)

            def neg(q, dst, row_sem):
                act.wait_ge(m_full, M_FULL.after(q, "maxT"))
                at_least(act, row_sem, q.n(32, 0))
                copy(dst, bankM[0:H, 0:S], m_free, scale=-1.0)

            def exp_head(q, h):
                k, g = h % 2, h // 2
                act.wait_ge(s_full[h % 4], X.after(q, f"exp{h // 4}"))
                if h % 4 == 0:
                    at_least(act, pv1, q.n(4, h // 4 - 1))
                act.activation(flat(P1[:, h % 8]), BANKS[:, h % 4, :], ACT.Exp, scale=SCALE)\
                    .then_inc(s_free[h % 4], 1)

            def exp_cross(q, v):
                k, w = v % 2, v // 2
                act.wait_ge(s_full[v % 4], X.after(q, f"exp{v // 4}"))
                if k == 0:
                    at_least(act, pv2, q.n(4, w - 1))
                act.activation(flat(P2[:, v % 4]), BANKS[0:SC, v % 4, :], ACT.Exp, scale=SCALE)\
                    .then_inc(s_free[v % 4], 1)

            def heads(q, u):
                if q.stage == B:
                    act.wait_ge(pv1, q.n(4, 2 * u + 2))
                    copy(flat(OT[:, 2 * u:2 * u + 2, :]), bankM, m_free)
                else:
                    act.wait_ge(pv2, q.n(4, 2 * u + 2))
                    copy(flat(OT2[:, 2 * u:2 * u + 2, :]), bankA, a_free)

            def x1_T(q):
                act.wait_ge(m_full, M_FULL.after(q, "xT"))
                copy(flat(xTb), bankM, m_free)

            def attn_T(q):
                act.wait_ge(a_full, A_FULL.after(q, "attnT"))
                copy(flat(aT), bankA, a_free)

            def q_cross(q):
                act.wait_ge(m_full, M_FULL.after(q, "q"))
                at_least(act, c_wr, q.n(C_WR, 0))
                at_least(act, q2_split, q.n(1, 0))
                for dst in (q2h, q2):
                    for g in range(KD):
                        ins = act.activation(dst[:, g, :], bankM[:, g * S:g * S + S], ACT.Identity, bias=bq[:, g:g + 1])
                ins.then_inc(m_free, 1)

            def x3_T(q):
                act.wait_ge(a_full, A_FULL.after(q, "xT"))
                copy(flat(xTp[0]), bankA, x3_hi)
                copy(flat(xTc), bankA, x3_copied)

            def gate_tanh(q):
                act.wait_ge(top_found, q.n(1, 1))
                act.activation(tg, top8[:, :, 0], ACT.Tanh, scale=0.5).then_inc(gated, 1)

            def ff(q, f):
                k, r = f % 2, frow(f)
                act.wait_ge(ff_full[k], q.n(4 - k, f // 2 + 1))
                at_least(act, ff_free[k], q.n(4 - k, f // 2))
                act.activation(thd[0:r, k, :], BANKS[0:r, 6 + k, 0:S], ACT.Tanh, scale=0.5).then_inc(ff_tanh, 1)

            def shared_weights():
                act.wait_ge(loaded_rest, 9 * 16)
                act.activation(flat(S1[0]), S1_in, ACT.Copy)
                act.activation(flat(S3[0]), S3_in, ACT.Copy)
                act.activation(flat(S2[0])[:, 0:(FT - 1) * D], S2_in[:, 0:(FT - 1) * D], ACT.Copy)
                act.activation(flat(S2[0])[0:FR, (FT - 1) * D:W2], S2_in[0:FR, (FT - 1) * D:W2], ACT.Copy)\
                    .then_inc(shared_hi, 1)
                act.wait_ge(shared_lo, 1)

            def body(j, i):
                on = Iteration(j, i)
                if isinstance(j, int) and i == 1:
                    shared_weights()
                    act.wait_ge(padded, 1)
                on(E, attn_T)
                on(B, values)
                on(E, x3_T)
                on(B, neg, neg1, mrow1)
                on(E, ff, 0)
                on(E, ff, 1)
                on(E, ff, 2)
                on(C, neg, neg2, mrow2)
                if isinstance(j, int) and i == LAST - 3:
                    expert_high(act, 0)
                for h in range(H):
                    on(B, exp_head, h)
                    if h == 1:
                        on(E, gate_tanh)
                        on(E, ff, 3)
                        on(A, a_xT)
                    if h == 4:
                        on(A, a_hi_part, "q", qh)
                    if h == 10:
                        on(B, heads, 0)
                        on(B, ctx_T)
                    if h == 13:
                        on(A, a_hi_part, "k", kh)
                on(B, ctx_k)
                on(B, heads, 1)
                for w in range(5):
                    if w < 4:
                        on(C, exp_cross, 2 * w)
                        on(C, exp_cross, 2 * w + 1)
                    if w == 1:
                        on(B, ctx_mean)
                    if w in (2, 4):
                        on(C, heads, w // 2 - 1)
                on(E, ff, 4)
                on(E, ff, 5)
                on(B, x1_T)
                on(B, q_cross)
                if isinstance(j, int) and i == LAST - 3:
                    expert_high(act, 1)

            over_iterations(act, body)
            act.wait_ge(dve, NB * sum(LINKS.values()))
            act.wait_ge(ff_free[0], NB * 4)
            act.wait_ge(m_free, NB * len(M_ORDER))
            act.wait_ge(a_free, NB * len(A_ORDER))
            act.wait_ge(table, 1)
            for half in rows_out:
                act.wait_ge(half, 16 * NB // 2)

            def slot_xT(q):
                act.wait_ge(gt_full, q.s + 1)
                copy(flat(gTp[0][:, q.ring % 2]), BANKS[:, 6, 0:KD * P], gt_hi)

            def slot_tanh(q):
                act.wait_ge(h1_full, q.s + 1)
                at_least(act, u_done, q.s)
                act.activation(split(th2, 2), BANKS[:, 0:2, 0:FH], ACT.Tanh, scale=0.5).then_inc(t_done, 1)

            def slot_midT(q):
                act.wait_ge(mt_full, q.s + 1)
                for r, f0, f1 in MID_PIECES:
                    ins = act.activation(flat(midTp[0][0:r, f0:f1, :]), mid_bank(r, f0, f1), ACT.Copy)
                    if f1 in (3, FT):
                        ins.then_inc(mt_hi, 1)

            def step(q):
                if q.of(-1).exists:
                    slot_midT(q.of(-1))
                if q.exists:
                    slot_tanh(q)
                e = SPLIT_AFTER.get(q.s) if isinstance(q.s, int) else None
                if e is not None:
                    expert_high(act, e, (0,))
                if q.of(1).exists:
                    slot_xT(q.of(1))
                if e is not None:
                    expert_high(act, e, (1, 2))

            slot_xT(Slot(0, 0))
            over_slots(act, step)

        @block.vector
        def _(v):
            v.wait_ge(consts, CONSTS)
            v.wait_ge(loaded_bias, 64)

            def paddings():
                v.memset(V1.rearrange("p t h d -> p (t h d)"), 0.0).then_inc(pads, 1)
                v.memset(V2.rearrange("p a h d -> p (a h d)"), 0.0).then_inc(pads, 1)
                v.wait_ge(pads, 2)
                v.memset(V1.rearrange("p t h d -> p (t h) d")[:, :, HD], 1.0)
                v.memset(V2.rearrange("p a h d -> p (a h) d")[:, :, HD], 1.0)
                v.memset(K1.rearrange("p a h s -> p (a h s)"), 1.0)
                v.memset(K2.rearrange("p a h s -> p (a h s)"), 1.0).then_inc(padded, 1)

            def sums(n, src, link):
                for t in range(TT):
                    ins = v.bn_stats(st[:, n, t, :], src[:, t, :])
                link(ins, True)

            def moments(n, link):
                for t in range(TT):
                    ins = v.bn_aggr(mv[:, n, t, :], st[:, n, t, :])
                link(ins)
                v.tensor_scalar(ve[:, n, :], mv[:, n, :, 1], EPS, None, ALU.add).then_inc(ln_v[n], 1)

            def a_stats(q, link):
                v.wait_ge(x_in[q.par], q.half(16, 16))
                sums(0, xa[:, q.par], link)
                moments(0, link)

            def a_lo_part(q, n, dst, hi):
                v.wait_ge(a_hi, q.n(2, n + 1))
                at_least(v, a_wr, q.n(A_WR, 0))
                v.tensor_tensor(dst.rearrange("p k s -> p (k s)"), bankA, hi.rearrange("p k s -> p (k s)"),
                                ALU.subtract).then_inc(a_free, 1)

            def parts_lo_bias(dst, bank, bias, hi, width, step, free):
                for g in range(KD):
                    ins = v.scalar_tensor_tensor(dst[:, g, 0:width], bank[:, g * step:g * step + width],
                                                 bias[:, g:g + 1], hi[:, g, 0:width], ALU.add, ALU.subtract)
                ins.then_inc(free, 1)

            def ctx_mask(q, link):
                v.wait_ge(c_in[q.par], q.half(32, 32))
                link(v.tensor_reduce(anyk[:, q.par, :], mk[:, q.par], AX.X, ALU.max))
                v.tensor_scalar(nany[:, q.par, :], anyk[:, q.par, :], -1.0, 1.0, ALU.mult, ALU.add)
                link(v.tensor_scalar(any9, anyk[:, q.par, :], NEG, None, ALU.mult))
                for t in range(TT):
                    ins = v.tensor_scalar(madd[:, q.par, t, 0:SC], mk[:, q.par, t, :], 1.0, any9[:, t:t + 1],
                                          ALU.subtract, ALU.mult)
                link(ins)
                v.wait_ge(a_full, A_FULL.after(q, "ctxT"))
                v.tensor_copy(signal1, tokf[:, 0:1]).then_inc(mask_done, 1)

            def ctx_k(q):
                v.wait_ge(k_hi, q.n(2, 2))
                at_least(v, k_wr, q.n(K_WR, 0))
                parts_lo_bias(k2l, bankA, bk, k2h, SC, SCP, a_free)

            def ctx_v(q):
                v.wait_ge(a_full, A_FULL.after(q, "v2"))
                v.tensor_tensor(V2[:, q.par, :, 0:HD], split(bankA[0:SC, 0:D], H), split(bv[0:SC], H), ALU.add)\
                    .then_inc(a_free, 1)

            def max_head(q, h):
                k, g = h % 2, h // 2
                v.wait_ge(s_full[h % 4], X.after(q, f"max{h // 4}"))
                v.tensor_reduce(m1[:, :, 8 * k + g], split(BANKS[:, h % 4, :], TT), AX.X, ALU.max)\
                    .then_inc(s_free[h % 4], 1)

            def normalise(q, t, link, scale=None):
                bank, full, free, nfull, nfree = ((bankA, a_full, a_free, A_FULL, A_FREE) if q.stage == C
                                                  else (bankM, m_full, m_free, M_FULL, M_FREE))
                v.wait_ge(full, nfull.after(q, f"T{t}"))
                heads = split(bank, H)
                link(v.reciprocal(rden, heads[:, :, HD]))
                if scale is not None:
                    link(v.tensor_scalar(rden, rden, scale, None, ALU.mult))
                v.tensor_tensor(split(tmp, H), heads[:, :, 0:HD], rden.unsqueeze(2).broadcast_to([P, H, HD]),
                                ALU.mult).then_inc(free, 1)
                v.wait_ge(free, nfree.after(q, f"T{t}"))

            def x1_tile(q, t, link):
                normalise(q, t, link)
                link(v.tensor_tensor(x1[:, q.par, t, :], xa[:, q.par, t, :], tmp, ALU.add))

            def x1_stats(q, link):
                v.tensor_copy(signal1, tokf[:, 0:1]).then_inc(x1_done, 1)
                sums(1, x1[:, q.par], link)
                moments(1, link)

            def x1_norm(q):
                v.wait_ge(ln_r[1], q.n(1, 1))
                for t in range(TT):
                    ins = v.tensor_scalar(xn[1][:, t, :], x1[:, q.par, t, :], mv[:, 1, t, 0:1], rstd[:, 1, t:t + 1],
                                          ALU.subtract, ALU.mult)
                ins.then_inc(ln_x[1], 1)

            def max_cross(q, n):
                k, quad, t = n % 2, (n // 2) % 2, n // 4
                v.wait_ge(s_full[n % 4], X.after(q, f"max{n // 4}"))
                v.tensor_reduce(m2[:, t, 8 * k + 4 * quad:8 * k + 4 * quad + 4], split(BANKS[:, n % 4, 0:4 * SC], 4),
                                AX.X, ALU.max).then_inc(s_free[n % 4], 1)

            def attn_tile(q, t, link):
                normalise(q, t, link, anyk[:, q.par, t:t + 1])
                link(v.scalar_tensor_tensor(attn[:, t, :], vmean[:, q.par], nany[:, q.par, t:t + 1], tmp,
                                            ALU.mult, ALU.add))
                if t == TT - 1:
                    v.tensor_copy(signal1, tokf[:, 0:1]).then_inc(attn_ready, 1)

            def x2_sum(q):
                v.wait_ge(a_full, A_FULL.after(q, "out"))
                v.wait_ge(x1_bias, q.n(1, 1))
                v.tensor_tensor(x2[:, q.par], split(bankA, TT), x1[:, q.par], ALU.add).then_inc(a_free, 1)

            def x2_stats(q, link):
                v.wait_ge(a_free, A_FREE.after(q, "out"))
                sums(2, x2[:, q.par], link)

            def x2_moments(q, link):
                moments(2, link)

            def route(q, link):
                v.wait_ge(a_full, A_FULL.after(q, "route"))
                v.tensor_copy(lg.rearrange("p t e -> p (t e)"), bankA[:, 0:TT * NE]).then_inc(a_free, 1)
                plain_wait(v, a_free, A_FREE.after(q, "route"))
                for t in range(TT):
                    link(v.max(top8[:, t, :], lg[:, t, :]), True)
                for t in range(TT):
                    link(v.max_index(idx8[:, t, :], top8[:, t, :], lg[:, t, :]), t == 0)
                link(v.tensor_copy(idxf, idx8[:, :, 0]))
                v.tensor_copy(signal1, tokf[:, 0:1]).then_inc(top_found, 1)
                for t in range(TT):
                    ins = v.tensor_scalar(oh[:, t, :], erow, idxf[:, t:t + 1], None, ALU.is_equal)
                ins.then_inc(onehot, 1)

            def rank(q, link):
                v.wait_ge(a_full, A_FULL.after(q, "rank"))
                link(v.tensor_tensor(pr, split(bankA[:, 0:TT * NE], TT), base.unsqueeze(1).broadcast_to([P, TT, NE]),
                                     ALU.add))
                v.tensor_tensor(base, base, bankA[:, 2 * NE:3 * NE], ALU.add).then_inc(a_free, 1)
                link(v.tensor_tensor(prm, pr, oh, ALU.mult))
                link(v.tensor_reduce(posf, prm, AX.X, ALU.add))
                at_least(v, listed[q.par], q.half(32, 0))
                v.tensor_copy(posi[:, q.par, :], posf)
                link(v.tensor_copy(toki[:, q.par, :], tokf))
                link(v.tensor_scalar(tokf, tokf, float(S), None, ALU.add))
                v.tensor_copy(signal1, tokf[:, 0:1]).then_inc(pos_ready, 1)

            def shared_weights():
                v.wait_ge(shared_hi, 1)
                for (hi, lo), src in ((S1, S1_in), (S3, S3_in)):
                    v.tensor_tensor(lo.rearrange("p k n -> p (k n)"), src, hi.rearrange("p k n -> p (k n)"),
                                    ALU.subtract)
                hi, lo = (w.rearrange("p k n -> p (k n)") for w in S2)
                full, last = slice(0, (FT - 1) * D), slice((FT - 1) * D, W2)
                v.tensor_tensor(lo[:, full], S2_in[:, full], hi[:, full], ALU.subtract)
                v.tensor_tensor(lo[0:FR, last], S2_in[0:FR, last], hi[0:FR, last], ALU.subtract).then_inc(shared_lo, 1)

            def x3_lo(q):
                v.wait_ge(x3_copied, q.n(1, 1))
                v.tensor_tensor(xTp[1].rearrange("p k s -> p (k s)"), bankA, xTp[0].rearrange("p k s -> p (k s)"),
                                ALU.subtract).then_inc(a_free, 1)

            def ff(q, f, link):
                k, r = f % 2, frow(f)
                v.wait_ge(ff_tanh, q.n(FT, f + 1))
                link(v.scalar_tensor_tensor(ud[0:r, k, :], thd[0:r, k, :], 1.0, BANKS[0:r, 6 + k, 0:S],
                                            ALU.add, ALU.mult))
                at_least(v, mid_parts, q.n(FT, f - 1))
                v.scalar_tensor_tensor(mid[0:r, k, :], ud[0:r, k, :], 0.5, BANKS[0:r, 6 + k, S:2 * S],
                                       ALU.mult, ALU.mult).then_inc(ff_free[k], 1)

            def ff_out(q, link):
                v.wait_ge(ff_full[0], q.n(4, 4))
                at_least(v, rows_out[q.par], q.half(16, 0))
                v.tensor_tensor(R[:, q.par, :, D:2 * D], split(BANKS[:, 6, :], TT), x2[:, q.par], ALU.add)\
                    .then_inc(ff_free[0], 1)
                link(v.tensor_copy(signal1, tokf[:, 0:1]))

            def slot_table():
                link = Chain(v, 0, table_chain)
                link(v.tensor_tensor(cnt, base[0:1], e4096[0:1], ALU.subtract))
                link(v.tensor_scalar(cnt, cnt, 1.0, float(P - 1), ALU.max, ALU.add))
                link(v.tensor_copy(cnti, cnt))
                link(v.tensor_scalar(cnti, cnti, 7, None, ALU.logical_shift_right))
                link(v.tensor_copy(tiles, cnti))
                link(v.tensor_copy(cum, tiles))
                for e in range(1, NE):
                    link(v.tensor_tensor(cum[:, e:e + 1], cum[:, e:e + 1], cum[:, e - 1:e], ALU.add))
                link(v.memset(acc.rearrange("p a s -> p (a s)"), 0.0))
                for e in range(NE):
                    link(v.tensor_scalar(accb[:, 0, :], srow, cum[:, e:e + 1], None, ALU.is_ge))
                    link(v.tensor_tensor(acc[:, 0, :], acc[:, 0, :], accb[:, 0, :], ALU.add))
                    link(v.scalar_tensor_tensor(acc[:, 1, :], accb[:, 0, :], tiles[:, e:e + 1], acc[:, 1, :],
                                                ALU.mult, ALU.add))
                link(v.tensor_tensor(accb[:, 1, :], srow, acc[:, 1, :], ALU.subtract))
                link(v.tensor_scalar(accb[:, 1, :], accb[:, 1, :], float(P), None, ALU.mult))
                link(v.scalar_tensor_tensor(accb[:, 0, :], acc[:, 0, :], float(NTOK), accb[:, 1, :], ALU.mult, ALU.add))
                link(v.tensor_copy(slot_i, accb[:, 0, :]))
                link(v.tensor_scalar(acc[:, 0, :], acc[:, 0, :], float(NE - 1), None, ALU.min))
                link(v.tensor_scalar(accb[:, 0, :], acc[:, 0, :], 1.0, 1.0, ALU.add, ALU.max))
                link(v.tensor_copy(slot_n, accb[:, 0, :]))
                link(v.tensor_scalar(acc[:, 0, :], acc[:, 0, :], float(2 * EW), None, ALU.mult))
                link(v.tensor_copy(slot_e, acc[:, 0, :]))
                v.memset(signal2, 0.0).then_inc(table, 1)

            def body(j, i):
                on = Iteration(j, i)
                if isinstance(j, int) and i == LAST - 2:
                    expert_low(v, 1)
                if isinstance(j, int) and i == LAST - 1:
                    slot_table()
                link = Chain(v, before_iteration(LINKS, j, i))
                if isinstance(j, int) and i == 1:
                    v.wait_ge(tables, 1)
                    shared_weights()
                for h in range(H):
                    on(B, max_head, h)
                    if h == 6:
                        on(E, x2_sum)
                    if h == 7:
                        on(E, x2_stats, link)
                    if h == 8:
                        on(E, x2_moments, link)
                on(C, max_cross, 0)
                on(D_, ff_out, link)
                on(E, x3_lo)
                on(C, max_cross, 1)
                on(C, max_cross, 2)
                on(E, ff, 0, link)
                on(C, max_cross, 3)
                on(A, a_stats, link)
                if isinstance(j, int) and i == 0:
                    paddings()
                on(C, max_cross, 4)
                on(C, max_cross, 5)
                on(C, max_cross, 6)
                on(C, max_cross, 7)
                on(E, ff, 1, link)
                on(E, route, link)
                on(E, ff, 2, link)
                on(E, ff, 3, link)
                on(A, a_lo_part, 0, ql, qh)
                on(E, rank, link)
                on(B, ctx_mask, link)
                on(A, a_lo_part, 1, kl, kh)
                on(B, ctx_k)
                on(B, ctx_v)
                on(B, x1_tile, 0, link)
                on(B, x1_tile, 1, link)
                on(B, x1_stats, link)
                on(B, x1_norm)
                if isinstance(j, int) and i == LAST - 3:
                    expert_low(v, 0)
                on(E, ff, 4, link)
                on(C, attn_tile, 0, link)
                on(C, attn_tile, 1, link)
                on(E, ff, 5, link)
                want = sum(n for stage, n in LINKS.items() if not isinstance(j, int) or live(stage, i))
                assert link.k == want, (link.k, want, i)

            over_iterations(v, body)

            def slot_u(q):
                v.wait_ge(t_done, q.s + 1)
                at_least(v, mid_done, q.s)
                v.scalar_tensor_tensor(split(u2, 2), split(th2, 2), 1.0, BANKS[:, 0:2, 0:FH], ALU.add, ALU.mult)\
                    .then_inc(u_done, 1)
                v.wait_ge(u_done, q.s + 1)
                v.wait_ge(h3_full, q.s + 1)
                at_least(v, mt_full, q.s)
                v.scalar_tensor_tensor(split(mid2, 2), split(u2, 2), 0.5, BANKS[:, 2:4, 0:FH], ALU.mult, ALU.mult)\
                    .then_inc(mid_done, 1)

            def slot_y(q):
                v.wait_ge(y_full, q.s + 1)
                at_least(v, y_out[q.ring], q.reads())
                v.tensor_tensor(y2[:, q.ring, :], BANKS[:, 7, 0:D], G[:, q.ring, D:2 * D], ALU.add).then_inc(y_ready, 1)

            def slot_midT(q):
                for r, f0, f1 in MID_PIECES:
                    if f0 in (0, 3):
                        v.wait_ge(mt_hi, q.s * 2 + (f0 // 3 + 1))
                    hi, lo = (p_[0:r, f0:f1, :].rearrange("p f s -> p (f s)") for p_ in midTp)
                    ins = v.tensor_tensor(lo, mid_bank(r, f0, f1), hi, ALU.subtract)
                ins.then_inc(mt_free, 1)

            def slot_xT(q):
                v.wait_ge(gt_hi, q.s + 1)
                hi, lo = (p_[:, q.ring % 2].rearrange("p k s -> p (k s)") for p_ in gTp)
                v.tensor_tensor(lo, BANKS[:, 6, 0:KD * P], hi, ALU.subtract).then_inc(gt_free, 1)

            def step(q):
                if q.of(-1).exists:
                    slot_midT(q.of(-1))
                if isinstance(q.s, int) and q.s - 1 in SPLIT_AFTER:
                    expert_low(v, SPLIT_AFTER[q.s - 1], (2,))
                if q.exists:
                    slot_u(q)
                if q.of(1).exists:
                    slot_xT(q.of(1))
                if q.of(-1).exists:
                    slot_y(q.of(-1))
                if isinstance(q.s, int) and q.s in SPLIT_AFTER:
                    expert_low(v, SPLIT_AFTER[q.s], (0, 1))

            slot_xT(Slot(0, 0))
            over_slots(v, step)

        @block.gpsimd
        def _(g):
            k = [0]

            def made(ins):
                k[0] += 1
                ins.then_inc(chain_c, 1)
                g.wait_ge(chain_c, k[0])

            made(g.memset(ident, 0.0))
            made(g.affine_select(out=ident, in_=ident, compare_op=ALU.not_equal, fill=1.0, base=0,
                                 pattern=[[-1, P]], channel_multiplier=1))
            g.memset(mhalf, -0.5).then_inc(consts, 1)
            for dst, src in ((bv, xbv), (bo, xbo)):
                g.dma_start(dst, src.rearrange("(a n) -> a n", a=1).broadcast_to([P, D])).then_inc(loaded_bias, 16)
            for dst, src in ((bq, xbq), (bk, xbk)):
                g.dma_start(dst, src.rearrange("(k p) -> p k", p=P), allow_slow_non_contiguous=True).then_inc(loaded_bias, 16)

            def make_tables():
                made(g.tensor_copy(identb, ident))
                made(g.memset(onesb, 1.0))
                made(g.memset(below, 0.0))
                made(g.affine_select(out=below, in_=below, compare_op=ALU.is_ge, fill=1.0, base=0,
                                     pattern=[[-1, P]], channel_multiplier=1))
                made(g.memset(mean77, 1.0 / SC))
                made(g.iota(erow, [[1, NE]], base=0, channel_multiplier=0, allow_small_or_imprecise_dtypes=True))
                made(g.iota(e4096, [[NTOK, NE]], base=0, channel_multiplier=0, allow_small_or_imprecise_dtypes=True))
                made(g.tensor_copy(base, e4096))
                made(g.iota(srow, [[1, 64]], base=0, channel_multiplier=0, allow_small_or_imprecise_dtypes=True))
                made(g.iota(tokf, [[P, TT]], base=0, channel_multiplier=1, allow_small_or_imprecise_dtypes=True))
                g.memset(signal1, 0.0).then_inc(tables, 1)
                made(g.iota(fill, [[0, NTOK * (NE + 1) // P]], base=PAD_ROW, channel_multiplier=0))
                made(g.memset(zrow, 0.0))
                g.dma_start(list_d.rearrange("(p n) a -> p (n a)", p=P), fill).then_inc(dram_init, 16)
                g.dma_start(rows_d[NTOK].rearrange("(p n) -> p n", p=P), zrow).then_inc(dram_init, 16)
                g.wait_ge(dram_init, 32)

            def rstd_of(q, n):
                plain_wait(g, ln_v[n], q.n(1, 1))
                g.tensor_tensor(rstd[:, n, :], ve[:, n, :], mhalf, ALU.pow).then_inc(ln_r[n], 1)

            def norm(q, n, src):
                rstd_of(q, n)
                if n == 2:
                    plain_wait(g, gated_rows, q.n(1, 0))
                plain_wait(g, ln_r[n], q.n(1, 1))
                for t in range(TT):
                    ins = g.tensor_scalar(xn[n][:, t, :], src[:, q.par, t, :], mv[:, n, t, 0:1], rstd[:, n, t:t + 1],
                                          ALU.subtract, ALU.mult)
                ins.then_inc(ln_x[n], 1)

            def bias_x1(q):
                plain_wait(g, ln_x[1], q.n(1, 1))
                g.tensor_tensor(x1[:, q.par], x1[:, q.par], bo.unsqueeze(1).broadcast_to([P, TT, D]), ALU.add)\
                    .then_inc(x1_bias, 1)

            def ff_parts(q, f):
                k, r = f % 2, frow(f)
                if f == 0:
                    plain_wait(g, ff_full[0], q.n(4, 0))
                plain_wait(g, ff_free[k], q.n(4 - k, f // 2 + 1))
                g.tensor_copy(midp[0][0:r, f, :], mid[0:r, k, :]).then_inc(mid_hi, 1)
                plain_wait(g, mid_hi, q.n(FT, f + 1))
                g.tensor_tensor(midp[1][0:r, f, :], mid[0:r, k, :], midp[0][0:r, f, :], ALU.subtract)\
                    .then_inc(mid_parts, 1)

            def q_cross(q):
                plain_wait(g, m_free, M_FREE.after(q, "q"))
                g.tensor_tensor(q2l, q2, q2h, ALU.subtract).then_inc(q2_split, 1)

            def gate_rows(q):
                plain_wait(g, gated, q.n(1, 1))
                g.tensor_scalar(gate, tg, 0.5, 0.5, ALU.mult, ALU.add).then_inc(gate_made, 1)
                plain_wait(g, rows_out[q.par], q.half(16, 0))
                plain_wait(g, gate_made, q.n(1, 1))
                for t in range(TT):
                    ins = g.tensor_scalar(R[:, q.par, t, 0:D], xn[2][:, t, :], gate[:, t:t + 1], None, ALU.mult)
                ins.then_inc(gated_rows, 1)

            def list_tokens(q):
                plain_wait(g, pos_ready, q.n(1, 1))
                for t in range(TT):
                    g.indirect_dma_start(out=list_d, out_offset=bass.IndirectOffsetOnAxis(ap=posi[:, q.par, t:t + 1], axis=0),
                                         in_=toki[:, q.par, t:t + 1], in_offset=None).then_inc(listed[q.par], 16)

            def body(j, i):
                on = Iteration(j, i)
                if isinstance(j, int) and i == 1:
                    make_tables()
                on(E, norm, 2, x2)
                if isinstance(j, int) and i == E:
                    g.wait_ge(shared_lo, 1)
                on(E, ff_parts, 0)
                on(A, norm, 0, xa)
                for f in (1, 2, 3):
                    on(E, ff_parts, f)
                on(E, gate_rows)
                on(E, list_tokens)
                on(B, rstd_of, 1)
                on(E, ff_parts, 4)
                on(B, bias_x1)
                on(E, ff_parts, 5)
                on(B, q_cross)

            over_iterations(g, body)
            g.wait_ge(table, 1)
            for half in rows_out:
                g.wait_ge(half, 16 * NB // 2)

            def gather(q):
                plain_wait(g, id_in[q.ring], q.reads(1))
                plain_wait(g, y_ready, q.s - RING + 1)
                g.indirect_dma_start(out=G[:, q.ring, :], out_offset=None, in_=rows_d,
                                     in_offset=bass.IndirectOffsetOnAxis(ap=idt[:, q.ring:q.ring + 1], axis=0))\
                    .then_inc(g_in[q.ring], 16)

            def scatter(q):
                plain_wait(g, y_ready, q.s + 1)
                g.indirect_dma_start(out=out, out_offset=bass.IndirectOffsetOnAxis(ap=idt[:, q.ring:q.ring + 1], axis=0),
                                     in_=y2[:, q.ring, :], in_offset=None, bounds_check=NTOK - 1, oob_is_err=False)\
                    .then_inc(y_out[q.ring], 16)

            def step(q):
                if q.of(GATHER).exists:
                    gather(q.of(GATHER))
                if q.of(-1).exists:
                    scatter(q.of(-1))

            for s in range(GATHER):
                gather(Slot(0, s))
            over_slots(g, step)
            for r in range(RING):
                g.wait_ge(y_out[r], 16 * ((NSLOT - r + RING - 1) // RING))


def kernel(x, ctx_1024, mask_Bx1xSxS2_bf1, L0_attn_w_Q, L0_attn_w_K, L0_attn_w_V,
           L0_xattn_Wq, L0_xattn_bq, L0_xattn_Wk, L0_xattn_bk, L0_xattn_Wv, L0_xattn_bv,
           L0_xattn_Wo, L0_xattn_bo, L0_ffn_router_DE, L0_ffn_w1_eDF, L0_ffn_w3_eDF, L0_ffn_w2_eFD,
           L0_ffn_ws1_DF, L0_ffn_ws3_DF, L0_ffn_ws2_FD):
    import concourse.bacc as bacc
    from concourse.bass_utils import run_bass_kernel_spmd

    def T(w):
        return np.ascontiguousarray(np.asarray(w).T)

    given = {
        "x": x, "ctx": ctx_1024, "mask": np.asarray(mask_Bx1xSxS2_bf1).view(np.uint8),
        "wq": L0_attn_w_Q, "wk": L0_attn_w_K, "wv": L0_attn_w_V,
        "xq": T(L0_xattn_Wq), "xbq": L0_xattn_bq, "xk": T(L0_xattn_Wk), "xbk": L0_xattn_bk,
        "xv": T(L0_xattn_Wv), "xbv": L0_xattn_bv, "xo": T(L0_xattn_Wo), "xbo": L0_xattn_bo,
        "router": L0_ffn_router_DE, "w1": L0_ffn_w1_eDF, "w3": L0_ffn_w3_eDF, "w2": L0_ffn_w2_eFD,
        "s1": L0_ffn_ws1_DF, "s3": L0_ffn_ws3_DF, "s2": L0_ffn_ws2_FD,
    }
    nc = bacc.Bacc("TRN2", target_bir_lowering=False, num_devices=1)
    arrays, aps = {}, {}
    for name, a in given.items():
        a = np.ascontiguousarray(np.asarray(a))
        arrays["in_" + name] = a
        aps[name] = nc.dram_tensor("in_" + name, a.shape, mybir.dt.from_np(a.dtype), kind="ExternalInput").ap()
    out = nc.dram_tensor("out", (NTOK, D), F32, kind="ExternalOutput").ap()
    decoder_layer(nc, out=out, **aps)
    r = run_bass_kernel_spmd(nc, [arrays], core_ids=[0])
    return r.results[0]["out"].reshape(NB, S, D)
```
